# Optimizing a Trainium2 kernel written in Bass

```python
import numpy as np
import jax
import jax.numpy as jnp

def _softmax(x, axis=-1):
    return jax.nn.softmax(x, axis=axis)

def _gelu(x):
    return jax.nn.gelu(x, approximate=True)

def _silu(x):
    return jax.nn.silu(x)

def _sigmoid(x):
    return jax.nn.sigmoid(x)

def _layernorm(x, axis=-1, eps=1e-05):
    m = jnp.mean(x, axis=axis, keepdims=True)
    v = jnp.var(x, axis=axis, keepdims=True)
    return (x - m) / jnp.sqrt(v + eps)

def _scatter_add(tgt, idx, src, axis=0):
    return tgt.at[idx].add(src)

def _segment_sum(src, seg, n):
    return jax.ops.segment_sum(src, seg, n)
kernel_name = 'mk_gnn_preln_d4_gnn_r64_89004d'

def setup_inputs(seed: int=0):
    np.random.seed(seed)
    _w = jnp.asarray

    def _rec_inputs():
        import jax
        import jax.numpy as jnp
        _gk = jax.random.key(seed)
        x = -0.0003713 + 1 * jax.random.normal(jax.random.fold_in(_gk, 1), (50000, 128), jnp.float32)
        src = jax.random.randint(jax.random.fold_in(_gk, 2), (25000,), 0, 50000, jnp.int32)
        dst = jax.random.randint(jax.random.fold_in(_gk, 3), (25000,), 0, 50000, jnp.int32)
        _o = jnp.argsort(dst, stable=True)
        src = src[_o]
        dst = dst[_o]
        edge_attr_4 = -0.00166765 + 0.999426 * jax.random.normal(jax.random.fold_in(_gk, 12), (25000, 4), jnp.float32)
        edge_attr_8 = -0.00016606 + 0.999594 * jax.random.normal(jax.random.fold_in(_gk, 13), (25000, 8), jnp.float32)
        edge_type_8 = jax.random.randint(jax.random.fold_in(_gk, 15), (25000,), 0, 8, jnp.int32)
        node_vec1 = 0.00192408 + 1.00201 * jax.random.normal(jax.random.fold_in(_gk, 16), (50000, 1), jnp.float32)
        node_vec1_n2 = 0.00192408 + 1.00201 * jax.random.normal(jax.random.fold_in(_gk, 17), (50000, 1), jnp.float32)
        return (x, src, dst, edge_attr_4, edge_attr_8, edge_type_8, node_vec1, node_vec1_n2)
    x, src, dst, edge_attr_4, edge_attr_8, edge_type_8, node_vec1, node_vec1_n2 = _rec_inputs()

    def _L0_gnn_setup():
        import jax, jax.numpy as jnp
        import numpy as np
        N, E, D_IN, D_OUT = (100000, 625000, 128, 128)
        key = jax.random.key(seed)
        k1, k2, k3 = jax.random.split(key, 3)
        x = jax.random.normal(k1, (N, D_IN), dtype=jnp.float32)
        edge_index = jax.random.randint(k2, (2, E), 0, N, dtype=jnp.int32)
        W = jax.random.normal(k3, (D_IN, D_OUT), dtype=jnp.float32)
        return {'x': x, 'edge_index': edge_index, 'W': W}
    _L0_gnn_all = _L0_gnn_setup()
    _L0_gnn_in = {k: v for k, v in _L0_gnn_all.items() if k in ('W',)}
    del _L0_gnn_all

    def _L1_gnn_setup():
        import jax, jax.numpy as jnp
        import numpy as np
        N_NODES = 50000
        N_EDGES = 500000
        F_DIM = 128
        N_REL = 8
        N_LAYERS = 2
        NEG_SLOPE = 0.2

        def _segment_softmax(logits, seg, num_segments):
            m = jax.ops.segment_max(logits, seg, num_segments=num_segments)
            m = jax.lax.stop_gradient(m)
            e = jnp.exp(logits - m[seg])
            denom = jax.ops.segment_sum(e, seg, num_segments=num_segments)
            return e / (denom[seg] + 1e-16)

        def _rgat_layer(h, src, dst, edge_type, W, q, k, b):
            n = h.shape[0]
            xw = jnp.einsum('nf,rfg->rng', h, W)
            out_j = xw[edge_type, src]
            out_i = xw[edge_type, dst]
            logits = jax.nn.leaky_relu((out_i @ q + out_j @ k)[:, 0], NEG_SLOPE)
            alpha = _segment_softmax(logits, dst, n)
            agg = jax.ops.segment_sum(alpha[:, None] * out_j, dst, num_segments=n)
            return agg + b
        key = jax.random.key(seed)
        ks = jax.random.split(key, 6)
        x = jax.random.normal(ks[0], (N_NODES, F_DIM), dtype=jnp.float32)
        edge_index = jax.random.randint(ks[1], (2, N_EDGES), 0, N_NODES)
        edge_type = jax.random.randint(ks[2], (N_EDGES,), 0, N_REL)
        W = jax.random.normal(ks[3], (N_LAYERS, N_REL, F_DIM, F_DIM), dtype=jnp.float32) * (1.0 / np.sqrt(F_DIM)).astype(np.float32)
        att_q = jax.random.normal(ks[4], (N_LAYERS, F_DIM, 1), dtype=jnp.float32) * 0.1
        att_k = jax.random.normal(ks[5], (N_LAYERS, F_DIM, 1), dtype=jnp.float32) * 0.1
        bias = jnp.zeros((N_LAYERS, F_DIM), dtype=jnp.float32)
        return {'x': x, 'W': W, 'att_q': att_q, 'att_k': att_k, 'bias': bias, 'edge_index': edge_index, 'edge_type': edge_type}
    _L1_gnn_all = _L1_gnn_setup()
    _L1_gnn_in = {k: v for k, v in _L1_gnn_all.items() if k in ('W', 'att_q', 'att_k', 'bias')}
    del _L1_gnn_all

    def _L2_gnn_setup():
        import jax, jax.numpy as jnp
        import numpy as np
        N = 25000
        E = 6250
        MUL = 32
        NSC = 8
        HID = 64
        WNUM = 4 * MUL
        NUM_NEIGH = 16.0
        INV_SQRT3 = 1.0 / np.sqrt(3.0)
        key = jax.random.key(seed)
        ks = jax.random.split(key, 13)
        return {'node_input': jax.random.normal(ks[0], (N, 4 * MUL), jnp.float32), 'node_attr_input': jax.random.normal(ks[1], (N, 1), jnp.float32), 'node_attr_output': jax.random.normal(ks[2], (N, 1), jnp.float32), 'edge_src': jax.random.randint(ks[3], (E,), 0, N), 'edge_dst': jax.random.randint(ks[4], (E,), 0, N), 'edge_attr': jax.random.normal(ks[5], (E, 4), jnp.float32), 'edge_scalar_attr': jax.random.normal(ks[6], (E, NSC), jnp.float32), 'w1_s': jax.random.normal(ks[7], (MUL, MUL), jnp.float32), 'w1_v': jax.random.normal(ks[8], (MUL, MUL), jnp.float32), 'Wfc1': jax.random.normal(ks[9], (NSC, HID), jnp.float32), 'Wfc2': jax.random.normal(ks[10], (HID, WNUM), jnp.float32), 'w2_s': jax.random.normal(ks[11], (2, MUL, MUL), jnp.float32), 'w2_v': jax.random.normal(ks[12], (2, MUL, MUL), jnp.float32)}
    _L2_gnn_all = _L2_gnn_setup()
    _L2_gnn_in = {k: v for k, v in _L2_gnn_all.items() if k in ('w1_s', 'w1_v', 'Wfc1', 'Wfc2', 'w2_s', 'w2_v')}
    del _L2_gnn_all

    def _L3_gnn_setup():
        import jax, jax.numpy as jnp
        import numpy as np
        N, C, E = (625, 128, 10000)
        H1, O1 = (4, 32)
        H2, O2 = (8, 16)
        CONCAT = H1 * O1 + H2 * O2

        def _layer_norm(x, g, b, eps=1e-05):
            mu = x.mean(-1, keepdims=True)
            var = ((x - mu) ** 2).mean(-1, keepdims=True)
            return (x - mu) * jax.lax.rsqrt(var + eps) * g + b

        def _gat(x, W, a_src, a_dst, bias, src, dst, n_nodes, heads, out_ch):
            h = (x @ W).reshape(n_nodes, heads, out_ch)
            alpha_s = (h * a_src).sum(-1)
            alpha_d = (h * a_dst).sum(-1)
            e = jax.nn.leaky_relu(alpha_s[src] + alpha_d[dst], negative_slope=0.2)
            m = jax.ops.segment_max(e, dst, num_segments=n_nodes)
            e = jnp.exp(e - m[dst])
            denom = jax.ops.segment_sum(e, dst, num_segments=n_nodes)
            alpha = e / (denom[dst] + 1e-16)
            msg = h[src] * alpha[:, :, None]
            out = jax.ops.segment_sum(msg, dst, num_segments=n_nodes)
            return out.reshape(n_nodes, heads * out_ch) + bias
        key = jax.random.key(seed)
        ks = jax.random.split(key, 12)
        x = jax.random.normal(ks[0], (N, C), jnp.float32)
        edge_index = jax.random.randint(ks[1], (2, E), 0, N, jnp.int64)
        s = 1.0 / np.sqrt(C)
        return {'x': x, 'edge_index': edge_index, 'ln_g': jnp.ones((C,), jnp.float32), 'ln_b': jnp.zeros((C,), jnp.float32), 'W1': jax.random.normal(ks[2], (C, H1 * O1), jnp.float32) * s, 'a1s': jax.random.normal(ks[3], (H1, O1), jnp.float32) * 0.1, 'a1d': jax.random.normal(ks[4], (H1, O1), jnp.float32) * 0.1, 'b1': jnp.zeros((H1 * O1,), jnp.float32), 'W2': jax.random.normal(ks[5], (C, H2 * O2), jnp.float32) * s, 'a2s': jax.random.normal(ks[6], (H2, O2), jnp.float32) * 0.1, 'a2d': jax.random.normal(ks[7], (H2, O2), jnp.float32) * 0.1, 'b2': jnp.zeros((H2 * O2,), jnp.float32), 'Wu': jax.random.normal(ks[8], (CONCAT, C), jnp.float32) / np.sqrt(CONCAT), 'bu': jnp.zeros((C,), jnp.float32)}
    _L3_gnn_all = _L3_gnn_setup()
    _L3_gnn_in = {k: v for k, v in _L3_gnn_all.items() if k in ('ln_g', 'ln_b', 'W1', 'a1s', 'a1d', 'b1', 'W2', 'a2s', 'a2d', 'b2', 'Wu', 'bu')}
    del _L3_gnn_all
    return {'x': x, 'src': src, 'dst': dst, 'edge_attr_4': edge_attr_4, 'edge_attr_8': edge_attr_8, 'edge_type_8': edge_type_8, 'node_vec1': node_vec1, 'node_vec1_n2': node_vec1_n2, 'L0_gnn_W': _L0_gnn_in['W'], 'L1_gnn_W': _L1_gnn_in['W'], 'L1_gnn_att_q': _L1_gnn_in['att_q'], 'L1_gnn_att_k': _L1_gnn_in['att_k'], 'L1_gnn_bias': _L1_gnn_in['bias'], 'L2_gnn_w1_s': _L2_gnn_in['w1_s'], 'L2_gnn_w1_v': _L2_gnn_in['w1_v'], 'L2_gnn_Wfc1': _L2_gnn_in['Wfc1'], 'L2_gnn_Wfc2': _L2_gnn_in['Wfc2'], 'L2_gnn_w2_s': _L2_gnn_in['w2_s'], 'L2_gnn_w2_v': _L2_gnn_in['w2_v'], 'L3_gnn_ln_g': _L3_gnn_in['ln_g'], 'L3_gnn_ln_b': _L3_gnn_in['ln_b'], 'L3_gnn_W1': _L3_gnn_in['W1'], 'L3_gnn_a1s': _L3_gnn_in['a1s'], 'L3_gnn_a1d': _L3_gnn_in['a1d'], 'L3_gnn_b1': _L3_gnn_in['b1'], 'L3_gnn_W2': _L3_gnn_in['W2'], 'L3_gnn_a2s': _L3_gnn_in['a2s'], 'L3_gnn_a2d': _L3_gnn_in['a2d'], 'L3_gnn_b2': _L3_gnn_in['b2'], 'L3_gnn_Wu': _L3_gnn_in['Wu'], 'L3_gnn_bu': _L3_gnn_in['bu']}

def reference(x, src, dst, edge_attr_4, edge_attr_8, edge_type_8, node_vec1, node_vec1_n2, L0_gnn_W, L1_gnn_W, L1_gnn_att_q, L1_gnn_att_k, L1_gnn_bias, L2_gnn_w1_s, L2_gnn_w1_v, L2_gnn_Wfc1, L2_gnn_Wfc2, L2_gnn_w2_s, L2_gnn_w2_v, L3_gnn_ln_g, L3_gnn_ln_b, L3_gnn_W1, L3_gnn_a1s, L3_gnn_a1d, L3_gnn_b1, L3_gnn_W2, L3_gnn_a2s, L3_gnn_a2d, L3_gnn_b2, L3_gnn_Wu, L3_gnn_bu):
    import jax
    import jax.numpy as jnp

    def _L0_gnn_ref(x, edge_index, W):
        import jax, jax.numpy as jnp
        import numpy as np
        N, E, D_IN, D_OUT = (100000, 625000, 128, 128)
        n = x.shape[0]
        loops = jnp.arange(n, dtype=edge_index.dtype)
        src = jnp.concatenate([edge_index[0], loops])
        dst = jnp.concatenate([edge_index[1], loops])
        h = x @ W
        deg = jax.ops.segment_sum(jnp.ones(src.shape, dtype=h.dtype), src, num_segments=n)
        norm = jnp.where(deg > 0, jax.lax.rsqrt(deg), jnp.zeros((), h.dtype))
        msg = h[src] * norm[src, None]
        agg = jax.ops.segment_sum(msg, dst, num_segments=n)
        agg = agg * norm[:, None]
        l2 = jnp.sqrt(jnp.sum(agg * agg, axis=1, keepdims=True))
        out = jnp.tanh(agg / jnp.maximum(l2, 1e-12))
        return out

    def _L1_gnn_ref(x, W, att_q, att_k, bias, edge_index, edge_type):
        import jax, jax.numpy as jnp
        import numpy as np
        N_NODES = 50000
        N_EDGES = 500000
        F_DIM = 128
        N_REL = 8
        N_LAYERS = 2
        NEG_SLOPE = 0.2

        def _segment_softmax(logits, seg, num_segments):
            m = jax.ops.segment_max(logits, seg, num_segments=num_segments)
            m = jax.lax.stop_gradient(m)
            e = jnp.exp(logits - m[seg])
            denom = jax.ops.segment_sum(e, seg, num_segments=num_segments)
            return e / (denom[seg] + 1e-16)

        def _rgat_layer(h, src, dst, edge_type, W, q, k, b):
            n = h.shape[0]
            xw = jnp.einsum('nf,rfg->rng', h, W)
            out_j = xw[edge_type, src]
            out_i = xw[edge_type, dst]
            logits = jax.nn.leaky_relu((out_i @ q + out_j @ k)[:, 0], NEG_SLOPE)
            alpha = _segment_softmax(logits, dst, n)
            agg = jax.ops.segment_sum(alpha[:, None] * out_j, dst, num_segments=n)
            return agg + b
        src, dst = (edge_index[0], edge_index[1])
        h = x
        for l in range(W.shape[0]):
            h = _rgat_layer(h, src, dst, edge_type, W[l], att_q[l], att_k[l], bias[l])
            h = jax.nn.relu(h)
        return h

    def _L2_gnn_ref(node_input, node_attr_input, node_attr_output, edge_src, edge_dst, edge_attr, edge_scalar_attr, w1_s, w1_v, Wfc1, Wfc2, w2_s, w2_v):
        import jax, jax.numpy as jnp
        import numpy as np
        N = 25000
        E = 6250
        MUL = 32
        NSC = 8
        HID = 64
        WNUM = 4 * MUL
        NUM_NEIGH = 16.0
        INV_SQRT3 = 1.0 / np.sqrt(3.0)
        n = node_input.shape[0]
        xs = node_input[:, :MUL]
        xv = node_input[:, MUL:].reshape(n, MUL, 3)
        a = node_attr_input[:, 0]
        inv1 = 1.0 / np.sqrt(MUL * 1.0)
        xs1 = jnp.einsum('nu,n,uw->nw', xs, a, w1_s) * inv1
        xv1 = jnp.einsum('nui,n,uw->nwi', xv, a, w1_v) * inv1
        h = jax.nn.silu(edge_scalar_attr @ Wfc1 * (1.0 / np.sqrt(NSC)))
        w = (h @ Wfc2 * (1.0 / np.sqrt(HID))).reshape(-1, 4, MUL)
        es = xs1[edge_src]
        ev = xv1[edge_src]
        ys = edge_attr[:, 0]
        yv = edge_attr[:, 1:4]
        m0 = w[:, 0] * es * ys[:, None]
        m3 = w[:, 3] * jnp.einsum('eui,ei->eu', ev, yv) * INV_SQRT3
        m1 = w[:, 1][:, :, None] * es[:, :, None] * yv[:, None, :]
        m2 = w[:, 2][:, :, None] * ev * ys[:, None, None]
        ne = m0.shape[0]
        edge_features = jnp.concatenate([m0, m3, m1.reshape(ne, 3 * MUL), m2.reshape(ne, 3 * MUL)], axis=1)
        mid = jax.ops.segment_sum(edge_features, edge_dst, num_segments=n)
        mid = mid / np.sqrt(NUM_NEIGH)
        b = node_attr_output[:, 0]
        inv2 = 1.0 / np.sqrt(2.0 * MUL)
        s0 = mid[:, :MUL]
        s1 = mid[:, MUL:2 * MUL]
        v1 = mid[:, 2 * MUL:2 * MUL + 3 * MUL].reshape(n, MUL, 3)
        v2 = mid[:, 2 * MUL + 3 * MUL:].reshape(n, MUL, 3)
        out_s = (jnp.einsum('nu,n,uw->nw', s0, b, w2_s[0]) + jnp.einsum('nu,n,uw->nw', s1, b, w2_s[1])) * inv2
        out_v = (jnp.einsum('nui,n,uw->nwi', v1, b, w2_v[0]) + jnp.einsum('nui,n,uw->nwi', v2, b, w2_v[1])) * inv2
        return jnp.concatenate([out_s, out_v.reshape(n, 3 * MUL)], axis=1)

    def _L3_gnn_ref(x, edge_index, ln_g, ln_b, W1, a1s, a1d, b1, W2, a2s, a2d, b2, Wu, bu):
        import jax, jax.numpy as jnp
        import numpy as np
        N, C, E = (625, 128, 10000)
        H1, O1 = (4, 32)
        H2, O2 = (8, 16)
        CONCAT = H1 * O1 + H2 * O2

        def _layer_norm(x, g, b, eps=1e-05):
            mu = x.mean(-1, keepdims=True)
            var = ((x - mu) ** 2).mean(-1, keepdims=True)
            return (x - mu) * jax.lax.rsqrt(var + eps) * g + b

        def _gat(x, W, a_src, a_dst, bias, src, dst, n_nodes, heads, out_ch):
            h = (x @ W).reshape(n_nodes, heads, out_ch)
            alpha_s = (h * a_src).sum(-1)
            alpha_d = (h * a_dst).sum(-1)
            e = jax.nn.leaky_relu(alpha_s[src] + alpha_d[dst], negative_slope=0.2)
            m = jax.ops.segment_max(e, dst, num_segments=n_nodes)
            e = jnp.exp(e - m[dst])
            denom = jax.ops.segment_sum(e, dst, num_segments=n_nodes)
            alpha = e / (denom[dst] + 1e-16)
            msg = h[src] * alpha[:, :, None]
            out = jax.ops.segment_sum(msg, dst, num_segments=n_nodes)
            return out.reshape(n_nodes, heads * out_ch) + bias
        n = x.shape[0]
        loops = jnp.arange(n, dtype=edge_index.dtype)
        src = jnp.concatenate([edge_index[0], loops])
        dst = jnp.concatenate([edge_index[1], loops])
        x_norm = _layer_norm(x, ln_g, ln_b)
        out1 = _gat(x_norm, W1, a1s, a1d, b1, src, dst, n, H1, O1)
        out2 = _gat(x_norm, W2, a2s, a2d, b2, src, dst, n, H2, O2)
        x_cat = jax.nn.elu(jnp.concatenate([out1, out2], axis=-1))
        return x + x_cat @ Wu + bu
    edge_index = jnp.stack([src, dst])
    h = jnp.maximum(_layernorm(x, axis=-1), 0.0)
    x = x + _L0_gnn_ref(h, edge_index, L0_gnn_W)
    h = jnp.maximum(_layernorm(x, axis=-1), 0.0)
    x = x + _L1_gnn_ref(h, L1_gnn_W, L1_gnn_att_q, L1_gnn_att_k, L1_gnn_bias, edge_index, edge_type_8)
    h = jnp.maximum(_layernorm(x, axis=-1), 0.0)
    x = x + _L2_gnn_ref(h, node_vec1, node_vec1_n2, src, dst, edge_attr_4, edge_attr_8, L2_gnn_w1_s, L2_gnn_w1_v, L2_gnn_Wfc1, L2_gnn_Wfc2, L2_gnn_w2_s, L2_gnn_w2_v)
    h = jnp.maximum(_layernorm(x, axis=-1), 0.0)
    x = x + _L3_gnn_ref(h, edge_index, L3_gnn_ln_g, L3_gnn_ln_b, L3_gnn_W1, L3_gnn_a1s, L3_gnn_a1d, L3_gnn_b1, L3_gnn_W2, L3_gnn_a2s, L3_gnn_a2d, L3_gnn_b2, L3_gnn_Wu, L3_gnn_bu)
    return x

_drawn_inputs = setup_inputs


def setup_inputs(seed=0):
    import zlib

    import numpy as np

    out = dict(_drawn_inputs(seed))
    spreads = {'L1_gnn_bias': (0.0, 0.1),
     'L3_gnn_ln_g': (1.0, 0.2),
     'L3_gnn_ln_b': (0.0, 0.1),
     'L3_gnn_b1': (0.0, 0.1),
     'L3_gnn_b2': (0.0, 0.1),
     'L3_gnn_bu': (0.0, 0.1)}
    factors = {'L1_gnn_att_q': 4.709, 'L1_gnn_att_k': 4.208, 'L3_gnn_a1d': 31.406, 'L3_gnn_a2d': 54.871}
    for name, (base, spread) in spreads.items():
        noise = np.random.default_rng([zlib.crc32(name.encode()), seed]).standard_normal(out[name].shape)
        drawn = base * np.exp(spread * noise) if base else spread * noise
        out[name] = jnp.asarray(drawn.astype(out[name].dtype))
    for name, factor in factors.items():
        out[name] = (out[name] * factor).astype(out[name].dtype)
    return out
```

```python
from collections import namedtuple
from contextlib import ExitStack

import numpy as np
import concourse.bass as bass
from concourse import mybir

F32 = mybir.dt.float32
F16 = mybir.dt.float16
I32 = mybir.dt.int32
ALU = mybir.AluOpType
ACT = mybir.ActivationFunctionType
AX = mybir.AxisListType

N, D = 50000, 128
E = 25000
P = 128
SUP = 1024
H, J = 2, 4
HW = J * P
NI = -(-E // SUP)
EP = NI * SUP
T = EP // P
W = EP // P
EROWS = E // W
HL = 512
NPAD = -(-N // HL) * HL
HR = NPAD // HL
NV = 400
NVR = N // NV
R_ = 8
NREL_LAYERS = 2
MUL, NSC, HID = 32, 8, 64
H1, O1, H2, O2 = 4, 32, 8, 16
NH = H1 + H2
EPS_LN = 1e-5
EPS_SM = 1e-16
BIG = 1e30
NOWHERE = 1 << 20

TABROWS = N + EP
HROWS = EP + 1


def now(i, h):
    return H * i + h + 1 + H


def before(i, h):
    return H * i + h + 1


class Chain:

    def __init__(self, eng, sem, per=0):
        self.eng, self.sem, self.per, self.n, self.i = eng, sem, per, 0, None

    def turn(self, i):
        if self.n:
            assert self.n == self.per, (self.n, self.per)
        self.n, self.i = 0, i

    def step(self, instruction):
        instruction.then_inc(self.sem, 1)
        self.n += 1
        value = self.n if self.i is None else self.i * self.per + self.n
        self.eng.wait_ge(self.sem, value)


def wait_alone(g, eng, sem, value):
    eng.wait_ge(sem, value)
    eng.sem_inc(g.state.waits, 1)


def events(g, prefix, names):
    return namedtuple("Events", names)(*[g.sem(prefix + n) for n in names])


class State:

    def __init__(self):
        self.sems, self.runs, self.waits, self.msg = [], 0, None, None


def dense_identity(nc, g):
    ctx = ExitStack()
    s_i = g.sem("s_ident")
    with ctx:
        iota_i = ctx.enter_context(nc.sbuf_tensor("iota_i", [P, HL], I32))
        iota_e = ctx.enter_context(nc.sbuf_tensor("iota_e", [P, T], I32))
        block = ctx.enter_context(nc.Block())

        @block.gpsimd
        def _(pool):
            pool.memset(g.ident[:, :], 0.0).then_inc(s_i, 1)
            pool.wait_ge(s_i, 1)
            pool.affine_select(out=g.ident[:, :], in_=g.ident[:, :], compare_op=ALU.not_equal, fill=1.0,
                               base=0, pattern=[[-1, P]], channel_multiplier=1).then_inc(s_i, 1)
            pool.iota(iota_i[:, :], pattern=[[1, HL]], base=0, channel_multiplier=0).then_inc(s_i, 1)
            pool.memset(g.ex[:, :, :], 1.0).then_inc(s_i, 1)
            n = 4
            for k, (first, width) in enumerate(((0, O1), (H1, O2))):
                for sign, base in ((1, width * first), (-1, width - 1 - width * first)):
                    pool.wait_ge(s_i, n)
                    pool.affine_select(out=g.ex[:, k, :], in_=g.ex[:, k, :], compare_op=ALU.is_ge, fill=0.0, base=base,
                                       pattern=[[sign, P]], channel_multiplier=-sign * width).then_inc(s_i, 1)
                    n += 1
            pool.iota(iota_e[:, :], pattern=[[P, T]], base=1, channel_multiplier=1).then_inc(s_i, 1)

        @block.vector
        def _(v):
            v.memset(g.eps_ln[:, :], EPS_LN)
            v.memset(g.ones_row[:, :], 1.0)
            v.memset(g.ones_col[:, :], 1.0)
            v.memset(g.log2_col[:, :], float(np.log(2.0)))
            v.wait_ge(s_i, 9)
            v.tensor_copy(g.iota_lo[:, :], iota_i[:, :])
            v.tensor_copy(g.edge_no[:, :], iota_e[:, :])


def edges_in(nc, g):
    ctx = ExitStack()
    s_load, s_dst, s_shift, s_vec, s_back = (g.sem(n) for n in ("ei_load", "ei_dst", "ei_shift", "ei_vec", "ei_back"))
    s_pad, s_v, s_wide, s_pe, s_attr = (g.sem(n) for n in ("ei_pad", "ei_v", "ei_wide", "ei_pe", "ei_attr"))
    K = 5
    SRC_H, SRC_C, DST_C, PUT, _TYP = range(K)
    TH = T // 2
    with ctx:
        sb = lambda n, s, d=F32: ctx.enter_context(nc.sbuf_tensor(n, s, d))
        raw = sb("ei_raw", [P, 3, W], I32)
        near = sb("ei_near", [P, 3, W], I32)
        nearf = sb("ei_nearf", [P, 3, W])
        vec = sb("ei_vec_t", [P, K, W])
        real = sb("ei_real", [P, W])
        tmp = sb("ei_tmp", [P, W])
        back = sb("ei_back_t", [TH, 2, K, P])
        ends = sb("ei_ends", [1, 2], I32)
        zero = sb("ei_zero", [P, W * NSC])
        ps = ctx.enter_context(nc.psum_tensor("ei_ps", [P, 2, HL], F32))
        block = ctx.enter_context(nc.Block())

        @block.sync
        def _(sp):
            sp.wait_ge(s_pad, 1)
            for rows, a, k in ((g.attr8_s, g.attr8, NSC), (g.attr4_s, g.attr4, 4)):
                sp.dma_start(rows[0:E, :].rearrange("(p w) k -> p (w k)", w=W), a.rearrange("(p w) k -> p (w k)", w=W)).then_inc(s_attr, 16)
                sp.dma_start(rows[E:EP, :].rearrange("(p w) k -> p (w k)", w=W), zero[0:P - EROWS, 0:W * k]).then_inc(s_attr, 16)
            for k, a in enumerate((g.src, g.dst, g.typ)):
                sp.dma_start(raw[0:EROWS, k, :], a.rearrange("(p w) -> p w", w=W)).then_inc(s_load, 16)
            sp.wait_ge(s_load, 48)
            sp.wait_ge(s_attr, 64)
            sp.dma_start(g.dst_s[1:1 + EP].rearrange("(p w) -> p w", w=W), raw[:, 1, :]).then_inc(s_dst, 16)
            sp.dma_start(g.dst_s[0:1].unsqueeze(0), ends[0:1, 0:1]).then_inc(s_dst, 16)
            sp.dma_start(g.dst_s[EP + 1:EP + 2].unsqueeze(0), ends[0:1, 1:2]).then_inc(s_dst, 16)
            sp.wait_ge(s_dst, 48)
            for k in range(3):
                sp.dma_start(near[:, k, :], g.dst_s[k:k + EP].rearrange("(p w) -> p w", w=W)).then_inc(s_shift, 16)
            sp.wait_ge(s_wide, 1)
            for k in range(K):
                sp.dma_start(g.vec_s[k, :].rearrange("(p w) -> p w", w=W), vec[:, k, :]).then_inc(s_vec, 16)
            sp.dma_start(g.keep_s.rearrange("(p w) -> p w", w=W), g.keep_w[:, :]).then_inc(s_vec, 16)
            sp.wait_ge(s_vec, 16 * (K + 1))
            for a in range(2):
                for k in range(K):
                    sp.dma_start(back[:, a, k, :],
                                 g.vec_s[k, a * TH * P:(a + 1) * TH * P].rearrange("(t p) -> t p", p=P)).then_inc(s_back, 16)

        @block.vector
        def _(v):
            c = Chain(v, s_v)
            v.memset(raw[:, 0, :], float(127 * HL))
            v.memset(raw[:, 1, :], float(N))
            v.memset(zero[:, :], 0.0)
            v.memset(ends[0:1, 0:1], -1.0)
            v.memset(ends[0:1, 1:2], float(N + 1))
            v.memset(raw[:, 2, :], 0.0).then_inc(s_pad, 1)
            v.wait_ge(s_shift, 48)
            v.wait_ge(s_load, 48)
            c.step(v.tensor_copy(nearf[:, :, :], near[:, :, :]))
            v.tensor_tensor(g.keep_w[:, :], nearf[:, 1, :], nearf[:, 0, :], ALU.is_equal)
            v.tensor_tensor(g.more_w[:, :], nearf[:, 1, :], nearf[:, 2, :], ALU.is_equal)
            v.tensor_copy(vec[:, SRC_H, :], raw[:, 0, :])
            c.step(v.tensor_copy(g.typ_w[:, :], raw[:, 2, :]))
            v.tensor_copy(vec[:, _TYP, :], g.typ_w[:, :])
            v.tensor_scalar(g.last_w[:, :], g.more_w[:, :], -1.0, 1.0, ALU.mult, ALU.add)
            v.tensor_scalar(g.keepneg_w[:, :], g.keep_w[:, :], -1.0, BIG, ALU.add, ALU.mult)
            v.tensor_scalar(vec[:, SRC_C, :], vec[:, SRC_H, :], float(N - 1), None, ALU.min)
            v.tensor_scalar(vec[:, DST_C, :], nearf[:, 1, :], float(N - 1), None, ALU.min)
            c.step(v.tensor_scalar(real[:, :], nearf[:, 1, :], float(N), None, ALU.is_lt))
            c.step(v.tensor_tensor(tmp[:, :], real[:, :], g.last_w[:, :], ALU.mult))
            c.step(v.scalar_tensor_tensor(real[:, :], nearf[:, 1, :], float(-NOWHERE), tmp[:, :], ALU.add, ALU.mult))
            c.step(v.tensor_scalar(real[:, :], real[:, :], float(NOWHERE), None, ALU.add))
            v.tensor_copy(vec[:, PUT, :], real[:, :]).then_inc(s_wide, 1)
            v.wait_ge(s_pe, 2 * K)
            for k, (dest, kind) in enumerate(((g.src_f, 0), (g.src_c, 1), (g.dst_c, 1), (g.put, 1), (g.typ_t, 0))):
                for a in range(2):
                    v.tensor_copy(dest[:, a * TH:(a + 1) * TH], ps[:, a, k * TH:(k + 1) * TH])

        @block.tensor
        def _(pe):
            pe.wait_ge(s_back, 16 * 2 * K)
            for a in range(2):
                for k in range(K):
                    pe.transpose(ps[:, a, k * TH:(k + 1) * TH], back[:, a, k, :], g.ident[0:TH, 0:TH]).then_inc(s_pe, 1)


def degrees(nc, g):
    ctx = ExitStack()
    PER = 8
    s_bits, s_cmp, s_mm, s_out, s_zero, s_put = (g.sem(n) for n in ("dg_bits", "dg_cmp", "dg_mm", "dg_out", "dg_zero", "dg_put"))
    s_v, s_z, s_p, s_deg = g.sem("dg_v"), g.sem("dg_z"), g.sem("dg_p"), g.sem("dg_deg")
    with ctx:
        sb = lambda n, s, d=F32: ctx.enter_context(nc.sbuf_tensor(n, s, d))
        src_i = sb("dg_src", [P, T], I32)
        part_i = sb("dg_part", [P, 2, T], I32)
        part = sb("dg_partf", [P, 2, T])
        lo1 = sb("dg_lo1", [P, PER, HL], F16)
        hi1 = sb("dg_hi1", [P, PER, P], F16)
        hist = sb("dg_hist", [HR, HL])
        zero = sb("dg_zero_t", [P, NPAD // P])
        zh = sb("dg_zh", [P, HL], F16)
        put_now = sb("dg_put_now", [P, PER], I32)
        no_now = sb("dg_no_now", [P, PER])
        ps = ctx.enter_context(nc.psum_tensor("dg_ps", [P, HL], F32))
        block = ctx.enter_context(nc.Block())

        @block.sync
        def _(sp):
            sp.wait_ge(s_z, 1)
            sp.dma_start(g.lastno_s[:, 0].rearrange("(p w) -> p w", p=P), zero[:, :]).then_inc(s_zero, 16)
            sp.wait_ge(s_out, 1)
            sp.dma_start(g.deg_s.rearrange("(p w) -> p w", w=HL), hist[:, :]).then_inc(s_deg, 16)
            sp.wait_ge(s_deg, 16)

        @block.gpsimd
        def _(pool):
            pool.wait_ge(s_zero, 16)
            with pool.Fori(0, T // PER) as i:
                pool.tensor_copy(put_now[:, :], g.put[:, bass.ds(i * PER, PER)]).then_inc(s_p, 1)
                pool.tensor_copy(no_now[:, :], g.edge_no[:, bass.ds(i * PER, PER)]).then_inc(s_p, 1)
                wait_alone(g, pool, s_p, i * 2 + 2)
                for k in range(PER):
                    pool.indirect_dma_start(g.lastno_s, bass.IndirectOffsetOnAxis(ap=put_now[:, k:k + 1], axis=0),
                                            no_now[:, k:k + 1], None, bounds_check=N - 1, oob_is_err=False).then_inc(s_put, 16)
                wait_alone(g, pool, s_put, i * 16 * PER + 16 * PER)

        @block.vector
        def _(v):
            v.memset(zh[:, :], 0.0)
            v.memset(zero[:, :], 0.0).then_inc(s_z, 1)
            c = Chain(v, s_v)
            c.step(v.tensor_copy(src_i[:, :], g.src_f[:, :]))
            v.tensor_scalar(part_i[:, 0, :], src_i[:, :], 9, None, ALU.logical_shift_right)
            c.step(v.tensor_scalar(part_i[:, 1, :], src_i[:, :], HL - 1, None, ALU.bitwise_and))
            c.step(v.tensor_copy(part[:, :, :], part_i[:, :, :]))
            v.sem_inc(s_cmp, PER)
            with v.Fori(0, T // PER) as i:
                for k in range(PER):
                    v.wait_ge(s_mm, i * PER + k + 1)
                    v.tensor_scalar(hi1[:, k, :], g.iota_lo[:, 0:P], part[:, 0, bass.ds(i * PER + k, 1)], None, ALU.is_equal)
                    v.tensor_scalar(lo1[:, k, :], g.iota_lo[:, :], part[:, 1, bass.ds(i * PER + k, 1)], None,
                                    ALU.is_equal).then_inc(s_cmp, 1)
            v.wait_ge(s_bits, 1)
            v.tensor_scalar(hist[:, :], ps[0:HR, :], 1.0, None, ALU.add).then_inc(s_out, 1)

        @block.tensor
        def _(pe):
            pe.wait_ge(s_z, 1)
            pe.matmul(ps[:, :], zh[:, 0:P], zh[:, :], start=True, stop=False)
            pe.sem_inc(s_mm, PER)
            with pe.Fori(0, T // PER) as i:
                for k in range(PER):
                    pe.wait_ge(s_cmp, i * PER + PER + k + 1)
                    pe.matmul(ps[:, :], hi1[:, k, :], lo1[:, k, :], start=False, stop=False).then_inc(s_mm, 1)
            pe.matmul(ps[:, :], zh[:, 0:P], zh[:, :], start=False, stop=True).then_inc(s_bits, 1)


def node_info(nc, g):
    ctx = ExitStack()
    s_in, s_v, s_a, s_row, s_out, s_p = (g.sem(n) for n in ("ni_in", "ni_v", "ni_a", "ni_row", "ni_out", "ni_p"))
    s_gs, s_gd, s_taken = g.sem("ni_gs"), g.sem("ni_gd"), g.sem("ni_taken")
    PER = 8
    with ctx:
        sb = lambda n, s, d=F32: ctx.enter_context(nc.sbuf_tensor(n, s, d))
        cols = sb("ni_cols", [NVR, 4, NV])
        rows = sb("ni_rows", [NVR, NV, 4])
        by_src = sb("ni_src", [P, T, 4])
        by_dst = sb("ni_dst", [P, T, 4])
        slot = sb("ni_slot", [P, 2, PER, 4])
        at_src = sb("ni_at_src", [P, PER], I32)
        at_dst = sb("ni_at_dst", [P, PER], I32)
        has = sb("ni_has", [P, T])
        part = sb("ni_part", [P, T])
        alls = sb("ni_alls", [P, T])
        block = ctx.enter_context(nc.Block())

        @block.sync
        def _(sp):
            for k, a in enumerate((g.deg_s[0:N], g.lastno_s[0:N, 0], g.vec1[:, 0], g.vec2[:, 0])):
                sp.dma_start(cols[:, k, :], a.rearrange("(p w) -> p w", w=NV)).then_inc(s_in, 16)
            sp.wait_ge(s_row, 1)
            sp.dma_start(g.info_s.rearrange("(p w) k -> p (w k)", w=NV), rows[:, :, :].rearrange("p w k -> p (w k)")).then_inc(s_out, 16)

        @block.scalar
        def _(a):
            a.preload_act_table_set("natural_log_exp_and_others")
            a.wait_ge(s_in, 64)
            a.activation(cols[:, 0, :], cols[:, 0, :], ACT.Ln).then_inc(s_a, 1)
            a.wait_ge(s_a, 1)
            a.activation(cols[:, 0, :], cols[:, 0, :], ACT.Exp, scale=-0.5).then_inc(s_a, 1)

        @block.gpsimd
        def _(pool):
            pool.wait_ge(s_out, 16)
            with pool.Fori(0, T // PER) as i:
                wait_alone(g, pool, s_taken, i * 2 + 2)
                pool.tensor_copy(at_src[:, :], g.src_c[:, bass.ds(i * PER, PER)]).then_inc(s_p, 1)
                pool.tensor_copy(at_dst[:, :], g.dst_c[:, bass.ds(i * PER, PER)]).then_inc(s_p, 1)
                wait_alone(g, pool, s_p, i * 2 + 2)
                for k in range(PER):
                    pool.indirect_dma_start(slot[:, 0, k, :], None, g.info_s,
                                            bass.IndirectOffsetOnAxis(ap=at_src[:, k:k + 1], axis=0)).then_inc(s_gs, 16)
                    pool.indirect_dma_start(slot[:, 1, k, :], None, g.info_s,
                                            bass.IndirectOffsetOnAxis(ap=at_dst[:, k:k + 1], axis=0)).then_inc(s_gd, 16)

        @block.vector
        def _(v):
            v.wait_ge(s_a, 2)
            v.wait_ge(s_in, 64)
            v.tensor_copy(rows[:, :, :].rearrange("p w k -> p k w"), cols[:, :, :]).then_inc(s_row, 1)
            c = Chain(v, s_v)
            v.sem_inc(s_taken, 2)
            with v.Fori(0, T // PER) as i:
                for k, (s_g, dest) in enumerate(((s_gs, by_src), (s_gd, by_dst))):
                    v.wait_ge(s_g, i * 16 * PER + 16 * PER)
                    v.tensor_copy(dest[:, bass.ds(i * PER, PER), :], slot[:, k, :, :]).then_inc(s_taken, 1)
            v.wait_ge(s_taken, 2 + 2 * T // PER)
            v.tensor_copy(g.norm_src[:, :], by_src[:, :, 0])
            v.tensor_copy(g.vec_src[:, :], by_src[:, :, 2])
            v.tensor_copy(g.norm_dst[:, :], by_dst[:, :, 0])
            v.tensor_scalar(g.vec_dst[:, :], by_dst[:, :, 3], 1.0 / (4.0 * 8.0), None, ALU.mult)
            c.step(v.tensor_scalar(has[:, :], by_src[:, :, 1], 0.5, None, ALU.is_gt))
            v.tensor_scalar(g.nohas[:, :], has[:, :], -1.0, 1.0, ALU.mult, ALU.add)
            c.step(v.tensor_copy(alls[:, :], g.src_c[:, :]))
            for dest, base, other in ((g.row_x, N, 0), (g.row_h, 0, EP)):
                if other:
                    c.step(v.tensor_scalar(part[:, :], by_src[:, :, 1], float(base - 1 - other), None, ALU.add))
                    c.step(v.tensor_tensor(part[:, :], part[:, :], has[:, :], ALU.mult))
                    c.step(v.tensor_scalar(dest[:, :], part[:, :], float(other), None, ALU.add))
                else:
                    c.step(v.scalar_tensor_tensor(part[:, :], by_src[:, :, 1], float(base - 1), alls[:, :], ALU.add, ALU.subtract))
                    c.step(v.tensor_tensor(part[:, :], part[:, :], has[:, :], ALU.mult))
                    c.step(v.tensor_tensor(dest[:, :], part[:, :], alls[:, :], ALU.add))


def weights(nc, g):
    ctx = ExitStack()
    s_ld, s_z, s_zd, s_big, s_bl, s_pe, s_v, s_a, s_d, s_w = (g.sem("wt_" + n) for n in ("ld", "z", "zd", "big", "bl", "pe", "v", "a", "d", "w"))
    with ctx:
        sb = lambda n, s, d=F32: ctx.enter_context(nc.sbuf_tensor(n, s, d))
        zero = sb("wt_zero", [P, 3 * P])
        wT = sb("wt_T", [P, 18, P])
        att = sb("wt_att", [P, 2, 2 * NH])
        bu = sb("wt_bu", [1, P])
        ps = ctx.enter_context(nc.psum_tensor("wt_ps", [P, 5, 4, P], F32))
        pm = ctx.enter_context(nc.psum_tensor("wt_pm", [P, 2, HL], F32))
        block = ctx.enter_context(nc.Block())
        col = lambda a: a.unsqueeze(1)
        loads = [(g.w0[:, :], g.L0_W), (g.w12[:, 0:P], g.L3_W1), (g.w12[:, P:2 * P], g.L3_W2),
                 (g.wu[:, :, :], g.L3_Wu.rearrange("(k p) n -> p k n", p=P)),
                 (g.wr[:, :, :], g.L1_W.rearrange("l r f g -> f (l r) g")),
                 (g.wfc1[:, :], g.L2_Wfc1), (g.wfc2[:, :], g.L2_Wfc2), (bu[0:1, :], g.L3_bu.unsqueeze(0)),
                 (g.b1_rows[:, :], g.L1_bias[1, :].partition_broadcast(P))]
        for l in range(2):
            loads += [(g.att_q[:, l:l + 1], g.L1_att_q[l, :, :]), (g.att_k[:, l:l + 1], g.L1_att_k[l, :, :]),
                      (g.b1_col[:, l:l + 1], col(g.L1_bias[l, :]))]
        loads += [(g.ln_g[:, :], col(g.L3_ln_g)), (g.ln_b[:, :], col(g.L3_ln_b)),
                  (g.b12[:, 0:1], col(g.L3_b1)), (g.b12[:, 1:2], col(g.L3_b2))]
        heads = []
        for h in range(H1):
            heads += [(att[O1 * h:O1 * h + O1, 0, h:h + 1], col(g.L3_a1s[h, :])),
                      (att[O1 * h:O1 * h + O1, 0, NH + h:NH + h + 1], col(g.L3_a1d[h, :]))]
        for h in range(H2):
            heads += [(att[O2 * h:O2 * h + O2, 1, H1 + h:H1 + h + 1], col(g.L3_a2s[h, :])),
                      (att[O2 * h:O2 * h + O2, 1, NH + H1 + h:NH + H1 + h + 1], col(g.L3_a2d[h, :]))]
        S, V = MUL, 3 * MUL
        pieces = [(g.w1big_s[0:S, 0:S], g.L2_w1_s), (g.w2big_s[0:S, 0:S], g.L2_w2_s[0, :, :]),
                  (g.w2big_s[S:2 * S, 0:S], g.L2_w2_s[1, :, :])]
        for i in range(3):
            at = lambda rows, base: rows[base:base + V, S:S + V].rearrange("(u a) (w b) -> a b u w", a=3, b=3)[i, i, :, :]
            pieces += [(at(g.w1big_s, S), g.L2_w1_v), (at(g.w2big_s, 2 * S), g.L2_w2_v[0, :, :]),
                       (at(g.w2big_s, 2 * S + V), g.L2_w2_v[1, :, :])]

        @block.sync
        def _(sp):
            for dest, src in loads:
                sp.dma_start(dest, src).then_inc(s_ld, 16)
            sp.wait_ge(s_z, 1)
            sp.dma_start(g.w1big_s, zero[:, 0:P]).then_inc(s_zd, 16)
            sp.dma_start(g.w2big_s.rearrange("(k p) n -> p k n", p=P), zero[:, P:3 * P].rearrange("p (k n) -> p k n", k=2)).then_inc(s_zd, 16)
            for dest, src in heads:
                sp.dma_start(dest, src).then_inc(s_ld, 16)
            sp.wait_ge(s_zd, 32)
            with nc.allow_non_contiguous_dma(reason="small weights laid out once"):
                for dest, src in pieces:
                    sp.dma_start(dest, src).then_inc(s_big, 16)
            sp.wait_ge(s_big, 16 * len(pieces))
            sp.dma_start(g.w1big[:, :], g.w1big_s).then_inc(s_bl, 16)
            sp.dma_start(g.w2big[:, :, :], g.w2big_s.rearrange("(k p) n -> p k n", p=P)).then_inc(s_bl, 16)
            sp.wait_ge(s_w, 1)
            sp.dma_start(g.h_tab[EP:EP + 1, :], g.b0_row[0:1, :]).then_inc(s_d, 16)
            sp.wait_ge(s_d, 16)

        @block.vector
        def _(v):
            v.memset(att[:, :, :], 0.0)
            v.memset(zero[:, :], 0.0).then_inc(s_z, 1)
            c = Chain(v, s_v)
            v.wait_ge(s_ld, 16 * (len(loads) + len(heads)))
            c.step(v.tensor_scalar(g.b1_rows[:, :], g.b1_rows[:, :], 0.0, None, ALU.max))
            v.wait_ge(s_pe, 18)
            for n in range(18):
                v.tensor_copy(wT[:, n, :], ps[:, n // 4, n % 4, :])
            v.wait_ge(s_bl, 32)
            v.tensor_scalar(g.w1big[:, :], g.w1big[:, :], float(1 / np.sqrt(MUL)), None, ALU.mult)
            v.tensor_scalar(g.w2big[S:2 * S, 0, :], g.w2big[S:2 * S, 0, :], float(1 / np.sqrt(3.0)), None, ALU.mult)
            c.step(v.tensor_scalar(g.wfc2[:, :], g.wfc2[:, :], float(1 / np.sqrt(HID)), None, ALU.mult))
            v.wait_ge(s_pe, 18 + 3)
            v.tensor_copy(g.wq[:, :], pm[:, 0, 0:16])
            v.tensor_copy(g.wa[:, :], pm[:, 0, 16:16 + 2 * NH])
            v.tensor_tensor(g.bu_row[0:1, :], bu[0:1, :], pm[0:1, 1, 0:P], ALU.subtract)
            v.tensor_scalar(g.b0_row[0:1, :], pm[0:1, 1, P:2 * P], 0.0, None, ALU.max).then_inc(s_w, 1)

        @block.tensor
        def _(pe):
            pe.wait_ge(s_ld, 16 * (len(loads) + len(heads)))
            for n in range(16):
                pe.transpose(ps[:, n // 4, n % 4, :], g.wr[:, n, :], g.ident[:, :]).then_inc(s_pe, 1)
            for n in range(2):
                pe.transpose(ps[:, 4, n, :], g.w12[:, n * P:(n + 1) * P], g.ident[:, :]).then_inc(s_pe, 1)
            pe.wait_ge(s_v, 2)
            for n in range(16):
                last = pe.matmul(pm[:, 0, n:n + 1], wT[:, n, :], g.att_q[:, n // R_:n // R_ + 1], start=True, stop=True)
            last.then_inc(s_pe, 1)
            for k in range(2):
                last = pe.matmul(pm[:, 0, 16:16 + 2 * NH], wT[:, 16 + k, :], att[:, k, :], start=(k == 0), stop=(k == 1))
            last.then_inc(s_pe, 1)
            for k in range(2):
                pe.matmul(pm[0:1, 1, 0:P], g.ones_col[:, :], g.wu[:, k, :], start=(k == 0), stop=(k == 1))
            pe.matmul(pm[0:1, 1, P:2 * P], g.b1_col[:, 0:1], g.ident[:, :], start=True, stop=True).then_inc(s_pe, 1)


def credit(eng, *sems):
    for s in sems:
        eng.sem_inc(s, H)


def stats(v, c, g, x4, st, mv, done):
    for j in range(J):
        last = v.bn_stats(st[:, j, :], x4[:, j, :])
    c.step(last)
    v.sem_inc(g.state.waits, 1)
    for j in range(J):
        last = v.bn_aggr(mv[:, j, :], st[:, j, :])
    last.then_inc(done, 1)


def rstd(a, g, s_self, value, mv, rs, done):
    a.activation(rs[:, :], mv[:, :, 1], ACT.Ln, bias=g.eps_ln[:, :]).then_inc(s_self, 1)
    a.wait_ge(s_self, value)
    a.activation(rs[:, :], rs[:, :], ACT.Exp, scale=-0.5).then_inc(done, 1)


def normalise(v, x4, mv, rs, y4, done):
    for j in range(J):
        last = v.tensor_scalar(y4[:, j, :], x4[:, j, :], mv[:, j, 0:1], rs[:, j:j + 1], ALU.subtract, ALU.mult)
    last.then_inc(done, 1)


def transpose4(pe, g, ps, y4, done):
    for j in range(J):
        last = pe.transpose(ps[:, j * P:(j + 1) * P], y4[:, j, :], g.ident[:, :])
    last.then_inc(done, 1)


def four(t):
    return t.rearrange("p (j f) -> p j f", j=J)


def node_dense(nc, g):
    ctx = ExitStack()
    names = "st rs ya t1 e1 yy ss ssw ri q r2 x1 z sz rz nm hh sh rh nn t2 e2 o eo u ou zh fo".split()
    ev = events(g, "nd_", names)
    s_v, s_a = g.sem("nd_v"), g.sem("nd_a")
    l_x, l_d, w_1, w_o = ([g.sem(f"nd_{n}{h}") for h in range(H)] for n in ("lx", "ld", "w1", "wo"))
    with ctx:
        sb = lambda n, s, d=F32: ctx.enter_context(nc.sbuf_tensor("nd_" + n, s, d))
        two = lambda n, s: [sb(f"{n}{h}", s) for h in range(H)]
        x, y, junk, x1, z, hh, n_, ot, et = (two(n, [P, J, P]) for n in ("x", "y", "junk", "x1", "z", "hh", "n", "ot", "et"))
        aT, nT = two("aT", [P, HW]), two("nT", [P, HW])
        eo, ro, u = (two(n, [P, 2, HW]) for n in ("eo", "ro", "u"))
        st, mv, stz, mvz, sth, mvh = (two(n, [P, J, 6 if n[:2] == "st" else 2]) for n in ("st", "mv", "stz", "mvz", "sth", "mvh"))
        rs, rz, rh, nm, ss, ssw, ri, q, deg, inv = (two(n, [P, J]) for n in ("rs", "rz", "rh", "nm", "ss", "ssw", "ri", "q", "deg", "inv"))
        pT = [ctx.enter_context(nc.psum_tensor(f"nd_pT{h}", [P, HW], F32)) for h in range(H)]
        pY = [ctx.enter_context(nc.psum_tensor(f"nd_pY{h}", [P, HW], F32)) for h in range(H)]
        pO = [ctx.enter_context(nc.psum_tensor(f"nd_pO{h}", [P, 2, HW], F32)) for h in range(H)]
        block = ctx.enter_context(nc.Block())
        FULL = N // SUP

        def sweep(eng, body):
            with eng.Fori(0, FULL) as i:
                body(i, i * SUP)
            body(FULL, N - SUP)

        def rows(a, base, h):
            return a[bass.ds(base, SUP), :].rearrange("(p j) f -> p j f", j=H * J)[:, h * J:(h + 1) * J, :]

        @block.sync
        def _(sp):
            def body(i, base):
                for h in range(H):
                    sp.wait_ge(ev.x1, before(i, h))
                    sp.dma_start(x[h][:, :, :], rows(g.x, base, h)).then_inc(l_x[h], 16)
                    sp.dma_start(deg[h][:, :], g.deg_s[bass.ds(base, SUP)].rearrange("(p j) -> p j", j=H * J)[:, h * J:(h + 1) * J]).then_inc(l_d[h], 16)
                for h in range(H):
                    sp.wait_ge(ev.x1, now(i, h))
                    if i is FULL and h == 0:
                        for k in range(H):
                            sp.wait_ge(w_1[k], 32 * FULL)
                            sp.wait_ge(w_o[k], 16 * FULL)
                    for table in (g.tab_a, g.tab_b):
                        sp.dma_start(rows(table, base, h), x1[h][:, :, :]).then_inc(w_1[h], 16)
                for h in range(H):
                    sp.wait_ge(ev.fo, now(i, h))
                    sp.dma_start(rows(g.out, base, h), ot[h][:, :, :]).then_inc(w_o[h], 16)
            sweep(sp, body)
            for h in range(H):
                sp.wait_ge(w_1[h], 32 * (FULL + 1))
                sp.wait_ge(w_o[h], 16 * (FULL + 1))

        @block.gpsimd
        def _(pool):
            credit(pool, ev.zh)

            def body(i, base):
                for h in range(H):
                    pool.wait_ge(ev.hh, now(i, h))
                    pool.tensor_tensor(z[h][:, :, :], z[h][:, :, :], hh[h][:, :, :], ALU.add).then_inc(ev.zh, 1)
            sweep(pool, body)

        @block.vector
        def _(v):
            credit(v, ev.st, ev.ya, ev.ssw, ev.q, ev.x1, ev.z, ev.sz, ev.nm, ev.sh, ev.nn, ev.u, ev.fo)
            c = Chain(v, s_v, 14)

            def body(i, base):
                c.turn(i)
                for h in range(H):
                    v.wait_ge(l_x[h], 16 * i + 16)
                    stats(v, c, g, x[h], st[h], mv[h], ev.st)
                for h in range(H):
                    v.wait_ge(ev.rs, now(i, h))
                    v.wait_ge(ev.t1, before(i, h))
                    normalise(v, x[h], mv[h], rs[h], y[h], ev.ya)
                for h in range(H):
                    v.wait_ge(l_d[h], 16 * i + 16)
                    c.step(v.reciprocal(inv[h][:, :], deg[h][:, :]))
                    v.wait_ge(ev.ss, now(i, h))
                    c.step(v.tensor_tensor(ssw[h][:, :], ss[h][:, :], inv[h][:, :], ALU.mult))
                    c.step(v.tensor_tensor(ssw[h][:, :], ssw[h][:, :], inv[h][:, :], ALU.mult))
                    v.tensor_scalar(ssw[h][:, :], ssw[h][:, :], 1e-30, None, ALU.max).then_inc(ev.ssw, 1)
                for h in range(H):
                    v.wait_ge(ev.ri, now(i, h))
                    c.step(v.scalar_tensor_tensor(q[h][:, :], ri[h][:, :], 1e12, inv[h][:, :], ALU.min, ALU.mult))
                    v.tensor_scalar(q[h][:, :], q[h][:, :], 2.0, None, ALU.mult).then_inc(ev.q, 1)
                for h in range(H):
                    v.wait_ge(ev.r2, now(i, h))
                    v.wait_ge(w_1[h], 32 * i)
                    v.scalar_tensor_tensor(x1[h][:, :, :], x[h][:, :, :], 1.0, et[h][:, :, :], ALU.add, ALU.subtract).then_inc(ev.x1, 1)
                    v.wait_ge(ev.x1, now(i, h))
                    v.wait_ge(ev.fo, before(i, h))
                    v.tensor_tensor(z[h][:, :, :], x1[h][:, :, :], g.b1_rows[:, :].unsqueeze(1).broadcast_to([P, J, P]), ALU.add).then_inc(ev.z, 1)
                    v.wait_ge(ev.z, now(i, h))
                    stats(v, c, g, z[h], stz[h], mvz[h], ev.sz)
                for h in range(H):
                    v.wait_ge(ev.rz, now(i, h))
                    v.scalar_tensor_tensor(nm[h][:, :], mvz[h][:, :, 0], -1.0, rz[h][:, :], ALU.mult, ALU.mult).then_inc(ev.nm, 1)
                for h in range(H):
                    v.wait_ge(ev.hh, now(i, h))
                    stats(v, c, g, hh[h], sth[h], mvh[h], ev.sh)
                for h in range(H):
                    v.wait_ge(ev.rh, now(i, h))
                    v.wait_ge(ev.t2, before(i, h))
                    normalise(v, hh[h], mvh[h], rh[h], n_[h], ev.nn)
                for h in range(H):
                    v.wait_ge(ev.eo, now(i, h))
                    v.wait_ge(ev.ou, before(i, h))
                    v.scalar_tensor_tensor(u[h][:, :, :], eo[h][:, :, :], 1.0, ro[h][:, :, :], ALU.min, ALU.add).then_inc(ev.u, 1)
                for h in range(H):
                    v.wait_ge(ev.ou, now(i, h))
                    v.wait_ge(ev.zh, now(i, h))
                    v.wait_ge(w_o[h], 16 * i)
                    v.tensor_tensor(ot[h][:, :, :], four(pY[h][:, :]), z[h][:, :, :], ALU.add).then_inc(ev.fo, 1)
            sweep(v, body)

        @block.scalar
        def _(a):
            a.preload_act_table_set("natural_log_exp_and_others")
            credit(a, ev.rs, ev.e1, ev.ss, ev.ri, ev.r2, ev.rz, ev.hh, ev.rh, ev.e2, ev.eo)

            def body(i, base):
                own = lambda k: i * 12 + k
                for h in range(H):
                    a.wait_ge(ev.st, now(i, h))
                    rstd(a, g, s_a, own(1 + h), mv[h], rs[h], ev.rs)
                for h in range(H):
                    a.wait_ge(ev.t1, now(i, h))
                    a.wait_ge(ev.yy, before(i, h))
                    a.activation(aT[h][:, :], pT[h][:, :], ACT.Relu).then_inc(ev.e1, 1)
                for h in range(H):
                    a.wait_ge(ev.yy, now(i, h))
                    a.wait_ge(ev.ss, before(i, h))
                    for j in range(J):
                        last = a.activation(junk[h][:, j, :], pY[h][:, j * P:(j + 1) * P], ACT.Square, accum_out=ss[h][:, j:j + 1])
                    last.then_inc(ev.ss, 1)
                for h in range(H):
                    a.wait_ge(ev.ssw, now(i, h))
                    a.activation(ri[h][:, :], ssw[h][:, :], ACT.Ln).then_inc(s_a, 1)
                    a.wait_ge(s_a, own(3 + h))
                    a.activation(ri[h][:, :], ri[h][:, :], ACT.Exp, scale=-0.5).then_inc(ev.ri, 1)
                for h in range(H):
                    a.wait_ge(ev.q, now(i, h))
                    a.wait_ge(ev.x1, before(i, h))
                    for j in range(J):
                        last = a.activation(et[h][:, j, :], pY[h][:, j * P:(j + 1) * P], ACT.Exp, scale=q[h][:, j:j + 1])
                    last.then_inc(s_a, 1)
                    a.wait_ge(s_a, own(5 + 2 * h))
                    a.activation(et[h][:, :, :], et[h][:, :, :], ACT.Ln, bias=1.0).then_inc(s_a, 1)
                    a.wait_ge(s_a, own(6 + 2 * h))
                    a.activation(et[h][:, :, :], et[h][:, :, :], ACT.Exp, scale=-1.0, bias=g.log2_col[:, :]).then_inc(ev.r2, 1)
                for h in range(H):
                    a.wait_ge(ev.sz, now(i, h))
                    rstd(a, g, s_a, own(9 + h), mvz[h], rz[h], ev.rz)
                for h in range(H):
                    a.wait_ge(ev.nm, now(i, h))
                    a.wait_ge(ev.zh, before(i, h))
                    a.wait_ge(ev.nn, before(i, h))
                    for j in range(J):
                        last = a.activation(hh[h][:, j, :], z[h][:, j, :], ACT.Relu, scale=rz[h][:, j:j + 1], bias=nm[h][:, j:j + 1])
                    last.then_inc(ev.hh, 1)
                for h in range(H):
                    a.wait_ge(ev.sh, now(i, h))
                    rstd(a, g, s_a, own(11 + h), mvh[h], rh[h], ev.rh)
                for h in range(H):
                    a.wait_ge(ev.t2, now(i, h))
                    a.wait_ge(ev.o, before(i, h))
                    a.activation(nT[h][:, :], pT[h][:, :], ACT.Identity, scale=g.ln_g[:, :], bias=g.ln_b[:, :]).then_inc(ev.e2, 1)
                for h in range(H):
                    a.wait_ge(ev.o, now(i, h))
                    a.wait_ge(ev.u, before(i, h))
                    for k in range(2):
                        a.activation(eo[h][:, k, :], pO[h][:, k, :], ACT.Exp, bias=g.b12[:, k:k + 1])
                        last = a.activation(ro[h][:, k, :], pO[h][:, k, :], ACT.Relu, bias=g.b12[:, k:k + 1])
                    last.then_inc(ev.eo, 1)
            sweep(a, body)

        @block.tensor
        def _(pe):
            credit(pe, ev.t1, ev.yy, ev.t2, ev.o, ev.ou)

            def body(i, base):
                for h in range(H):
                    pe.wait_ge(ev.ya, now(i, h))
                    pe.wait_ge(ev.e2, before(i, h))
                    transpose4(pe, g, pT[h], y[h], ev.t1)
                for h in range(H):
                    pe.wait_ge(ev.e1, now(i, h))
                    pe.wait_ge(ev.fo, before(i, h))
                    for j in range(J):
                        last = pe.matmul(pY[h][:, j * P:(j + 1) * P], aT[h][:, j * P:(j + 1) * P], g.w0[:, :], start=True, stop=True)
                    last.then_inc(ev.yy, 1)
                for h in range(H):
                    pe.wait_ge(ev.nn, now(i, h))
                    transpose4(pe, g, pT[h], n_[h], ev.t2)
                for h in range(H):
                    pe.wait_ge(ev.e2, now(i, h))
                    pe.wait_ge(ev.eo, before(i, h))
                    for k in range(2):
                        last = pe.matmul(pO[h][:, k, :], g.w12[:, k * P:(k + 1) * P], nT[h][:, :], start=True, stop=True)
                    last.then_inc(ev.o, 1)
                for h in range(H):
                    pe.wait_ge(ev.u, now(i, h))
                    pe.wait_ge(ev.r2, now(i, h))
                    for j in range(J):
                        o = pY[h][:, j * P:(j + 1) * P]
                        pe.matmul(o, u[h][:, 0, j * P:(j + 1) * P], g.wu[:, 0, :], start=True, stop=False)
                        pe.matmul(o, u[h][:, 1, j * P:(j + 1) * P], g.wu[:, 1, :], start=False, stop=False)
                        last = pe.matmul(o, g.ones_row[:, :], g.bu_row[:, :], start=False, stop=True)
                    last.then_inc(ev.ou, 1)
            sweep(pe, body)


def halves(nc, ctx, prefix):
    sb = lambda n, s, d=F32: ctx.enter_context(nc.sbuf_tensor(prefix + n, s, d))
    two = lambda n, s, d=F32: [sb(f"{n}{h}", s, d) for h in range(H)]
    bank = lambda n: [ctx.enter_context(nc.psum_tensor(f"{prefix}{n}{h}", [P, HW], F32)) for h in range(H)]
    return sb, two, bank


def edge_rows(a, base, i, h):
    return a[bass.ds(i * SUP + base + h * HW, HW), :].rearrange("(j p) f -> p j f", p=P)


def row_part(a, i, h):
    return a[bass.ds(i * SUP + h * HW, HW)].partition_broadcast(P)


def gather(pool, table, index, dest, done):
    for j in range(J):
        pool.indirect_dma_start(dest[:, j, :], None, table, bass.IndirectOffsetOnAxis(ap=index[:, j:j + 1], axis=0)).then_inc(done, 16)


def layer0_edges(nc, g):
    ctx = ExitStack()
    names = "st sd rs rd ys yd ts td gs gd sc yy ss ssw ri q r2 x1 sx rx yx tx hx pq pe".split()
    ev = events(g, "e0_", names)
    s_v, s_a, s_p, s_0 = g.sem("e0_v"), g.sem("e0_a"), g.sem("e0_p"), g.sem("e0_zero")
    l_s, l_d, l_k, w_x, w_q = ([g.sem(f"e0_{n}{h}") for h in range(H)] for n in ("ls", "ld", "lk", "wx", "wq"))
    with ctx:
        sb, two, bank = halves(nc, ctx, "e0_")
        xs, xd, y, yx, junk, et, x1 = (two(n, [P, J, P]) for n in ("xs", "xd", "y", "yx", "junk", "et", "x1"))
        yd = two("yd", [P, J, P])
        keep, gT, dT, hT = (two(n, [P, HW]) for n in ("keep", "gT", "dT", "hT"))
        agg = two("agg", [P, HW])
        at_s, at_d = two("at_s", [P, J], I32), two("at_d", [P, J], I32)
        st, mv, sd, md, sx, mx = (two(n, [P, J, 6 if n[0] == "s" else 2]) for n in ("st", "mv", "sd", "md", "sx", "mx"))
        rs, rd, rx, ns, nd, ss, ssw, ri, q = (two(n, [P, J]) for n in ("rs", "rd", "rx", "ns", "nd", "ss", "ssw", "ri", "q"))
        pq = two("pq", [R_, HW])
        pS, pD, pY, pQ = bank("pS"), bank("pD"), bank("pY"), bank("pQ")
        block = ctx.enter_context(nc.Block())

        @block.sync
        def _(sp):
            with sp.Fori(0, NI) as i:
                for h in range(H):
                    sp.wait_ge(ev.sc, before(i, h))
                    sp.dma_start(keep[h][:, :], row_part(g.keep_s, i, h)).then_inc(l_k[h], 16)
                for h in range(H):
                    sp.wait_ge(ev.x1, now(i, h))
                    sp.dma_start(edge_rows(g.tab_a, N, i, h), x1[h][:, :, :]).then_inc(w_x[h], 16)
                for h in range(H):
                    sp.wait_ge(ev.pe, now(i, h))
                    sp.dma_start(g.pq_s[:, bass.ds(i * SUP + h * HW, HW)], pq[h][:, :]).then_inc(w_q[h], 16)
            for h in range(H):
                sp.wait_ge(w_x[h], 16 * NI)
                sp.wait_ge(w_q[h], 16 * NI)

        @block.gpsimd
        def _(pool):
            with pool.Fori(0, NI) as i:
                for h in range(H):
                    wait_alone(g, pool, ev.ys, before(i, h))
                    pool.tensor_copy(at_s[h][:, :], g.src_c[:, bass.ds(i * H * J + h * J, J)]).then_inc(s_p, 1)
                    wait_alone(g, pool, s_p, i * 4 + h + 1)
                    gather(pool, g.x, at_s[h], xs[h], l_s[h])
                for h in range(H):
                    wait_alone(g, pool, ev.x1, before(i, h))
                    pool.tensor_copy(at_d[h][:, :], g.dst_c[:, bass.ds(i * H * J + h * J, J)]).then_inc(s_p, 1)
                    wait_alone(g, pool, s_p, i * 4 + h + 3)
                    gather(pool, g.x, at_d[h], xd[h], l_d[h])

        @block.vector
        def _(v):
            credit(v, ev.st, ev.sd, ev.ys, ev.yd, ev.sc, ev.ssw, ev.q, ev.x1, ev.sx, ev.yx)
            v.memset(agg[H - 1][:, HW - 1:HW], 0.0).then_inc(s_0, 1)
            v.wait_ge(s_0, 1)
            c = Chain(v, s_v, 16)
            with v.Fori(0, NI) as i:
                c.turn(i)
                for h in range(H):
                    v.wait_ge(l_s[h], 64 * i + 64)
                    stats(v, c, g, xs[h], st[h], mv[h], ev.st)
                for h in range(H):
                    v.wait_ge(l_d[h], 64 * i + 64)
                    stats(v, c, g, xd[h], sd[h], md[h], ev.sd)
                for h in range(H):
                    tiles = bass.ds(i * H * J + h * J, J)
                    v.wait_ge(ev.rs, now(i, h))
                    c.step(v.tensor_tensor(ns[h][:, :], rs[h][:, :], g.norm_src[:, tiles], ALU.mult))
                    v.wait_ge(ev.ts, before(i, h))
                    normalise(v, xs[h], mv[h], ns[h], y[h], ev.ys)
                for h in range(H):
                    tiles = bass.ds(i * H * J + h * J, J)
                    v.wait_ge(ev.rd, now(i, h))
                    c.step(v.tensor_tensor(nd[h][:, :], rd[h][:, :], g.norm_dst[:, tiles], ALU.mult))
                    v.wait_ge(ev.td, before(i, h))
                    normalise(v, xd[h], md[h], nd[h], yd[h], ev.yd)
                for h in range(H):
                    v.wait_ge(ev.gs, now(i, h))
                    v.wait_ge(l_k[h], 16 * i + 16)
                    v.wait_ge(ev.yy, before(i, h))
                    if h:
                        v.wait_ge(ev.sc, now(i, 0))
                    v.tensor_tensor_scan(agg[h][:, :], keep[h][:, :], gT[h][:, :], agg[1 - h][:, HW - 1:HW], ALU.mult, ALU.add).then_inc(ev.sc, 1)
                for h in range(H):
                    tiles = bass.ds(i * H * J + h * J, J)
                    v.wait_ge(ev.ss, now(i, h))
                    c.step(v.tensor_tensor(ssw[h][:, :], ss[h][:, :], g.norm_dst[:, tiles], ALU.mult))
                    c.step(v.tensor_tensor(ssw[h][:, :], ssw[h][:, :], g.norm_dst[:, tiles], ALU.mult))
                    v.tensor_scalar(ssw[h][:, :], ssw[h][:, :], 1e-30, None, ALU.max).then_inc(ev.ssw, 1)
                for h in range(H):
                    tiles = bass.ds(i * H * J + h * J, J)
                    v.wait_ge(ev.ri, now(i, h))
                    c.step(v.scalar_tensor_tensor(q[h][:, :], ri[h][:, :], 1e12, g.norm_dst[:, tiles], ALU.min, ALU.mult))
                    v.tensor_scalar(q[h][:, :], q[h][:, :], 2.0, None, ALU.mult).then_inc(ev.q, 1)
                for h in range(H):
                    v.wait_ge(ev.r2, now(i, h))
                    v.wait_ge(w_x[h], 16 * i)
                    v.scalar_tensor_tensor(x1[h][:, :, :], xd[h][:, :, :], 1.0, et[h][:, :, :], ALU.add, ALU.subtract).then_inc(ev.x1, 1)
                    v.wait_ge(ev.x1, now(i, h))
                    stats(v, c, g, x1[h], sx[h], mx[h], ev.sx)
                for h in range(H):
                    v.wait_ge(ev.rx, now(i, h))
                    v.wait_ge(ev.tx, before(i, h))
                    normalise(v, x1[h], mx[h], rx[h], yx[h], ev.yx)
                c.turn(i)

        @block.scalar
        def _(a):
            a.preload_act_table_set("natural_log_exp_and_others")
            credit(a, ev.rs, ev.rd, ev.gs, ev.gd, ev.ss, ev.ri, ev.r2, ev.rx, ev.hx, ev.pe)
            with a.Fori(0, NI) as i:
                own = lambda k: i * 12 + k
                for h in range(H):
                    a.wait_ge(ev.st, now(i, h))
                    rstd(a, g, s_a, own(1 + h), mv[h], rs[h], ev.rs)
                for h in range(H):
                    a.wait_ge(ev.sd, now(i, h))
                    rstd(a, g, s_a, own(3 + h), md[h], rd[h], ev.rd)
                for h in range(H):
                    a.wait_ge(ev.ts, now(i, h))
                    a.wait_ge(ev.sc, before(i, h))
                    a.activation(gT[h][:, :], pS[h][:, :], ACT.Relu).then_inc(ev.gs, 1)
                for h in range(H):
                    a.wait_ge(ev.td, now(i, h))
                    a.wait_ge(ev.yy, before(i, h))
                    a.activation(dT[h][:, :], pD[h][:, :], ACT.Relu).then_inc(ev.gd, 1)
                for h in range(H):
                    a.wait_ge(ev.yy, now(i, h))
                    a.wait_ge(ev.ss, before(i, h))
                    for j in range(J):
                        last = a.activation(junk[h][:, j, :], pY[h][:, j * P:(j + 1) * P], ACT.Square, accum_out=ss[h][:, j:j + 1])
                    last.then_inc(ev.ss, 1)
                for h in range(H):
                    a.wait_ge(ev.ssw, now(i, h))
                    a.activation(ri[h][:, :], ssw[h][:, :], ACT.Ln).then_inc(s_a, 1)
                    a.wait_ge(s_a, own(5 + h))
                    a.activation(ri[h][:, :], ri[h][:, :], ACT.Exp, scale=-0.5).then_inc(ev.ri, 1)
                for h in range(H):
                    a.wait_ge(ev.q, now(i, h))
                    a.wait_ge(ev.x1, before(i, h))
                    for j in range(J):
                        last = a.activation(et[h][:, j, :], pY[h][:, j * P:(j + 1) * P], ACT.Exp, scale=q[h][:, j:j + 1])
                    last.then_inc(s_a, 1)
                    a.wait_ge(s_a, own(7 + 2 * h))
                    a.activation(et[h][:, :, :], et[h][:, :, :], ACT.Ln, bias=1.0).then_inc(s_a, 1)
                    a.wait_ge(s_a, own(8 + 2 * h))
                    a.activation(et[h][:, :, :], et[h][:, :, :], ACT.Exp, scale=-1.0, bias=g.log2_col[:, :]).then_inc(ev.r2, 1)
                for h in range(H):
                    a.wait_ge(ev.sx, now(i, h))
                    rstd(a, g, s_a, own(11 + h), mx[h], rx[h], ev.rx)
                for h in range(H):
                    a.wait_ge(ev.tx, now(i, h))
                    a.wait_ge(ev.pq, before(i, h))
                    a.activation(hT[h][:, :], pS[h][:, :], ACT.Relu).then_inc(ev.hx, 1)
                for h in range(H):
                    a.wait_ge(ev.pq, now(i, h))
                    a.wait_ge(w_q[h], 16 * i)
                    a.activation(pq[h][:, :], pQ[h][0:R_, :], ACT.Copy).then_inc(ev.pe, 1)

        @block.tensor
        def _(pe):
            credit(pe, ev.ts, ev.td, ev.yy, ev.tx, ev.pq)
            with pe.Fori(0, NI) as i:
                for h in range(H):
                    pe.wait_ge(ev.ys, now(i, h))
                    pe.wait_ge(ev.hx, before(i, h))
                    transpose4(pe, g, pS[h], y[h], ev.ts)
                for h in range(H):
                    pe.wait_ge(ev.yd, now(i, h))
                    pe.wait_ge(ev.gd, before(i, h))
                    transpose4(pe, g, pD[h], yd[h], ev.td)
                for h in range(H):
                    pe.wait_ge(ev.sc, now(i, h))
                    pe.wait_ge(ev.gd, now(i, h))
                    pe.wait_ge(ev.r2, before(i, h))
                    for j in range(J):
                        part = slice(j * P, (j + 1) * P)
                        pe.matmul(pY[h][:, part], agg[h][:, part], g.w0[:, :], start=True, stop=False)
                        last = pe.matmul(pY[h][:, part], dT[h][:, part], g.w0[:, :], start=False, stop=True)
                    last.then_inc(ev.yy, 1)
                for h in range(H):
                    pe.wait_ge(ev.yx, now(i, h))
                    pe.wait_ge(ev.gs, now(i, h))
                    transpose4(pe, g, pS[h], yx[h], ev.tx)
                for h in range(H):
                    pe.wait_ge(ev.hx, now(i, h))
                    pe.wait_ge(ev.pe, before(i, h))
                    pe.matmul(pQ[h][0:R_, :], g.wq[:, 0:R_], hT[h][:, :], start=True, stop=True).then_inc(ev.pq, 1)


def relations(nc, g, layer):
    ctx = ExitStack()
    names = "st rs ys ts hT mk mm om kq ke".split()
    pre = f"r{layer}_"
    ev = events(g, pre, names)
    s_v, s_a, s_p = g.sem(pre + "v"), g.sem(pre + "a"), g.sem(pre + "p")
    l_s, l_t, w_k = ([g.sem(f"{pre}{n}{h}") for h in range(H)] for n in ("ls", "lt", "wk"))
    table, index = (g.tab_a, g.row_x) if layer == 0 else (g.h_tab, g.row_h)
    with ctx:
        sb, two, bank = halves(nc, ctx, pre)
        xs, y = two("xs", [P, J, P]), two("y", [P, J, P])
        hT, typ = two("hT", [P, HW]), two("typ", [P, HW])
        NM = 4
        masked = sb("masked", [P, NM, HW])
        at_s = two("at_s", [P, J], I32)
        st, mv, rs = two("st", [P, J, 6]), two("mv", [P, J, 2]), two("rs", [P, J])
        kq = two("kq", [1, HW])
        pS, pM, pK = bank("pS"), bank("pM"), bank("pK")
        block = ctx.enter_context(nc.Block())

        @block.sync
        def _(sp):
            with sp.Fori(0, NI) as i:
                for h in range(H):
                    wait_alone(g, sp, ev.mk, (i * H + h + 1) * R_)
                    sp.dma_start(typ[h][:, :], row_part(g.vec_s[4, :], i, h)).then_inc(l_t[h], 16)
                for h in range(H):
                    wait_alone(g, sp, ev.ke, now(i, h))
                    sp.dma_start(g.kq_s[bass.ds(i * SUP + h * HW, HW)].unsqueeze(0), kq[h][:, :]).then_inc(w_k[h], 16)
            for h in range(H):
                sp.wait_ge(w_k[h], 16 * NI)

        @block.gpsimd
        def _(pool):
            with pool.Fori(0, NI) as i:
                for h in range(H):
                    wait_alone(g, pool, ev.ys if layer == 0 else ev.ts, before(i, h))
                    pool.tensor_copy(at_s[h][:, :], index[:, bass.ds(i * H * J + h * J, J)]).then_inc(s_p, 1)
                    wait_alone(g, pool, s_p, i * 2 + h + 1)
                    gather(pool, table, at_s[h], xs[h], l_s[h])

        @block.vector
        def _(v):
            credit(v, ev.st, ev.ys)
            v.sem_inc(ev.mk, H * R_)
            c = Chain(v, s_v, 2 if layer == 0 else 0)
            with v.Fori(0, NI) as i:
                c.turn(i)
                if layer == 0:
                    for h in range(H):
                        v.wait_ge(l_s[h], 64 * i + 64)
                        stats(v, c, g, xs[h], st[h], mv[h], ev.st)
                    for h in range(H):
                        v.wait_ge(ev.rs, now(i, h))
                        v.wait_ge(ev.ts, before(i, h))
                        normalise(v, xs[h], mv[h], rs[h], y[h], ev.ys)
                for h in range(H):
                    v.wait_ge(ev.hT, now(i, h))
                    v.wait_ge(l_t[h], 16 * i + 16)
                    for r in range(R_):
                        n = h * R_ + r
                        v.wait_ge(ev.mm, i * H * R_ + n + 1)
                        v.scalar_tensor_tensor(masked[:, n % NM, :], typ[h][:, :], float(r), hT[h][:, :], ALU.is_equal,
                                               ALU.mult).then_inc(ev.mk, 1)
                c.turn(i)

        @block.scalar
        def _(a):
            a.preload_act_table_set("natural_log_exp_and_others")
            credit(a, ev.rs, ev.hT, ev.om, ev.ke)
            with a.Fori(0, NI) as i:
                if layer == 0:
                    for h in range(H):
                        a.wait_ge(ev.st, now(i, h))
                        rstd(a, g, s_a, i * 2 + 1 + h, mv[h], rs[h], ev.rs)
                for h in range(H):
                    a.wait_ge(ev.ts, now(i, h))
                    a.wait_ge(ev.mk, (i * H + h + 1) * R_)
                    a.activation(hT[h][:, :], pS[h][:, :], ACT.Relu).then_inc(ev.hT, 1)
                for h in range(H):
                    wait_alone(g, a, ev.mm, (i * H + h + 1) * R_ + NM)
                    a.activation(g.state.msg[:, bass.ds(i * SUP + h * HW, HW)], pM[h][:, :], ACT.Copy).then_inc(ev.om, 1)
                for h in range(H):
                    a.wait_ge(ev.kq, now(i, h))
                    a.wait_ge(w_k[h], 16 * i)
                    a.activation(kq[h][:, :], pK[h][0:1, :], ACT.Copy).then_inc(ev.ke, 1)

        @block.tensor
        def _(pe):
            credit(pe, ev.ts, ev.kq)
            pe.sem_inc(ev.mm, NM)
            with pe.Fori(0, NI) as i:
                for h in range(H):
                    if layer == 0:
                        pe.wait_ge(ev.ys, now(i, h))
                    else:
                        pe.wait_ge(l_s[h], 64 * i + 64)
                    pe.wait_ge(ev.hT, before(i, h))
                    transpose4(pe, g, pS[h], y[h] if layer == 0 else xs[h], ev.ts)
                for h in range(H):
                    pe.wait_ge(ev.om, before(i, h))
                    for r in range(R_):
                        n = h * R_ + r
                        pe.wait_ge(ev.mk, (i + 1) * H * R_ + n + 1)
                        pe.matmul(pM[h][:, :], g.wr[:, layer * R_ + r, :], masked[:, n % NM, :], start=(r == 0), stop=(r == R_ - 1)).then_inc(ev.mm, 1)
                for h in range(H):
                    wait_alone(g, pe, ev.om, now(i, h))
                    wait_alone(g, pe, ev.ke, before(i, h))
                    pe.matmul(pK[h][0:1, :], g.att_k[:, layer:layer + 1], g.state.msg[:, bass.ds(i * SUP + h * HW, HW)], start=True, stop=True).then_inc(ev.kq, 1)


class Segments:

    def __init__(self, nc, ctx, g, prefix, most):
        sb = lambda n, s: ctx.enter_context(nc.sbuf_tensor(prefix + n, s, F32))
        self.ends, self.whole, self.carry = sb("ends", [P, most]), sb("whole", [P, most]), sb("carry", [P, most])
        self.row_ends, self.row_whole, self.row_carry = (sb(n, [most, P]) for n in ("rowe", "roww", "rowc"))
        self.totals = sb("totals", [P, 3])
        self.ps = ctx.enter_context(nc.psum_tensor(prefix + "ps", [P, 4, P], F32))
        self.ends_done, self.turned, self.row_done, self.back = (g.sem(prefix + n) for n in ("e", "t", "r", "b"))
        self.calls = 0
        self.g = g

    def prepare(self, v, c):
        g = self.g
        v.tensor_reduce(self.totals[:, 0:1], g.keep_w[:, :], AX.X, ALU.min)
        v.tensor_reduce(self.totals[:, 1:2], g.keepneg_w[:, :], AX.X, ALU.add)
        c.step(v.tensor_reduce(self.totals[:, 2:3], g.more_w[:, :], AX.X, ALU.min))

    def scan(self, v, c, kind, K, out, data):
        g, n = self.g, self.calls
        self.calls += 1
        mask, total, op0, op1, zero = dict(sum=(g.keep_w, 0, ALU.mult, ALU.add, 0.0), max=(g.keepneg_w, 1, ALU.add, ALU.max, -BIG),
                                           back=(g.more_w, 2, ALU.mult, ALU.add, 0.0))[kind]
        way = (lambda a: a[:, ::-1]) if kind == "back" else (lambda a: a)
        for k in range(K):
            last = v.tensor_tensor_scan(way(out(k)), way(mask[:, :]), way(data(k)), zero, op0, op1)
        c.step(last)
        end = 0 if kind == "back" else W - 1
        for k in range(K):
            v.tensor_copy(self.ends[:, k:k + 1], out(k)[:, end:end + 1])
        v.tensor_copy(self.whole[:, 0:K], self.totals[:, total:total + 1].broadcast_to([P, K])).then_inc(self.ends_done, 1)
        v.wait_ge(self.turned, n + 1)
        v.memset(self.row_carry[0:K, :], zero)
        v.tensor_copy(self.row_ends[0:K, :], self.ps[0:K, 0, :])
        c.step(v.tensor_copy(self.row_whole[0:K, :], self.ps[0:K, 1, :]))
        if kind == "back":
            to, frm = slice(0, P - 1), slice(1, P)
        else:
            to, frm = slice(1, P), slice(0, P - 1)
        v.tensor_tensor_scan(way(self.row_carry[0:K, to]), way(self.row_whole[0:K, frm]), way(self.row_ends[0:K, frm]),
                             zero, op0, op1).then_inc(self.row_done, 1)
        v.wait_ge(self.back, n + 1)
        c.step(v.tensor_copy(self.carry[:, 0:K], self.ps[:, 2, 0:K]))
        for k in range(K):
            last = v.tensor_tensor_scan(way(out(k)), way(mask[:, :]), way(data(k)), self.carry[:, k:k + 1], op0, op1)
        c.step(last)

    def turns(self, pe, Ks):
        g = self.g
        for n, K in enumerate(Ks):
            pe.wait_ge(self.ends_done, n + 1)
            pe.transpose(self.ps[0:K, 0, :], self.ends[:, 0:K], g.ident[:, :])
            pe.transpose(self.ps[0:K, 1, :], self.whole[:, 0:K], g.ident[:, :]).then_inc(self.turned, 1)
            pe.wait_ge(self.row_done, n + 1)
            pe.matmul(self.ps[:, 2, 0:K], self.row_carry[0:K, :], g.ident[0:K, 0:K], start=True, stop=True).then_inc(self.back, 1)


def wide(a):
    return a.rearrange("(p w) -> p w", w=W)


def each(mask, K):
    return mask[:, :].unsqueeze(1).broadcast_to([P, K, W])


def edge_softmax(nc, g, layer):
    ctx = ExitStack()
    pre = f"s{layer}_"
    s_in, s_v, s_l, s_p, s_out = (g.sem(pre + n) for n in ("in", "v", "l", "p", "out"))
    with ctx:
        sb = lambda n, s: ctx.enter_context(nc.sbuf_tensor(pre + n, s, F32))
        pq, pb = sb("pq", [P, R_, W]), sb("pb", [P, R_, W])
        kq, logit, one, most, tot, al = (sb(n, [P, W]) for n in ("kq", "logit", "one", "most", "tot", "al"))
        seg = Segments(nc, ctx, g, pre, R_)
        block = ctx.enter_context(nc.Block())

        @block.sync
        def _(sp):
            for r in range(R_):
                sp.dma_start(pq[:, r, :], wide(g.pq_s[r, :])).then_inc(s_in, 16)
            sp.dma_start(kq[:, :], wide(g.kq_s)).then_inc(s_in, 16)
            sp.wait_ge(s_out, 1)
            sp.dma_start(wide(g.alpha_s), al[:, :]).then_inc(s_p, 16)
            sp.wait_ge(s_p, 16)

        @block.vector
        def _(v):
            c = Chain(v, s_v)
            seg.prepare(v, c)
            v.wait_ge(s_in, 16 * (R_ + 1))
            c.step(v.tensor_tensor(pq[:, :, :], pq[:, :, :], each(g.last_w, R_), ALU.mult))
            seg.scan(v, c, "back", R_, lambda k: pb[:, k, :], lambda k: pq[:, k, :])
            for r in range(R_):
                last = v.scalar_tensor_tensor(pq[:, r, :], g.typ_w[:, :], float(r), pb[:, r, :], ALU.is_equal, ALU.mult)
            c.step(last)
            for r in range(R_):
                c.step(v.tensor_tensor(kq[:, :], kq[:, :], pq[:, r, :], ALU.add))
            c.step(v.scalar_tensor_tensor(logit[:, :], kq[:, :], 0.2, kq[:, :], ALU.mult, ALU.max))
            seg.scan(v, c, "max", 1, lambda k: most[:, :], lambda k: logit[:, :])
            c.step(v.tensor_tensor(one[:, :], most[:, :], g.last_w[:, :], ALU.mult))
            seg.scan(v, c, "back", 1, lambda k: most[:, :], lambda k: one[:, :])
            v.tensor_tensor(logit[:, :], logit[:, :], most[:, :], ALU.subtract).then_inc(s_l, 1)
            v.wait_ge(s_l, 2)
            seg.scan(v, c, "sum", 1, lambda k: tot[:, :], lambda k: logit[:, :])
            c.step(v.tensor_tensor(one[:, :], tot[:, :], g.last_w[:, :], ALU.mult))
            seg.scan(v, c, "back", 1, lambda k: tot[:, :], lambda k: one[:, :])
            c.step(v.tensor_scalar(tot[:, :], tot[:, :], EPS_SM, None, ALU.add))
            c.step(v.reciprocal(one[:, :], tot[:, :]))
            v.tensor_tensor(al[:, :], one[:, :], logit[:, :], ALU.mult).then_inc(s_out, 1)

        @block.scalar
        def _(a):
            a.preload_act_table_set("natural_log_exp_and_others")
            a.wait_ge(s_l, 1)
            a.activation(logit[:, :], logit[:, :], ACT.Exp).then_inc(s_l, 1)

        @block.tensor
        def _(pe):
            seg.turns(pe, (R_, 1, 1, 1, 1))


def aggregate(nc, g, layer):
    ctx = ExitStack()
    pre = f"g{layer}_"
    ev = events(g, pre, "wt sc hT tr ro pq pe".split())
    s_0 = g.sem(pre + "zero")
    l_a, l_k, l_x, w_r, w_q = ([g.sem(f"{pre}{n}{h}") for h in range(H)] for n in ("la", "lk", "lx", "wr", "wq"))
    with ctx:
        sb, two, bank = halves(nc, ctx, pre)
        al, keep, wt, agg, hT = (two(n, [P, HW]) for n in ("al", "keep", "wt", "agg", "hT"))
        rows, x1 = two("rows", [P, J, P]), two("x1", [P, J, P])
        pq = two("pq", [R_, HW])
        pT, pQ = bank("pT"), bank("pQ")
        table, first = (g.h_tab, 0) if layer == 0 else (g.tab_a, N)
        block = ctx.enter_context(nc.Block())

        @block.sync
        def _(sp):
            with sp.Fori(0, NI) as i:
                for h in range(H):
                    wait_alone(g, sp, ev.sc, before(i, h))
                    sp.dma_start(al[h][:, :], row_part(g.alpha_s, i, h)).then_inc(l_a[h], 16)
                    sp.dma_start(keep[h][:, :], row_part(g.keep_s, i, h)).then_inc(l_k[h], 16)
                    if layer:
                        wait_alone(g, sp, ev.ro, before(i, h))
                        sp.dma_start(x1[h][:, :, :], edge_rows(g.tab_a, N, i, h)).then_inc(l_x[h], 16)
                for h in range(H):
                    wait_alone(g, sp, ev.ro, now(i, h))
                    sp.dma_start(edge_rows(table, first, i, h), rows[h][:, :, :]).then_inc(w_r[h], 16)
                    if not layer:
                        wait_alone(g, sp, ev.pe, now(i, h))
                        sp.dma_start(g.pq_s[:, bass.ds(i * SUP + h * HW, HW)], pq[h][:, :]).then_inc(w_q[h], 16)
            for h in range(H):
                sp.wait_ge(w_r[h], 16 * NI)
                if not layer:
                    sp.wait_ge(w_q[h], 16 * NI)

        @block.vector
        def _(v):
            credit(v, ev.wt, ev.sc)
            v.memset(agg[H - 1][:, HW - 1:HW], 0.0).then_inc(s_0, 1)
            v.wait_ge(s_0, 1)
            if layer:
                credit(v, ev.ro)
            with v.Fori(0, NI) as i:
                for h in range(H):
                    v.wait_ge(l_a[h], 16 * i + 16)
                    v.tensor_tensor(wt[h][:, :], g.state.msg[:, bass.ds(i * SUP + h * HW, HW)], al[h][:, :], ALU.mult).then_inc(ev.wt, 1)
                for h in range(H):
                    v.wait_ge(ev.wt, now(i, h))
                    v.wait_ge(l_k[h], 16 * i + 16)
                    v.wait_ge(ev.hT, before(i, h))
                    if h:
                        v.wait_ge(ev.sc, now(i, 0))
                    v.tensor_tensor_scan(agg[h][:, :], keep[h][:, :], wt[h][:, :], agg[1 - h][:, HW - 1:HW], ALU.mult, ALU.add).then_inc(ev.sc, 1)
                if layer:
                    for h in range(H):
                        v.wait_ge(ev.tr, now(i, h))
                        v.wait_ge(l_x[h], 16 * i + 16)
                        v.wait_ge(w_r[h], 16 * i)
                        v.tensor_tensor(rows[h][:, :, :], four(pT[h][:, :]), x1[h][:, :, :], ALU.add).then_inc(ev.ro, 1)

        @block.scalar
        def _(a):
            credit(a, ev.hT, ev.pe)
            if not layer:
                credit(a, ev.ro)
            with a.Fori(0, NI) as i:
                for h in range(H):
                    a.wait_ge(ev.sc, now(i, h))
                    a.wait_ge(ev.tr, before(i, h))
                    if not layer:
                        a.wait_ge(ev.pq, before(i, h))
                    a.activation(hT[h][:, :], agg[h][:, :], ACT.Relu, bias=g.b1_col[:, layer:layer + 1]).then_inc(ev.hT, 1)
                if not layer:
                    for h in range(H):
                        a.wait_ge(ev.tr, now(i, h))
                        a.wait_ge(w_r[h], 16 * i)
                        a.activation(rows[h][:, :, :], four(pT[h][:, :]), ACT.Copy).then_inc(ev.ro, 1)
                        a.wait_ge(ev.pq, now(i, h))
                        a.wait_ge(w_q[h], 16 * i)
                        a.activation(pq[h][:, :], pQ[h][0:R_, :], ACT.Copy).then_inc(ev.pe, 1)

        @block.tensor
        def _(pe):
            credit(pe, ev.tr, ev.pq)
            with pe.Fori(0, NI) as i:
                for h in range(H):
                    pe.wait_ge(ev.hT, now(i, h))
                    pe.wait_ge(ev.ro, before(i, h))
                    transpose4(pe, g, pT[h], four(hT[h][:, :]), ev.tr)
                    if layer == 0:
                        pe.wait_ge(ev.pe, before(i, h))
                        pe.matmul(pQ[h][0:R_, :], g.wq[:, R_:2 * R_], hT[h][:, :], start=True, stop=True).then_inc(ev.pq, 1)


def interaction(nc, g):
    ctx = ExitStack()
    names = "xx st rs ys ts hT ff at ac hd si hi ww wc y4 mm tm mc ll sc tb x3".split()
    ev = events(g, "i_", names)
    s_v, s_a, s_p, s_0 = (g.sem("i_" + n) for n in ("v", "a", "p", "zero"))
    l_s, l_8, l_4, l_k, l_x, w_x = ([g.sem(f"i_{n}{h}") for h in range(H)] for n in ("ls", "l8", "l4", "lk", "lx", "wx"))
    c_in = float(1 / np.sqrt(NSC))
    V3 = 3 * MUL
    with ctx:
        sb, two, bank = halves(nc, ctx, "i_")
        raw, x, y, x2, x3, ws = (two(n, [P, J, P]) for n in ("raw", "x", "y", "x2", "x3", "ws"))
        a8, a4, ya = two("a8", [P, J, NSC]), two("a4", [P, J, 4]), two("ya", [P, J, 4])
        st, mv, rs, nohas, vd = two("st", [P, J, 6]), two("mv", [P, J, 2]), two("rs", [P, J]), two("nohas", [P, J]), two("vd", [P, J])
        keep, hT, agg = two("keep", [P, HW]), two("hT", [P, HW]), two("agg", [P, HW])
        a8T, sg, hid = two("a8T", [NSC, HW]), two("sg", [HID, HW]), two("hid", [HID, HW])
        m, mT = two("m", [P, J, 2 * P]), two("mT", [P, 2, HW])
        t02, t1, g3, r3 = two("t02", [P, J, 2, MUL]), two("t1", [P, J, MUL]), two("g3", [P, J, V3]), two("r3", [P, J, MUL])
        at_s = two("at_s", [P, J], I32)
        pT, pF, pW, pH = bank("pT"), bank("pF"), bank("pW"), bank("pH")
        block = ctx.enter_context(nc.Block())

        @block.sync
        def _(sp):
            with sp.Fori(0, NI) as i:
                for h in range(H):
                    wait_alone(g, sp, ev.at, before(i, h))
                    sp.dma_start(a8[h][:, :, :], edge_rows(g.attr8_s, 0, i, h)).then_inc(l_8[h], 16)
                    wait_alone(g, sp, ev.y4, before(i, h))
                    sp.dma_start(a4[h][:, :, :], edge_rows(g.attr4_s, 0, i, h)).then_inc(l_4[h], 16)
                    wait_alone(g, sp, ev.x3, before(i, h))
                    sp.dma_start(keep[h][:, :], row_part(g.keep_s, i, h)).then_inc(l_k[h], 16)
                    sp.dma_start(x2[h][:, :, :], edge_rows(g.tab_a, N, i, h)).then_inc(l_x[h], 16)
                for h in range(H):
                    wait_alone(g, sp, ev.x3, now(i, h))
                    sp.dma_start(edge_rows(g.tab_b, N, i, h), x3[h][:, :, :]).then_inc(w_x[h], 16)
            for h in range(H):
                sp.wait_ge(w_x[h], 16 * NI)

        @block.gpsimd
        def _(pool):
            with pool.Fori(0, NI) as i:
                for h in range(H):
                    wait_alone(g, pool, ev.xx, before(i, h))
                    pool.tensor_copy(at_s[h][:, :], g.row_x[:, bass.ds(i * H * J + h * J, J)]).then_inc(s_p, 1)
                    wait_alone(g, pool, s_p, i * 2 + h + 1)
                    gather(pool, g.tab_a, at_s[h], raw[h], l_s[h])

        @block.vector
        def _(v):
            credit(v, ev.xx, ev.st, ev.ys, ev.hi, ev.y4, ev.mm, ev.sc, ev.x3)
            v.memset(agg[H - 1][:, HW - 1:HW], 0.0).then_inc(s_0, 1)
            v.wait_ge(s_0, 1)
            c = Chain(v, s_v, 10)
            with v.Fori(0, NI) as i:
                c.turn(i)
                for h in range(H):
                    tiles = bass.ds(i * H * J + h * J, J)
                    v.wait_ge(l_s[h], 64 * i + 64)
                    c.step(v.tensor_copy(nohas[h][:, :], g.nohas[:, tiles]))
                    for j in range(J):
                        last = v.scalar_tensor_tensor(x[h][:, j, :], g.b1_rows[:, :], nohas[h][:, j:j + 1], raw[h][:, j, :], ALU.mult, ALU.add)
                    last.then_inc(ev.xx, 1)
                    v.wait_ge(ev.xx, now(i, h))
                    stats(v, c, g, x[h], st[h], mv[h], ev.st)
                for h in range(H):
                    v.wait_ge(ev.rs, now(i, h))
                    v.wait_ge(ev.ts, before(i, h))
                    normalise(v, x[h], mv[h], rs[h], y[h], ev.ys)
                for h in range(H):
                    v.wait_ge(ev.si, now(i, h))
                    v.scalar_tensor_tensor(hid[h][:, :], pH[h][0:HID, :], c_in, sg[h][:, :], ALU.mult, ALU.mult).then_inc(ev.hi, 1)
                for h in range(H):
                    tiles = bass.ds(i * H * J + h * J, J)
                    v.wait_ge(l_4[h], 16 * i + 16)
                    v.tensor_tensor(ya[h][:, :, :], a4[h][:, :, :], g.vec_src[:, tiles].unsqueeze(2).broadcast_to([P, J, 4]), ALU.mult).then_inc(ev.y4, 1)
                    v.wait_ge(ev.y4, now(i, h))
                    v.wait_ge(ev.wc, now(i, h))
                    v.wait_ge(ev.ff, now(i, h))
                    v.wait_ge(ev.tm, before(i, h))
                    s_f = four(pF[h][:, :])[:, :, 0:MUL]
                    v_f = four(pF[h][:, :])[:, :, MUL:P].rearrange("p j (u i) -> p j u i", i=3)
                    w4 = ws[h][:, :, :].rearrange("p j (k u) -> p j k u", k=4)
                    ys = ya[h][:, :, 0:1]
                    yv = ya[h][:, :, 1:4].unsqueeze(2).broadcast_to([P, J, MUL, 3])
                    g34 = g3[h][:, :, :].rearrange("p j (u i) -> p j u i", i=3)
                    over = lambda a: a.unsqueeze(3).broadcast_to([P, J, MUL, 3])
                    m_v = lambda n: m[h][:, :, 2 * MUL + n * V3:2 * MUL + (n + 1) * V3].rearrange("p j (u i) -> p j u i", i=3)
                    v.tensor_tensor(t02[h][:, :, :, :], w4[:, :, 0::2, :], ys.unsqueeze(3).broadcast_to([P, J, 2, MUL]), ALU.mult)
                    v.tensor_tensor(t1[h][:, :, :], s_f, w4[:, :, 1, :], ALU.mult)
                    c.step(v.tensor_tensor(g34, v_f, yv, ALU.mult))
                    v.tensor_tensor(m[h][:, :, 0:MUL], s_f, t02[h][:, :, 0, :], ALU.mult)
                    v.tensor_tensor(m_v(0), over(t1[h][:, :, :]), yv, ALU.mult)
                    v.tensor_tensor(m_v(1), v_f, over(t02[h][:, :, 1, :]), ALU.mult)
                    c.step(v.tensor_reduce(r3[h][:, :, :], g34, AX.X, ALU.add))
                    v.tensor_tensor(m[h][:, :, MUL:2 * MUL], r3[h][:, :, :], w4[:, :, 3, :], ALU.mult).then_inc(ev.mm, 1)
                for h in range(H):
                    v.wait_ge(ev.ll, now(i, h))
                    v.wait_ge(l_k[h], 16 * i + 16)
                    v.wait_ge(ev.tb, before(i, h))
                    if h:
                        v.wait_ge(ev.sc, now(i, 0))
                    v.tensor_tensor_scan(agg[h][:, :], keep[h][:, :], pT[h][:, :], agg[1 - h][:, HW - 1:HW], ALU.mult, ALU.add).then_inc(ev.sc, 1)
                for h in range(H):
                    tiles = bass.ds(i * H * J + h * J, J)
                    c.step(v.tensor_copy(vd[h][:, :], g.vec_dst[:, tiles]))
                    v.wait_ge(ev.tb, now(i, h))
                    v.wait_ge(l_x[h], 16 * i + 16)
                    v.wait_ge(w_x[h], 16 * i)
                    for j in range(J):
                        last = v.scalar_tensor_tensor(x3[h][:, j, :], pH[h][:, j * P:(j + 1) * P], vd[h][:, j:j + 1], x2[h][:, j, :], ALU.mult, ALU.add)
                    last.then_inc(ev.x3, 1)
                c.turn(i)

        @block.scalar
        def _(a):
            a.preload_act_table_set("natural_log_exp_and_others")
            credit(a, ev.rs, ev.hT, ev.ac, ev.si, ev.wc, ev.mc)
            with a.Fori(0, NI) as i:
                own = lambda k: i * 6 + k
                for h in range(H):
                    a.wait_ge(ev.at, now(i, h))
                    a.wait_ge(ev.hd, before(i, h))
                    a.activation(a8T[h][:, :], pW[h][0:NSC, :], ACT.Copy).then_inc(ev.ac, 1)
                for h in range(H):
                    a.wait_ge(ev.st, now(i, h))
                    rstd(a, g, s_a, own(1 + h), mv[h], rs[h], ev.rs)
                for h in range(H):
                    a.wait_ge(ev.hd, now(i, h))
                    a.wait_ge(ev.hi, before(i, h))
                    a.activation(sg[h][:, :], pH[h][0:HID, :], ACT.Exp, scale=-c_in).then_inc(s_a, 1)
                    a.wait_ge(s_a, own(3 + 2 * h))
                    a.activation(sg[h][:, :], sg[h][:, :], ACT.Ln, bias=1.0).then_inc(s_a, 1)
                    a.wait_ge(s_a, own(4 + 2 * h))
                    a.activation(sg[h][:, :], sg[h][:, :], ACT.Exp, scale=-1.0).then_inc(ev.si, 1)
                for h in range(H):
                    a.wait_ge(ev.ts, now(i, h))
                    a.wait_ge(ev.ff, before(i, h))
                    a.activation(hT[h][:, :], pT[h][:, :], ACT.Relu).then_inc(ev.hT, 1)
                for h in range(H):
                    a.wait_ge(ev.ww, now(i, h))
                    a.wait_ge(ev.mm, before(i, h))
                    a.activation(ws[h][:, :, :], four(pW[h][:, :]), ACT.Copy).then_inc(ev.wc, 1)
                for h in range(H):
                    a.wait_ge(ev.tm, now(i, h))
                    a.wait_ge(ev.ll, before(i, h))
                    a.activation(mT[h][:, 0, :], pF[h][:, :], ACT.Copy)
                    a.activation(mT[h][:, 1, :], pW[h][:, :], ACT.Copy).then_inc(ev.mc, 1)

        @block.tensor
        def _(pe):
            credit(pe, ev.ts, ev.ff, ev.at, ev.hd, ev.ww, ev.tm, ev.ll, ev.tb)
            with pe.Fori(0, NI) as i:
                for h in range(H):
                    pe.wait_ge(l_8[h], 16 * i + 16)
                    pe.wait_ge(ev.mc, before(i, h))
                    for j in range(J):
                        last = pe.transpose(pW[h][0:NSC, j * P:(j + 1) * P], a8[h][:, j, :], g.ident[:, :])
                    last.then_inc(ev.at, 1)
                for h in range(H):
                    pe.wait_ge(ev.ac, now(i, h))
                    pe.wait_ge(ev.x3, before(i, h))
                    pe.matmul(pH[h][0:HID, :], g.wfc1[:, :], a8T[h][:, :], start=True, stop=True).then_inc(ev.hd, 1)
                for h in range(H):
                    pe.wait_ge(ev.ys, now(i, h))
                    pe.wait_ge(ev.sc, before(i, h))
                    transpose4(pe, g, pT[h], y[h], ev.ts)
                for h in range(H):
                    pe.wait_ge(ev.hi, now(i, h))
                    for j in range(J):
                        last = pe.matmul(pW[h][:, j * P:(j + 1) * P], hid[h][:, j * P:(j + 1) * P], g.wfc2[:, :], start=True, stop=True)
                    last.then_inc(ev.ww, 1)
                for h in range(H):
                    pe.wait_ge(ev.hT, now(i, h))
                    for j in range(J):
                        last = pe.matmul(pF[h][:, j * P:(j + 1) * P], hT[h][:, j * P:(j + 1) * P], g.w1big[:, :], start=True, stop=True)
                    last.then_inc(ev.ff, 1)
                for h in range(H):
                    pe.wait_ge(ev.mm, now(i, h))
                    for k, bank_ in enumerate((pF, pW)):
                        for j in range(J):
                            last = pe.transpose(bank_[h][:, j * P:(j + 1) * P], m[h][:, j, k * P:(k + 1) * P], g.ident[:, :])
                    last.then_inc(ev.tm, 1)
                for h in range(H):
                    pe.wait_ge(ev.mc, now(i, h))
                    for k in range(2):
                        last = pe.matmul(pT[h][:, :], g.w2big[:, k, :], mT[h][:, k, :], start=(k == 0), stop=(k == 1))
                    last.then_inc(ev.ll, 1)
                for h in range(H):
                    pe.wait_ge(ev.sc, now(i, h))
                    transpose4(pe, g, pH[h], four(agg[h][:, :]), ev.tb)


def gat_rows(nc, g):
    ctx = ExitStack()
    names = "xx st rs nm hh sh rh ys ts nT at ae ba nd".split()
    ev = [events(g, f"q{s}_", names) for s in range(2)]
    s_v, s_a, s_p = (g.sem("q_" + n) for n in ("v", "a", "p"))
    l_s, w_a, w_n, w_b = ([[g.sem(f"q{s}_{n}{h}") for h in range(H)] for s in range(2)] for n in ("ls", "wa", "wn", "wb"))
    with ctx:
        sb, two, bank = halves(nc, ctx, "q_")
        side = lambda n, s, d=F32: [two(f"{n}{k}_", s, d) for k in range(2)]
        raw, hh, y = side("raw", [P, J, P]), side("hh", [P, J, P]), side("y", [P, J, P])
        x = two("x", [P, J, P])
        st, mv, sh, mh = side("st", [P, J, 6]), side("mv", [P, J, 2]), side("sh", [P, J, 6]), side("mh", [P, J, 2])
        rs, rh, nm = side("rs", [P, J]), side("rh", [P, J]), side("nm", [P, J])
        nohas = two("nohas", [P, J])
        ndT, base = two("ndT", [P, HW]), two("base", [P, J, P])
        att = [two("att0_", [NH, HW]), two("att1_", [2 * NH, HW])]
        at_s = two("at_s", [P, J], I32)
        pT = [bank("pS"), bank("pD")]
        pA = [bank("pA"), bank("pB")]
        xx = [x, raw[1]]
        block = ctx.enter_context(nc.Block())
        turns = [(s, h) for s in range(2) for h in range(H)]
        span = lambda i, h: bass.ds(i * SUP + h * HW, HW)

        @block.sync
        def _(sp):
            with sp.Fori(0, NI) as i:
                for h in range(H):
                    wait_alone(g, sp, ev[1].ba, before(i, h))
                    wait_alone(g, sp, ev[1].hh, before(i, h))
                    sp.dma_start(raw[1][h][:, :, :], edge_rows(g.tab_b, N, i, h)).then_inc(l_s[1][h], 16)
                for h in range(H):
                    wait_alone(g, sp, ev[1].ba, now(i, h))
                    sp.dma_start(edge_rows(g.base_s, 0, i, h), base[h][:, :, :]).then_inc(w_b[1][h], 16)
                for h in range(H):
                    wait_alone(g, sp, ev[1].nT, now(i, h))
                    sp.dma_start(g.ndt_s[:, span(i, h)], ndT[h][:, :]).then_inc(w_n[1][h], 16)
                for s, h in turns:
                    wait_alone(g, sp, ev[s].ae, now(i, h))
                    rows = g.att_s[0:NH, :] if s == 0 else g.att_s[NH:3 * NH, :]
                    sp.dma_start(rows[:, span(i, h)], att[s][h][:, :]).then_inc(w_a[s][h], 16)
            for h in range(H):
                for w in (w_b[1][h], w_n[1][h], w_a[0][h], w_a[1][h]):
                    sp.wait_ge(w, 16 * NI)

        @block.gpsimd
        def _(pool):
            with pool.Fori(0, NI) as i:
                for h in range(H):
                    wait_alone(g, pool, ev[0].xx, before(i, h))
                    pool.tensor_copy(at_s[h][:, :], g.row_x[:, bass.ds(i * H * J + h * J, J)]).then_inc(s_p, 1)
                    wait_alone(g, pool, s_p, i * 2 + h + 1)
                    gather(pool, g.tab_b, at_s[h], raw[0][h], l_s[0][h])

        @block.vector
        def _(v):
            for s in range(2):
                credit(v, ev[s].xx, ev[s].st, ev[s].nm, ev[s].sh, ev[s].ys, ev[s].ba)
            c = Chain(v, s_v, 10)
            with v.Fori(0, NI) as i:
                c.turn(i)
                for s, h in turns:
                    if s == 0:
                        tiles = bass.ds(i * H * J + h * J, J)
                        v.wait_ge(l_s[0][h], 64 * i + 64)
                        c.step(v.tensor_copy(nohas[h][:, :], g.nohas[:, tiles]))
                        v.wait_ge(ev[0].hh, before(i, h))
                        for j in range(J):
                            last = v.scalar_tensor_tensor(x[h][:, j, :], g.b1_rows[:, :], nohas[h][:, j:j + 1], raw[0][h][:, j, :], ALU.mult, ALU.add)
                        last.then_inc(ev[0].xx, 1)
                        v.wait_ge(ev[0].xx, now(i, h))
                    else:
                        v.wait_ge(l_s[1][h], 16 * i + 16)
                    stats(v, c, g, xx[s][h], st[s][h], mv[s][h], ev[s].st)
                for s, h in turns:
                    v.wait_ge(ev[s].rs, now(i, h))
                    v.scalar_tensor_tensor(nm[s][h][:, :], mv[s][h][:, :, 0], -1.0, rs[s][h][:, :], ALU.mult, ALU.mult).then_inc(ev[s].nm, 1)
                for s, h in turns:
                    v.wait_ge(ev[s].hh, now(i, h))
                    stats(v, c, g, hh[s][h], sh[s][h], mh[s][h], ev[s].sh)
                for h in range(H):
                    v.wait_ge(w_b[1][h], 16 * i)
                    v.tensor_tensor(base[h][:, :, :], raw[1][h][:, :, :], hh[1][h][:, :, :], ALU.add).then_inc(ev[1].ba, 1)
                for s, h in turns:
                    v.wait_ge(ev[s].rh, now(i, h))
                    v.wait_ge(ev[s].ts, before(i, h))
                    normalise(v, hh[s][h], mh[s][h], rh[s][h], y[s][h], ev[s].ys)
                c.turn(i)

        @block.scalar
        def _(a):
            a.preload_act_table_set("natural_log_exp_and_others")
            for s in range(2):
                credit(a, ev[s].rs, ev[s].hh, ev[s].rh, ev[s].nT, ev[s].ae)
            with a.Fori(0, NI) as i:
                own = lambda k: i * 8 + k
                for s, h in turns:
                    a.wait_ge(ev[s].st, now(i, h))
                    rstd(a, g, s_a, own(1 + s * H + h), mv[s][h], rs[s][h], ev[s].rs)
                for s, h in turns:
                    a.wait_ge(ev[s].nm, now(i, h))
                    a.wait_ge(ev[s].ys, before(i, h))
                    if s:
                        a.wait_ge(ev[1].ba, before(i, h))
                    for j in range(J):
                        last = a.activation(hh[s][h][:, j, :], xx[s][h][:, j, :], ACT.Relu, scale=rs[s][h][:, j:j + 1], bias=nm[s][h][:, j:j + 1])
                    last.then_inc(ev[s].hh, 1)
                for s, h in turns:
                    a.wait_ge(ev[s].sh, now(i, h))
                    rstd(a, g, s_a, own(5 + s * H + h), mh[s][h], rh[s][h], ev[s].rh)
                for s, h in turns:
                    wait_alone(g, a, ev[s].ts, now(i, h))
                    if s:
                        a.wait_ge(w_n[1][h], 16 * i)
                        a.wait_ge(ev[1].at, before(i, h))
                    dest = ndT[h][:, :] if s else g.state.msg[:, span(i, h)]
                    a.activation(dest, pT[s][h][:, :], ACT.Identity, scale=g.ln_g[:, :], bias=g.ln_b[:, :]).then_inc(ev[s].nT, 1)
                for s, h in turns:
                    a.wait_ge(ev[s].at, now(i, h))
                    a.wait_ge(w_a[s][h], 16 * i)
                    a.activation(att[s][h][:, :], pA[s][h][0:(s + 1) * NH, :], ACT.Copy).then_inc(ev[s].ae, 1)

        @block.tensor
        def _(pe):
            for s in range(2):
                credit(pe, ev[s].ts, ev[s].at)
            with pe.Fori(0, NI) as i:
                for s, h in turns:
                    pe.wait_ge(ev[s].ys, now(i, h))
                    pe.wait_ge(ev[s].nT, before(i, h))
                    transpose4(pe, g, pT[s][h], y[s][h], ev[s].ts)
                for s, h in turns:
                    wait_alone(g, pe, ev[s].nT, now(i, h))
                    wait_alone(g, pe, ev[s].ae, before(i, h))
                    rhs = ndT[h][:, :] if s else g.state.msg[:, span(i, h)]
                    M = (s + 1) * NH
                    pe.matmul(pA[s][h][0:M, :], g.wa[:, 0:M], rhs, start=True, stop=True).then_inc(ev[s].at, 1)


def head_softmax(nc, g):
    ctx = ExitStack()
    s_in, s_v, s_l, s_p, s_out = (g.sem("h_" + n) for n in ("in", "v", "l", "p", "out"))
    with ctx:
        sb = lambda n, s: ctx.enter_context(nc.sbuf_tensor("h_" + n, s, F32))
        a_, b_, c_ = sb("a", [P, 3 * NH, W]), sb("b", [P, 2 * NH, W]), sb("c", [P, NH, W])
        part = lambda t, n: t[:, n * NH:(n + 1) * NH, :]
        of = lambda t, n: (lambda k: t[:, n * NH + k, :])
        seg = Segments(nc, ctx, g, "h_", 2 * NH)
        block = ctx.enter_context(nc.Block())
        logit, own = part(a_, 0), part(b_, 0)

        @block.sync
        def _(sp):
            for k in range(3 * NH):
                sp.dma_start(a_[:, k, :], wide(g.att_s[k, :])).then_inc(s_in, 16)
            sp.wait_ge(s_out, 1)
            for k in range(NH):
                sp.dma_start(wide(g.alpha3_s[k, :]), a_[:, 2 * NH + k, :]).then_inc(s_p, 16)
                sp.dma_start(wide(g.alpha3_s[NH + k, :]), a_[:, k, :]).then_inc(s_p, 16)
            sp.wait_ge(s_p, 2 * NH * 16)

        @block.vector
        def _(v):
            c = Chain(v, s_v)
            seg.prepare(v, c)
            v.wait_ge(s_in, 16 * 3 * NH)
            c.step(v.tensor_tensor(a_[:, NH:, :], a_[:, NH:, :], each(g.last_w, 2 * NH), ALU.mult))
            seg.scan(v, c, "back", 2 * NH, of(b_, 0), of(a_, 1))
            v.tensor_tensor(logit, logit, part(b_, 1), ALU.add)
            c.step(v.tensor_tensor(own, own, part(b_, 1), ALU.add))
            v.scalar_tensor_tensor(logit, logit, 0.2, logit, ALU.mult, ALU.max)
            c.step(v.scalar_tensor_tensor(own, own, 0.2, own, ALU.mult, ALU.max))
            seg.scan(v, c, "max", NH, of(a_, 1), of(a_, 0))
            c.step(v.tensor_tensor(part(a_, 2), part(a_, 1), each(g.last_w, NH), ALU.mult))
            seg.scan(v, c, "back", NH, of(c_, 0), of(a_, 2))
            c.step(v.tensor_tensor(part(a_, 1), c_[:, :, :], own, ALU.max))
            v.tensor_tensor(logit, logit, part(a_, 1), ALU.subtract)
            v.tensor_tensor(own, own, part(a_, 1), ALU.subtract).then_inc(s_l, 1)
            v.wait_ge(s_l, 3)
            seg.scan(v, c, "sum", NH, of(a_, 1), of(a_, 0))
            c.step(v.tensor_tensor(part(a_, 2), part(a_, 1), each(g.last_w, NH), ALU.mult))
            seg.scan(v, c, "back", NH, of(c_, 0), of(a_, 2))
            c.step(v.tensor_tensor(c_[:, :, :], c_[:, :, :], own, ALU.add))
            c.step(v.tensor_scalar(c_[:, :, :], c_[:, :, :], EPS_SM, None, ALU.add))
            c.step(v.reciprocal(part(a_, 1), c_[:, :, :]))
            c.step(v.tensor_tensor(part(a_, 2), logit, part(a_, 1), ALU.mult))
            v.tensor_tensor(part(a_, 0), own, part(a_, 1), ALU.mult).then_inc(s_out, 1)

        @block.scalar
        def _(a):
            a.preload_act_table_set("natural_log_exp_and_others")
            a.wait_ge(s_l, 1)
            a.activation(logit, logit, ACT.Exp).then_inc(s_l, 1)
            a.activation(own, own, ACT.Exp).then_inc(s_l, 1)

        @block.tensor
        def _(pe):
            seg.turns(pe, (2 * NH, NH, NH, NH, NH))


def gat_out(nc, g):
    ctx = ExitStack()
    names = "os xs cs wt sc od xd cd wd eo u ou ot".split()
    ev = events(g, "o_", names)
    s_v, s_p, s_0 = (g.sem("o_" + n) for n in ("v", "p", "zero"))
    l_a, l_k, l_n, l_b, w_o = ([g.sem(f"o_{n}{h}") for h in range(H)] for n in ("la", "lk", "ln", "lb", "wo"))
    with ctx:
        sb, two, _ = halves(nc, ctx, "o_")
        al, own = two("al", [NH, HW]), two("own", [NH, HW])
        keep, ndT = two("keep", [P, HW]), two("ndT", [P, HW])
        ax, wt, agg = (two(n, [P, 2, HW]) for n in ("ax", "wt", "agg"))
        base, ot = two("base", [P, J, P]), two("ot", [P, J, P])
        at_o = two("at_o", [P, J], I32)
        pO = [ctx.enter_context(nc.psum_tensor(f"o_pO{h}", [P, 2, HW], F32)) for h in range(H)]
        pX = [ctx.enter_context(nc.psum_tensor(f"o_pX{h}", [P, 2, HW], F32)) for h in range(H)]
        block = ctx.enter_context(nc.Block())
        span = lambda i, h: bass.ds(i * SUP + h * HW, HW)

        @block.sync
        def _(sp):
            with sp.Fori(0, NI) as i:
                for h in range(H):
                    wait_alone(g, sp, ev.xd, before(i, h))
                    sp.dma_start(al[h][:, :], g.alpha3_s[0:NH, :][:, span(i, h)]).then_inc(l_a[h], 16)
                    sp.dma_start(own[h][:, :], g.alpha3_s[NH:2 * NH, :][:, span(i, h)]).then_inc(l_a[h], 16)
                    sp.dma_start(ndT[h][:, :], g.ndt_s[:, span(i, h)]).then_inc(l_n[h], 16)
                    wait_alone(g, sp, ev.ot, before(i, h))
                    sp.dma_start(keep[h][:, :], row_part(g.keep_s, i, h)).then_inc(l_k[h], 16)
                    sp.dma_start(base[h][:, :, :], edge_rows(g.base_s, 0, i, h)).then_inc(l_b[h], 16)

        @block.gpsimd
        def _(pool):
            with pool.Fori(0, NI) as i:
                for h in range(H):
                    pool.tensor_copy(at_o[h][:, :], g.put[:, bass.ds(i * H * J + h * J, J)]).then_inc(s_p, 1)
                    wait_alone(g, pool, s_p, i * 2 + h + 1)
                    wait_alone(g, pool, ev.ot, now(i, h))
                    for j in range(J):
                        pool.indirect_dma_start(g.out, bass.IndirectOffsetOnAxis(ap=at_o[h][:, j:j + 1], axis=0), ot[h][:, j, :], None,
                                                bounds_check=N - 1, oob_is_err=False).then_inc(w_o[h], 16)
                for h in range(H):
                    wait_alone(g, pool, w_o[h], 64 * i + 64)

        @block.vector
        def _(v):
            credit(v, ev.wt, ev.sc, ev.wd, ev.u, ev.ot)
            v.memset(agg[H - 1][:, :, HW - 1:HW], 0.0).then_inc(s_0, 1)
            v.wait_ge(s_0, 1)
            c = Chain(v, s_v, 2)
            with v.Fori(0, NI) as i:
                c.turn(i)
                for h in range(H):
                    v.wait_ge(ev.cs, now(i, h))
                    v.tensor_tensor(wt[h][:, :, :], pO[h][:, :, :], ax[h][:, :, :], ALU.mult).then_inc(ev.wt, 1)
                for h in range(H):
                    v.wait_ge(ev.wt, now(i, h))
                    v.wait_ge(l_k[h], 16 * i + 16)
                    if h:
                        v.wait_ge(ev.sc, now(i, 0))
                    for k in range(2):
                        last = v.tensor_tensor_scan(agg[h][:, k, :], keep[h][:, :], wt[h][:, k, :], agg[1 - h][:, k, HW - 1:HW], ALU.mult, ALU.add)
                    last.then_inc(ev.sc, 1)
                for h in range(H):
                    v.wait_ge(ev.cd, now(i, h))
                    v.wait_ge(ev.sc, now(i, h))
                    c.step(v.tensor_tensor(wt[h][:, :, :], pO[h][:, :, :], ax[h][:, :, :], ALU.mult))
                    v.tensor_tensor(wt[h][:, :, :], wt[h][:, :, :], agg[h][:, :, :], ALU.add).then_inc(ev.wd, 1)
                for h in range(H):
                    v.wait_ge(ev.eo, now(i, h))
                    v.scalar_tensor_tensor(wt[h][:, :, :], ax[h][:, :, :], 1.0, wt[h][:, :, :], ALU.min, ALU.add).then_inc(ev.u, 1)
                for h in range(H):
                    v.wait_ge(ev.ou, now(i, h))
                    v.wait_ge(l_b[h], 16 * i + 16)
                    v.wait_ge(w_o[h], 64 * i)
                    v.tensor_tensor(ot[h][:, :, :], four(pO[h][:, 0, :]), base[h][:, :, :], ALU.add).then_inc(ev.ot, 1)
                c.turn(i)

        @block.scalar
        def _(a):
            a.preload_act_table_set("natural_log_exp_and_others")
            credit(a, ev.cs, ev.cd, ev.eo)
            with a.Fori(0, NI) as i:
                for h in range(H):
                    a.wait_ge(ev.xs, now(i, h))
                    a.wait_ge(ev.u, before(i, h))
                    a.activation(ax[h][:, :, :], pX[h][:, :, :], ACT.Copy).then_inc(ev.cs, 1)
                for h in range(H):
                    a.wait_ge(ev.xd, now(i, h))
                    a.wait_ge(ev.wt, now(i, h))
                    a.activation(ax[h][:, :, :], pX[h][:, :, :], ACT.Copy).then_inc(ev.cd, 1)
                for h in range(H):
                    a.wait_ge(ev.wd, now(i, h))
                    for k in range(2):
                        a.activation(ax[h][:, k, :], wt[h][:, k, :], ACT.Exp, bias=g.b12[:, k:k + 1])
                    for k in range(2):
                        last = a.activation(wt[h][:, k, :], wt[h][:, k, :], ACT.Relu, bias=g.b12[:, k:k + 1])
                    last.then_inc(ev.eo, 1)

        @block.tensor
        def _(pe):
            credit(pe, ev.xs, ev.xd, ev.ou)
            with pe.Fori(0, NI) as i:
                for h in range(H):
                    wait_alone(g, pe, ev.ot, before(i, h))
                    for k in range(2):
                        pe.matmul(pO[h][:, k, :], g.w12[:, k * P:(k + 1) * P], g.state.msg[:, span(i, h)], start=True, stop=True)
                    pe.wait_ge(l_a[h], 32 * i + 32)
                    pe.wait_ge(ev.cd, before(i, h))
                    for k in range(2):
                        last = pe.matmul(pX[h][:, k, :], g.ex[:, k, :], al[h][:, :], start=True, stop=True)
                    last.then_inc(ev.xs, 1)
                for h in range(H):
                    pe.wait_ge(ev.wt, now(i, h))
                    pe.wait_ge(l_n[h], 16 * i + 16)
                    for k in range(2):
                        pe.matmul(pO[h][:, k, :], g.w12[:, k * P:(k + 1) * P], ndT[h][:, :], start=True, stop=True)
                    pe.wait_ge(ev.cs, now(i, h))
                    for k in range(2):
                        last = pe.matmul(pX[h][:, k, :], g.ex[:, k, :], own[h][:, :], start=True, stop=True)
                    last.then_inc(ev.xd, 1)
                for h in range(H):
                    pe.wait_ge(ev.u, now(i, h))
                    pe.wait_ge(ev.wd, now(i, h))
                    for j in range(J):
                        o = pO[h][:, 0, j * P:(j + 1) * P]
                        pe.matmul(o, wt[h][:, 0, j * P:(j + 1) * P], g.wu[:, 0, :], start=True, stop=False)
                        pe.matmul(o, wt[h][:, 1, j * P:(j + 1) * P], g.wu[:, 1, :], start=False, stop=False)
                        last = pe.matmul(o, g.ones_row[:, :], g.bu_row[:, :], start=False, stop=True)
                    last.then_inc(ev.ou, 1)


def shared(nc, ctx, inputs):
    state = State()

    def sem(name):
        state.sems.append(nc.alloc_semaphore(name=name))
        return state.sems[-1]

    sb = lambda n, s, d=F32: ctx.enter_context(nc.sbuf_tensor(n, s, d))
    have = dict(inputs, state=state, sem=sem)
    for name, shape in dict(
            ident=[P, P], eps_ln=[P, 1], ones_row=[1, P], ones_col=[P, 1], log2_col=[P, 1], edge_no=[P, T],
            w0=[P, P], w12=[P, 2 * P], wu=[P, 2, P], wr=[P, NREL_LAYERS * R_, P], wfc1=[NSC, HID], wfc2=[HID, P],
            b1_rows=[P, P], b0_row=[1, P], att_q=[P, 2], att_k=[P, 2], b1_col=[P, 2], ln_g=[P, 1], ln_b=[P, 1],
            b12=[P, 2], w1big=[P, P], w2big=[P, 2, P], wq=[P, NREL_LAYERS * R_], wa=[P, 2 * NH], bu_row=[1, P], ex=[NH, 2, P],
            keep_w=[P, W], more_w=[P, W], last_w=[P, W], keepneg_w=[P, W], typ_w=[P, W],
            src_f=[P, T], typ_t=[P, T], norm_src=[P, T], norm_dst=[P, T], vec_src=[P, T], vec_dst=[P, T], nohas=[P, T]).items():
        have[name] = sb(name, shape)
    for name in ("src_c", "dst_c", "put", "row_x", "row_h"):
        have[name] = sb(name, [P, T], I32)
    have["iota_lo"] = sb("iota_lo", [P, HL], F16)
    for name, shape, dt in (
            ("dst_s", [EP + 2], I32), ("vec_s", [5, EP], F32), ("keep_s", [EP], F32), ("lastno_s", [NPAD, 1], F32),
            ("deg_s", [NPAD], F32), ("info_s", [N, 4], F32), ("w1big_s", [P, P], F32), ("w2big_s", [2 * P, P], F32),
            ("tab_a", [TABROWS, D], F32), ("tab_b", [TABROWS, D], F32), ("h_tab", [HROWS, D], F32),
            ("pq_s", [R_, EP], F32), ("kq_s", [EP], F32), ("alpha_s", [EP], F32),
            ("att_s", [3 * NH, EP], F32), ("alpha3_s", [2 * NH, EP], F32), ("ndt_s", [P, EP], F32),
            ("base_s", [EP, D], F32), ("attr8_s", [EP, NSC], F32), ("attr4_s", [EP, 4], F32)):
        have[name] = nc.dram_tensor(name, shape, dt, kind="Internal").ap()
    return namedtuple("Shared", list(have))(**have)


def run(nc, g, stage, *args):
    outer, g.state.sems = g.state.sems, []
    g.state.runs += 1
    g.state.waits = g.sem(f"waits{g.state.runs}")
    stage(nc, g, *args)
    nc.clear_and_free_semaphores(g.state.sems)
    nc.all_engine_barrier()
    g.state.sems = outer


def gnn(nc, inputs, out):
    ctx = ExitStack()
    with ctx:
        g = shared(nc, ctx, dict(inputs, out=out))
        for stage in STAGES:
            run(nc, g, stage)


def rgat(nc, g):
    with nc.sbuf_tensor("msg", [P, EP], F32) as msg:
        g.state.msg = msg
        for layer in range(NREL_LAYERS):
            run(nc, g, relations, layer)
            run(nc, g, edge_softmax, layer)
            run(nc, g, aggregate, layer)


def gat(nc, g):
    with nc.sbuf_tensor("source_rows", [P, EP], F32) as msg:
        g.state.msg = msg
        run(nc, g, gat_rows)
        run(nc, g, head_softmax)
        run(nc, g, gat_out)


STAGES = [dense_identity, edges_in, degrees, node_info, weights, node_dense, layer0_edges, rgat, interaction, gat]

_INS = ["x", "src", "dst", "edge_attr_4", "edge_attr_8", "edge_type_8", "node_vec1", "node_vec1_n2", "L0_gnn_W",
        "L1_gnn_W", "L1_gnn_att_q", "L1_gnn_att_k", "L1_gnn_bias", "L2_gnn_w1_s", "L2_gnn_w1_v", "L2_gnn_Wfc1",
        "L2_gnn_Wfc2", "L2_gnn_w2_s", "L2_gnn_w2_v", "L3_gnn_ln_g", "L3_gnn_ln_b", "L3_gnn_W1", "L3_gnn_a1s",
        "L3_gnn_a1d", "L3_gnn_b1", "L3_gnn_W2", "L3_gnn_a2s", "L3_gnn_a2d", "L3_gnn_b2", "L3_gnn_Wu", "L3_gnn_bu"]
_NAMES = {"edge_attr_4": "attr4", "edge_attr_8": "attr8", "edge_type_8": "typ", "node_vec1": "vec1", "node_vec1_n2": "vec2"}


def short(name):
    return _NAMES.get(name, name.replace("_gnn_", "_"))


def kernel(**inputs):
    import numpy as _np
    import concourse.bacc as _bacc
    from concourse import mybir as _mybir
    from concourse.bass_utils import run_bass_kernel_spmd as _run

    nc = _bacc.Bacc("TRN2", target_bir_lowering=False, num_devices=1)
    arrays, aps = {}, {}
    for name in _INS:
        a = _np.ascontiguousarray(inputs[name])
        arrays[f"in_{name}"] = a
        aps[short(name)] = nc.dram_tensor(f"in_{name}", a.shape, _mybir.dt.from_np(a.dtype), kind="ExternalInput").ap()
    out = nc.dram_tensor("out_0", (N, D), _mybir.dt.float32, kind="ExternalOutput").ap()
    gnn(nc, aps, out)
    r = _run(nc, [arrays], core_ids=[0])
    return r.results[0]["out_0"]
```

```python
from collections import namedtuple
from contextlib import ExitStack

import numpy as np
import concourse.bass as bass
from concourse import mybir

F32 = mybir.dt.float32
F16 = mybir.dt.float16
I32 = mybir.dt.int32
ALU = mybir.AluOpType
ACT = mybir.ActivationFunctionType
AX = mybir.AxisListType

N, D = 50000, 128
E = 25000
P = 128
J = 4
HW = J * P
EP = -(-E // 1024) * 1024
T = EP // P
W = EP // P
EROWS = E // W
HL = 512
NPAD = -(-N // HL) * HL
HR = NPAD // HL
NV = 400
NVR = N // NV
R_ = 8
NREL_LAYERS = 2
MUL, NSC, HID = 32, 8, 64
H1, O1, H2, O2 = 4, 32, 8, 16
NH = H1 + H2
EPS_LN = 1e-5
EPS_SM = 1e-16
BIG = 1e30
NOWHERE = 1 << 20

TABROWS = N + EP
HROWS = EP + 1


class Chain:

    def __init__(self, eng, sem, per=0, g=None):
        self.eng, self.sem, self.per, self.n, self.i, self.g = eng, sem, per, 0, None, g

    def turn(self, i):
        if self.n:
            assert self.n == self.per, (self.n, self.per)
        self.n, self.i = 0, i

    def step(self, instruction):
        instruction.then_inc(self.sem, 1)
        self.n += 1
        value = self.n if self.i is None else self.i * self.per + self.n
        self.eng.wait_ge(self.sem, value)
        if self.g:
            self.eng.sem_inc(self.g.state.waits, 1)


def wait_alone(g, eng, sem, value):
    eng.wait_ge(sem, value)
    eng.sem_inc(g.state.waits, 1)


def events(g, prefix, names):
    return namedtuple("Events", names)(*[g.sem(prefix + n) for n in names])


class State:

    def __init__(self):
        self.sems, self.runs, self.waits, self.msg = [], 0, None, None


def edges_copy(nc, g):
    ctx = ExitStack()
    s_pad, s_in, s_copy, s_v, s_flag, s_pe = (g.sem("ec_" + n) for n in ("pad", "in", "copy", "v", "flag", "pe"))
    with ctx:
        sb = lambda n, s, d=F32: ctx.enter_context(nc.sbuf_tensor(n, s, d))
        one = sb("ec_one", [P, 3, W], I32)
        zero = sb("ec_zero", [P, W * NSC])
        ends = sb("ec_ends", [1, 2], I32)
        near = sb("ec_near", [P, 2, W], I32)
        nearf = sb("ec_nearf", [P, 2, W])
        below = sb("ec_below", [P, W])
        any_ = sb("ec_any", [P, 1])
        ps = ctx.enter_context(nc.psum_tensor("ec_ps", [P, HL], F32))
        block = ctx.enter_context(nc.Block())

        @block.sync
        def _(sp):
            sp.dma_start(g.dst_s[1:1 + E, :].rearrange("(p w) k -> p (w k)", w=W), g.dst.rearrange("(p w) -> p w", w=W)).then_inc(s_in, 16)
            sp.wait_ge(s_pad, 1)
            sp.dma_start(g.dst_s[1 + E:1 + EP, :].rearrange("(p w) k -> p (w k)", w=W), one[0:P - EROWS, 1, :]).then_inc(s_in, 16)
            sp.dma_start(g.dst_s[0:1, :], ends[0:1, 0:1]).then_inc(s_in, 16)
            sp.dma_start(g.dst_s[EP + 1:EP + 2, :], ends[0:1, 1:2]).then_inc(s_in, 16)
            sp.wait_ge(s_in, 64)
            for k in range(2):
                sp.dma_start(near[:, k, :], g.dst_s[k:k + EP, 0].rearrange("(p w) -> p w", w=W)).then_inc(s_in, 16)
            for rows, a, pad, k in ((g.attr8_s, g.attr8, zero, NSC), (g.attr4_s, g.attr4, zero, 4)):
                sp.dma_start(rows[0:E, :].rearrange("(p w) k -> p (w k)", w=W), a.rearrange("(p w) k -> p (w k)", w=W)).then_inc(s_copy, 16)
                sp.dma_start(rows[E:EP, :].rearrange("(p w) k -> p (w k)", w=W), pad[0:P - EROWS, 0:W * k]).then_inc(s_copy, 16)
            for rows, a, k in ((g.src_s, g.src, 0), (g.typ_s, g.typ, 2)):
                sp.dma_start(rows[0:E, :].rearrange("(p w) k -> p (w k)", w=W), a.rearrange("(p w) -> p w", w=W)).then_inc(s_copy, 16)
                sp.dma_start(rows[E:EP, :].rearrange("(p w) k -> p (w k)", w=W), one[0:P - EROWS, k, :]).then_inc(s_copy, 16)
            sp.wait_ge(s_copy, 16 * 8)

        @block.vector
        def _(v):
            v.memset(one[:, 0, :], float(127 * HL))
            v.memset(one[:, 1, :], float(N))
            v.memset(one[:, 2, :], 0.0)
            v.memset(zero[:, :], 0.0)
            v.memset(ends[0:1, 0:1], -1.0)
            v.memset(ends[0:1, 1:2], float(N + 1)).then_inc(s_pad, 1)
            c = Chain(v, s_v)
            v.wait_ge(s_in, 96)
            c.step(v.tensor_copy(nearf[:, :, :], near[:, :, :]))
            c.step(v.tensor_tensor(below[:, :], nearf[:, 1, :], nearf[:, 0, :], ALU.is_lt))
            v.tensor_reduce(any_[:, :], below[:, :], AX.X, ALU.max).then_inc(s_flag, 1)
            v.wait_ge(s_pe, 1)
            c.step(v.tensor_copy(g.unsorted[:, :], ps[0:1, 0:1]))

        @block.tensor
        def _(pe):
            pe.wait_ge(s_flag, 1)
            pe.matmul(ps[0:1, 0:1], any_[:, :], g.ones_col[:, :], start=True, stop=True).then_inc(s_pe, 1)


def if_unsorted(g, eng):
    return eng.If(eng.value_load(g.unsorted[0:1, 0:1], min_val=0, max_val=P) > 0)


def edges_sorted(nc, g):
    ctx = ExitStack()
    CUT = 5
    EC = E // CUT
    FULL, LEFT = E // P, E % P
    s_row, s_taken, s_tri, s_col, s_v, s_place, s_read, s_put = (
        g.sem("ep_" + n) for n in ("row", "taken", "tri", "col", "v", "place", "read", "put"))
    with ctx:
        sb = lambda n, s, d=F32: ctx.enter_context(nc.sbuf_tensor(n, s, d))
        row = sb("ep_row", [P, E])
        part = sb("ep_part", [P, EC], I32)
        less = sb("ep_less", [P, EC])
        tri = sb("ep_tri", [P, 2, P])
        lists = sb("ep_lists", [P, 3], I32)
        a4, a8 = sb("ep_a4", [P, 4]), sb("ep_a8", [P, NSC])
        own = sb("ep_own", [P, 1])
        counts = sb("ep_counts", [P, CUT])
        total = sb("ep_total", [P, 1])
        place = sb("ep_place", [P, 2], I32)
        block = ctx.enter_context(nc.Block())
        outs = ((g.src_s, lists[:, 0:1]), (g.dst_s, lists[:, 1:2]), (g.typ_s, lists[:, 2:3]), (g.attr4_s, a4), (g.attr8_s, a8))

        def tiles(eng, body):
            with eng.Fori(0, FULL) as i:
                body(i, i * P, P)
            body(FULL, FULL * P, LEFT)

        @block.sync
        def _(sp):
            with if_unsorted(g, sp):
                for k in range(CUT):
                    if k:
                        sp.wait_ge(s_taken, k)
                    sp.dma_start(part[:, :], g.dst[k * EC:(k + 1) * EC].partition_broadcast(P)).then_inc(s_row, 16)

                sp.sem_inc(s_read, 1)

                def body(i, base, n):
                    wait_alone(g, sp, s_read, i + 1)
                    for k, a in enumerate((g.src, g.dst, g.typ)):
                        sp.dma_start(lists[0:n, k:k + 1], a[bass.ds(base, n)].unsqueeze(1)).then_inc(s_col, 16)
                    sp.dma_start(a4[0:n, :], g.attr4[bass.ds(base, n), :]).then_inc(s_col, 16)
                    sp.dma_start(a8[0:n, :], g.attr8[bass.ds(base, n), :]).then_inc(s_col, 16)
                tiles(sp, body)

        @block.gpsimd
        def _(pool):
            with if_unsorted(g, pool):
                pool.memset(tri[:, :, :], 0.5).then_inc(s_tri, 1)
                pool.wait_ge(s_tri, 1)
                pool.affine_select(out=tri[:, 0, :], in_=tri[:, 0, :], compare_op=ALU.is_gt, fill=0.0, base=0,
                                   pattern=[[-1, P]], channel_multiplier=1).then_inc(s_tri, 1)
                pool.affine_select(out=tri[:, 1, :], in_=tri[:, 1, :], compare_op=ALU.is_ge, fill=0.0, base=0,
                                   pattern=[[1, P]], channel_multiplier=-1).then_inc(s_tri, 1)

                def body(i, base, n):
                    wait_alone(g, pool, s_place, i + 1)
                    wait_alone(g, pool, s_col, i * 80 + 80)
                    for dest, rows in outs:
                        k = 1 if dest is g.dst_s else 0
                        pool.indirect_dma_start(dest, bass.IndirectOffsetOnAxis(ap=place[0:n, k:k + 1], axis=0), rows[0:n, :], None).then_inc(s_put, 16)
                    wait_alone(g, pool, s_put, i * 80 + 80)
                    pool.sem_inc(s_read, 1)
                tiles(pool, body)

        @block.vector
        def _(v):
            with if_unsorted(g, v):
                for k in range(CUT):
                    v.wait_ge(s_row, 16 * k + 16)
                    v.tensor_copy(row[:, k * EC:(k + 1) * EC], part[:, :]).then_inc(s_taken, 1)
                v.wait_ge(s_taken, CUT)
                v.wait_ge(s_tri, 3)
                c = Chain(v, s_v, 4 + 2 * CUT)

                def body(i, base, n):
                    c.turn(i)
                    block_ = row[0:n, bass.ds(base, n)]
                    wait_alone(g, v, s_col, i * 80 + 80)
                    c.step(v.tensor_copy(own[0:n, :], lists[0:n, 1:2]))
                    c.step(v.tensor_tensor(block_, block_, tri[0:n, 0, 0:n], ALU.subtract))
                    for k in range(CUT):
                        c.step(v.tensor_tensor(less[0:n, :], row[0:n, k * EC:(k + 1) * EC], own[0:n, 0:1].broadcast_to([n, EC]), ALU.is_lt))
                        c.step(v.tensor_reduce(counts[0:n, k:k + 1], less[0:n, :], AX.X, ALU.add))
                    c.step(v.tensor_tensor(block_, block_, tri[0:n, 1, 0:n], ALU.subtract))
                    c.step(v.tensor_reduce(total[0:n, :], counts[0:n, :], AX.X, ALU.add))
                    v.tensor_copy(place[0:n, 0:1], total[0:n, :])
                    v.tensor_scalar(place[0:n, 1:2], total[0:n, :], 1.0, None, ALU.add).then_inc(s_place, 1)
                tiles(v, body)


def dense_identity(nc, g):
    ctx = ExitStack()
    s_i = g.sem("s_ident")
    with ctx:
        iota_i = ctx.enter_context(nc.sbuf_tensor("iota_i", [P, HL], I32))
        iota_e = ctx.enter_context(nc.sbuf_tensor("iota_e", [P, T], I32))
        block = ctx.enter_context(nc.Block())

        @block.gpsimd
        def _(pool):
            pool.memset(g.ident[:, :], 0.0).then_inc(s_i, 1)
            pool.wait_ge(s_i, 1)
            pool.affine_select(out=g.ident[:, :], in_=g.ident[:, :], compare_op=ALU.not_equal, fill=1.0,
                               base=0, pattern=[[-1, P]], channel_multiplier=1).then_inc(s_i, 1)
            pool.iota(iota_i[:, :], pattern=[[1, HL]], base=0, channel_multiplier=0).then_inc(s_i, 1)
            pool.memset(g.ex[:, :, :], 1.0).then_inc(s_i, 1)
            n = 4
            for k, (first, width) in enumerate(((0, O1), (H1, O2))):
                for sign, base in ((1, width * first), (-1, width - 1 - width * first)):
                    pool.wait_ge(s_i, n)
                    pool.affine_select(out=g.ex[:, k, :], in_=g.ex[:, k, :], compare_op=ALU.is_ge, fill=0.0, base=base,
                                       pattern=[[sign, P]], channel_multiplier=-sign * width).then_inc(s_i, 1)
                    n += 1
            pool.iota(iota_e[:, :], pattern=[[P, T]], base=1, channel_multiplier=1).then_inc(s_i, 1)

        @block.vector
        def _(v):
            v.memset(g.eps_ln[:, :], EPS_LN)
            v.memset(g.ones_row[:, :], 1.0)
            v.memset(g.ones_col[:, :], 1.0)
            v.memset(g.log2_col[:, :], float(np.log(2.0)))
            v.wait_ge(s_i, 9)
            v.tensor_copy(g.iota_lo[:, :], iota_i[:, :])
            v.tensor_copy(g.edge_no[:, :], iota_e[:, :])


def edges_in(nc, g):
    ctx = ExitStack()
    s_load, s_vec, s_back, s_v, s_wide, s_pe = (g.sem("ei_" + n) for n in ("load", "vec", "back", "v", "wide", "pe"))
    K = 4
    SRC_H, SRC_C, DST_C, PUT = range(K)
    TYP = K
    TH = T // 2
    with ctx:
        sb = lambda n, s, d=F32: ctx.enter_context(nc.sbuf_tensor(n, s, d))
        raw = sb("ei_raw", [P, 2, W], I32)
        near = sb("ei_near", [P, 3, W], I32)
        nearf = sb("ei_nearf", [P, 3, W])
        vec = sb("ei_vec_t", [P, K + 1, W])
        real = sb("ei_real", [P, W])
        tmp = sb("ei_tmp", [P, W])
        back = sb("ei_back_t", [TH, 2, K, P])
        ps = ctx.enter_context(nc.psum_tensor("ei_ps", [P, 2, HL], F32))
        block = ctx.enter_context(nc.Block())

        @block.sync
        def _(sp):
            for k in range(3):
                sp.dma_start(near[:, k, :], g.dst_s[k:k + EP, 0].rearrange("(p w) -> p w", w=W)).then_inc(s_load, 16)
            for k, a in enumerate((g.src_s, g.typ_s)):
                sp.dma_start(raw[:, k, :], a[:, 0].rearrange("(p w) -> p w", w=W)).then_inc(s_load, 16)
            sp.wait_ge(s_wide, 1)
            for k in range(K + 1):
                sp.dma_start(g.vec_s[k, :].rearrange("(p w) -> p w", w=W), vec[:, k, :]).then_inc(s_vec, 16)
            sp.dma_start(g.keep_s.rearrange("(p w) -> p w", w=W), g.keep_w[:, :]).then_inc(s_vec, 16)
            sp.wait_ge(s_vec, 16 * (K + 2))
            for a in range(2):
                for k in range(K):
                    sp.dma_start(back[:, a, k, :],
                                 g.vec_s[k, a * TH * P:(a + 1) * TH * P].rearrange("(t p) -> t p", p=P)).then_inc(s_back, 16)

        @block.vector
        def _(v):
            c = Chain(v, s_v)
            v.wait_ge(s_load, 80)
            c.step(v.tensor_copy(nearf[:, :, :], near[:, :, :]))
            v.tensor_tensor(g.keep_w[:, :], nearf[:, 1, :], nearf[:, 0, :], ALU.is_equal)
            v.tensor_tensor(g.more_w[:, :], nearf[:, 1, :], nearf[:, 2, :], ALU.is_equal)
            v.tensor_copy(vec[:, SRC_H, :], raw[:, 0, :])
            c.step(v.tensor_copy(g.typ_w[:, :], raw[:, 1, :]))
            v.tensor_copy(vec[:, TYP, :], g.typ_w[:, :])
            v.tensor_scalar(g.last_w[:, :], g.more_w[:, :], -1.0, 1.0, ALU.mult, ALU.add)
            v.tensor_scalar(g.keepneg_w[:, :], g.keep_w[:, :], -1.0, BIG, ALU.add, ALU.mult)
            v.tensor_scalar(vec[:, SRC_C, :], vec[:, SRC_H, :], float(N - 1), None, ALU.min)
            v.tensor_scalar(vec[:, DST_C, :], nearf[:, 1, :], float(N - 1), None, ALU.min)
            c.step(v.tensor_scalar(real[:, :], nearf[:, 1, :], float(N), None, ALU.is_lt))
            c.step(v.tensor_tensor(tmp[:, :], real[:, :], g.last_w[:, :], ALU.mult))
            c.step(v.scalar_tensor_tensor(real[:, :], nearf[:, 1, :], float(-NOWHERE), tmp[:, :], ALU.add, ALU.mult))
            c.step(v.tensor_scalar(real[:, :], real[:, :], float(NOWHERE), None, ALU.add))
            v.tensor_copy(vec[:, PUT, :], real[:, :]).then_inc(s_wide, 1)
            v.wait_ge(s_pe, 2 * K)
            for a in range(2):
                v.tensor_scalar(g.put_info[:, a * TH:(a + 1) * TH], ps[:, a, PUT * TH:(PUT + 1) * TH], 4.0, 1.0, ALU.mult, ALU.add)
                for k, dest in enumerate((g.src_f, g.src_c, g.dst_c, g.put)):
                    v.tensor_copy(dest[:, a * TH:(a + 1) * TH], ps[:, a, k * TH:(k + 1) * TH])

        @block.tensor
        def _(pe):
            pe.wait_ge(s_back, 16 * 2 * K)
            for a in range(2):
                for k in range(K):
                    pe.transpose(ps[:, a, k * TH:(k + 1) * TH], back[:, a, k, :], g.ident[0:TH, 0:TH]).then_inc(s_pe, 1)


def degrees(nc, g):
    ctx = ExitStack()
    PER = 8
    s_all, s_cmp, s_mm, s_out, s_v, s_z, s_deg = (g.sem("dg_" + n) for n in ("all", "cmp", "mm", "out", "v", "z", "deg"))
    with ctx:
        sb = lambda n, s, d=F32: ctx.enter_context(nc.sbuf_tensor(n, s, d))
        src_i = sb("dg_src", [P, T], I32)
        part_i = sb("dg_part", [P, 2, T], I32)
        part = sb("dg_partf", [P, 2, T])
        lo1 = sb("dg_lo1", [P, PER, HL], F16)
        hi1 = sb("dg_hi1", [P, PER, P], F16)
        hist = sb("dg_hist", [HR, HL])
        zh = sb("dg_zh", [P, HL], F16)
        ps = ctx.enter_context(nc.psum_tensor("dg_ps", [P, HL], F32))
        block = ctx.enter_context(nc.Block())

        @block.sync
        def _(sp):
            sp.wait_ge(s_out, 1)
            sp.dma_start(g.deg_s.rearrange("(p w) -> p w", w=HL), hist[:, :]).then_inc(s_deg, 16)
            sp.wait_ge(s_deg, 16)

        @block.vector
        def _(v):
            v.memset(zh[:, :], 0.0).then_inc(s_z, 1)
            c = Chain(v, s_v)
            c.step(v.tensor_copy(src_i[:, :], g.src_f[:, :]))
            v.tensor_scalar(part_i[:, 0, :], src_i[:, :], 9, None, ALU.logical_shift_right)
            c.step(v.tensor_scalar(part_i[:, 1, :], src_i[:, :], HL - 1, None, ALU.bitwise_and))
            c.step(v.tensor_copy(part[:, :, :], part_i[:, :, :]))
            v.sem_inc(s_cmp, PER)
            with v.Fori(0, T // PER) as i:
                for k in range(PER):
                    v.wait_ge(s_mm, i * PER + k + 1)
                    v.tensor_scalar(hi1[:, k, :], g.iota_lo[:, 0:P], part[:, 0, bass.ds(i * PER + k, 1)], None, ALU.is_equal)
                    v.tensor_scalar(lo1[:, k, :], g.iota_lo[:, :], part[:, 1, bass.ds(i * PER + k, 1)], None,
                                    ALU.is_equal).then_inc(s_cmp, 1)
            v.wait_ge(s_all, 1)
            v.tensor_scalar(hist[:, :], ps[0:HR, :], 1.0, None, ALU.add).then_inc(s_out, 1)

        @block.tensor
        def _(pe):
            pe.wait_ge(s_z, 1)
            pe.matmul(ps[:, :], zh[:, 0:P], zh[:, :], start=True, stop=False)
            pe.sem_inc(s_mm, PER)
            with pe.Fori(0, T // PER) as i:
                for k in range(PER):
                    pe.wait_ge(s_cmp, i * PER + PER + k + 1)
                    pe.matmul(ps[:, :], hi1[:, k, :], lo1[:, k, :], start=False, stop=False).then_inc(s_mm, 1)
            pe.matmul(ps[:, :], zh[:, 0:P], zh[:, :], start=False, stop=True).then_inc(s_all, 1)


def node_info(nc, g):
    ctx = ExitStack()
    s_in, s_a, s_z, s_row, s_out = (g.sem("ni_" + n) for n in ("in", "a", "z", "row", "out"))
    with ctx:
        sb = lambda n, s, d=F32: ctx.enter_context(nc.sbuf_tensor(n, s, d))
        cols = sb("ni_cols", [NVR, 4, NV])
        rows = sb("ni_rows", [NVR, NV, 4])
        block = ctx.enter_context(nc.Block())

        @block.sync
        def _(sp):
            for k, a in ((0, g.deg_s[0:N]), (2, g.vec1[:, 0]), (3, g.vec2[:, 0])):
                sp.dma_start(cols[:, k, :], a.rearrange("(p w) -> p w", w=NV)).then_inc(s_in, 16)
            sp.wait_ge(s_row, 1)
            sp.dma_start(g.info_s.rearrange("(p w) k -> p (w k)", w=NV * 4), rows[:, :, :].rearrange("p w k -> p (w k)")).then_inc(s_out, 16)
            sp.wait_ge(s_out, 16)

        @block.scalar
        def _(a):
            a.preload_act_table_set("natural_log_exp_and_others")
            a.wait_ge(s_in, 48)
            a.activation(cols[:, 0, :], cols[:, 0, :], ACT.Ln).then_inc(s_a, 1)
            a.wait_ge(s_a, 1)
            a.activation(cols[:, 0, :], cols[:, 0, :], ACT.Exp, scale=-0.5).then_inc(s_a, 1)

        @block.vector
        def _(v):
            v.memset(cols[:, 1, :], 0.0).then_inc(s_z, 1)
            v.wait_ge(s_z, 1)
            v.wait_ge(s_a, 2)
            v.wait_ge(s_in, 48)
            v.tensor_copy(rows[:, :, :].rearrange("p w k -> p k w"), cols[:, :, :]).then_inc(s_row, 1)


def edge_columns(nc, g):
    ctx = ExitStack()
    s_v = g.sem("cl_v")
    with ctx:
        has, part, alls = (ctx.enter_context(nc.sbuf_tensor("cl_" + n, [P, T], F32)) for n in ("has", "part", "alls"))
        block = ctx.enter_context(nc.Block())

        @block.vector
        def _(v):
            c = Chain(v, s_v)
            v.tensor_copy(g.norm_src[:, :], g.by_src[:, :, 0])
            v.tensor_copy(g.vec_src[:, :], g.by_src[:, :, 2])
            v.tensor_copy(g.norm_dst[:, :], g.by_dst[:, :, 0])
            v.tensor_scalar(g.vec_dst[:, :], g.by_dst[:, :, 3], 1.0 / (4.0 * 8.0), None, ALU.mult)
            c.step(v.tensor_scalar(has[:, :], g.by_src[:, :, 1], 0.5, None, ALU.is_gt))
            v.tensor_scalar(g.nohas[:, :], has[:, :], -1.0, 1.0, ALU.mult, ALU.add)
            c.step(v.tensor_copy(alls[:, :], g.src_c[:, :]))
            for dest, base, other in ((g.row_x, N, 0), (g.row_h, 0, EP)):
                if other:
                    c.step(v.tensor_scalar(part[:, :], g.by_src[:, :, 1], float(base - 1 - other), None, ALU.add))
                    c.step(v.tensor_tensor(part[:, :], part[:, :], has[:, :], ALU.mult))
                    c.step(v.tensor_scalar(dest[:, :], part[:, :], float(other), None, ALU.add))
                else:
                    c.step(v.scalar_tensor_tensor(part[:, :], g.by_src[:, :, 1], float(base - 1), alls[:, :], ALU.add, ALU.subtract))
                    c.step(v.tensor_tensor(part[:, :], part[:, :], has[:, :], ALU.mult))
                    c.step(v.tensor_tensor(dest[:, :], part[:, :], alls[:, :], ALU.add))


def weights(nc, g):
    ctx = ExitStack()
    s_ld, s_z, s_zd, s_big, s_bl, s_pe, s_v, s_a, s_d, s_w = (g.sem("wt_" + n) for n in ("ld", "z", "zd", "big", "bl", "pe", "v", "a", "d", "w"))
    with ctx:
        sb = lambda n, s, d=F32: ctx.enter_context(nc.sbuf_tensor(n, s, d))
        zero = sb("wt_zero", [P, 3 * P])
        wT = sb("wt_T", [P, 18, P])
        att = sb("wt_att", [P, 2, 2 * NH])
        bu = sb("wt_bu", [1, P])
        ps = ctx.enter_context(nc.psum_tensor("wt_ps", [P, 5, 4, P], F32))
        pm = ctx.enter_context(nc.psum_tensor("wt_pm", [P, 2, HL], F32))
        block = ctx.enter_context(nc.Block())
        col = lambda a: a.unsqueeze(1)
        loads = [(g.w0[:, :], g.L0_W), (g.w12[:, 0:P], g.L3_W1), (g.w12[:, P:2 * P], g.L3_W2),
                 (g.wu[:, :, :], g.L3_Wu.rearrange("(k p) n -> p k n", p=P)),
                 (g.wr[:, :, :], g.L1_W.rearrange("l r f g -> f (l r) g")),
                 (g.wfc1[:, :], g.L2_Wfc1), (g.wfc2[:, :], g.L2_Wfc2), (bu[0:1, :], g.L3_bu.unsqueeze(0)),
                 (g.b1_rows[:, :], g.L1_bias[1, :].partition_broadcast(P))]
        for l in range(2):
            loads += [(g.att_q[:, l:l + 1], g.L1_att_q[l, :, :]), (g.att_k[:, l:l + 1], g.L1_att_k[l, :, :]),
                      (g.b1_col[:, l:l + 1], col(g.L1_bias[l, :]))]
        loads += [(g.ln_g[:, :], col(g.L3_ln_g)), (g.ln_b[:, :], col(g.L3_ln_b)),
                  (g.b12[:, 0:1], col(g.L3_b1)), (g.b12[:, 1:2], col(g.L3_b2))]
        heads = []
        for h in range(H1):
            heads += [(att[O1 * h:O1 * h + O1, 0, h:h + 1], col(g.L3_a1s[h, :])),
                      (att[O1 * h:O1 * h + O1, 0, NH + h:NH + h + 1], col(g.L3_a1d[h, :]))]
        for h in range(H2):
            heads += [(att[O2 * h:O2 * h + O2, 1, H1 + h:H1 + h + 1], col(g.L3_a2s[h, :])),
                      (att[O2 * h:O2 * h + O2, 1, NH + H1 + h:NH + H1 + h + 1], col(g.L3_a2d[h, :]))]
        S, V = MUL, 3 * MUL
        pieces = [(g.w1big_s[0:S, 0:S], g.L2_w1_s), (g.w2big_s[0:S, 0:S], g.L2_w2_s[0, :, :]),
                  (g.w2big_s[S:2 * S, 0:S], g.L2_w2_s[1, :, :])]
        for i in range(3):
            at = lambda rows, base: rows[base:base + V, S:S + V].rearrange("(u a) (w b) -> a b u w", a=3, b=3)[i, i, :, :]
            pieces += [(at(g.w1big_s, S), g.L2_w1_v), (at(g.w2big_s, 2 * S), g.L2_w2_v[0, :, :]),
                       (at(g.w2big_s, 2 * S + V), g.L2_w2_v[1, :, :])]

        @block.sync
        def _(sp):
            for dest, src in loads:
                sp.dma_start(dest, src).then_inc(s_ld, 16)
            sp.wait_ge(s_z, 1)
            sp.dma_start(g.w1big_s, zero[:, 0:P]).then_inc(s_zd, 16)
            sp.dma_start(g.w2big_s.rearrange("(k p) n -> p k n", p=P), zero[:, P:3 * P].rearrange("p (k n) -> p k n", k=2)).then_inc(s_zd, 16)
            for dest, src in heads:
                sp.dma_start(dest, src).then_inc(s_ld, 16)
            sp.wait_ge(s_zd, 32)
            with nc.allow_non_contiguous_dma(reason="small weights laid out once"):
                for dest, src in pieces:
                    sp.dma_start(dest, src).then_inc(s_big, 16)
            sp.wait_ge(s_big, 16 * len(pieces))
            sp.dma_start(g.w1big[:, :], g.w1big_s).then_inc(s_bl, 16)
            sp.dma_start(g.w2big[:, :, :], g.w2big_s.rearrange("(k p) n -> p k n", p=P)).then_inc(s_bl, 16)
            sp.wait_ge(s_w, 1)
            sp.dma_start(g.h_tab[EP:EP + 1, :], g.b0_row[0:1, :]).then_inc(s_d, 16)
            sp.wait_ge(s_d, 16)

        @block.vector
        def _(v):
            v.memset(att[:, :, :], 0.0)
            v.memset(zero[:, :], 0.0).then_inc(s_z, 1)
            c = Chain(v, s_v)
            v.wait_ge(s_ld, 16 * (len(loads) + len(heads)))
            c.step(v.tensor_scalar(g.b1_rows[:, :], g.b1_rows[:, :], 0.0, None, ALU.max))
            v.wait_ge(s_pe, 18)
            for n in range(18):
                v.tensor_copy(wT[:, n, :], ps[:, n // 4, n % 4, :])
            v.wait_ge(s_bl, 32)
            v.tensor_scalar(g.w1big[:, :], g.w1big[:, :], float(1 / np.sqrt(MUL)), None, ALU.mult)
            v.tensor_scalar(g.w2big[S:2 * S, 0, :], g.w2big[S:2 * S, 0, :], float(1 / np.sqrt(3.0)), None, ALU.mult)
            c.step(v.tensor_scalar(g.wfc2[:, :], g.wfc2[:, :], float(1 / np.sqrt(HID)), None, ALU.mult))
            v.wait_ge(s_pe, 18 + 3)
            v.tensor_copy(g.wq[:, :], pm[:, 0, 0:16])
            v.tensor_copy(g.wa[:, :], pm[:, 0, 16:16 + 2 * NH])
            v.tensor_tensor(g.bu_row[0:1, :], bu[0:1, :], pm[0:1, 1, 0:P], ALU.subtract)
            v.tensor_scalar(g.b0_row[0:1, :], pm[0:1, 1, P:2 * P], 0.0, None, ALU.max).then_inc(s_w, 1)

        @block.tensor
        def _(pe):
            pe.wait_ge(s_ld, 16 * (len(loads) + len(heads)))
            for n in range(16):
                pe.transpose(ps[:, n // 4, n % 4, :], g.wr[:, n, :], g.ident[:, :]).then_inc(s_pe, 1)
            for n in range(2):
                pe.transpose(ps[:, 4, n, :], g.w12[:, n * P:(n + 1) * P], g.ident[:, :]).then_inc(s_pe, 1)
            pe.wait_ge(s_v, 2)
            for n in range(16):
                last = pe.matmul(pm[:, 0, n:n + 1], wT[:, n, :], g.att_q[:, n // R_:n // R_ + 1], start=True, stop=True)
            last.then_inc(s_pe, 1)
            for k in range(2):
                last = pe.matmul(pm[:, 0, 16:16 + 2 * NH], wT[:, 16 + k, :], att[:, k, :], start=(k == 0), stop=(k == 1))
            last.then_inc(s_pe, 1)
            for k in range(2):
                pe.matmul(pm[0:1, 1, 0:P], g.ones_col[:, :], g.wu[:, k, :], start=(k == 0), stop=(k == 1))
            pe.matmul(pm[0:1, 1, P:2 * P], g.b1_col[:, 0:1], g.ident[:, :], start=True, stop=True).then_inc(s_pe, 1)


def stats(v, c, g, x4, st, mv, done):
    for j in range(J):
        last = v.bn_stats(st[:, j, :], x4[:, j, :])
    c.step(last)
    v.sem_inc(g.state.waits, 1)
    for j in range(J):
        last = v.bn_aggr(mv[:, j, :], st[:, j, :])
    last.then_inc(done, 1)


def rstd(a, g, c, mv, rs, done):
    c.step(a.activation(rs[:, :], mv[:, :, 1], ACT.Ln, bias=g.eps_ln[:, :]))
    a.activation(rs[:, :], rs[:, :], ACT.Exp, scale=-0.5).then_inc(done, 1)


def normalise(v, x4, mv, rs, y4, done):
    for j in range(J):
        last = v.tensor_scalar(y4[:, j, :], x4[:, j, :], mv[:, j, 0:1], rs[:, j:j + 1], ALU.subtract, ALU.mult)
    last.then_inc(done, 1)


def transpose4(pe, g, ps, y4, done):
    for j in range(J):
        last = pe.transpose(ps[:, j * P:(j + 1) * P], y4[:, j, :], g.ident[:, :])
    last.then_inc(done, 1)


def four(t):
    return t.rearrange("p (j f) -> p j f", j=J)


def node_dense(nc, g):
    by = Cut(4)
    H, SUP = by.H, by.size
    ctx = ExitStack()
    names = "st rs ya t1 e1 yy ss ssw ri q r2 x1 z sz rz nm hh sh rh nn t2 e2 o eo u ou zh fo".split()
    ev = events(g, "nd_", names)
    s_v, s_a, s_p, s_q, l_i, w_i = (g.sem("nd_" + n) for n in ("v", "a", "p", "pq", "li", "wi"))
    l_x, l_d, w_1, w_o = ([g.sem(f"nd_{n}{h}") for h in range(H)] for n in ("lx", "ld", "w1", "wo"))
    with ctx:
        sb = lambda n, s, d=F32: ctx.enter_context(nc.sbuf_tensor("nd_" + n, s, d))
        each_part = lambda n, s: [sb(f"{n}{h}", s) for h in range(H)]
        x, y, junk, x1, z, hh, n_, ot, et = (each_part(n, [P, J, P]) for n in ("x", "y", "junk", "x1", "z", "hh", "n", "ot", "et"))
        aT, nT = each_part("aT", [P, HW]), each_part("nT", [P, HW])
        eo, ro, u = (each_part(n, [P, 2, HW]) for n in ("eo", "ro", "u"))
        st, mv, stz, mvz, sth, mvh = (each_part(n, [P, J, 6 if n[:2] == "st" else 2]) for n in ("st", "mv", "stz", "mvz", "sth", "mvh"))
        rs, rz, rh, nm, ss, ssw, ri, q, deg, inv = (each_part(n, [P, J]) for n in ("rs", "rz", "rh", "nm", "ss", "ssw", "ri", "q", "deg", "inv"))
        pO = [ctx.enter_context(nc.psum_tensor(f"nd_pO{h}", [P, 2, HW], F32)) for h in range(H)]
        block = ctx.enter_context(nc.Block())
        FULL = N // SUP
        TURNS = FULL + 1
        PUTS = 5
        PER_PUT, PER = T // PUTS, T // (TURNS - PUTS)
        assert PER_PUT * PUTS == T and PER * (TURNS - PUTS) == T
        put_now, no_now = sb("put_now", [P, PER_PUT], I32), sb("no_now", [P, PER_PUT])
        slot = sb("slot", [P, 2, PER, 4])
        at_src, at_dst = sb("at_src", [P, PER], I32), sb("at_dst", [P, PER], I32)

        def sweep(eng, body):
            with eng.Fori(0, FULL) as i:
                body(i, i * SUP)
            body(FULL, N - SUP)

        def rows(a, base, h):
            return a[bass.ds(base, SUP), :].rearrange("(p j) f -> p j f", j=H * J)[:, h * J:(h + 1) * J, :]

        @block.sync
        def _(sp):
            def load(i, base):
                for h in range(H):
                    if i is not None:
                        sp.wait_ge(ev.x1, by.now(i, h))
                    sp.dma_start(x[h][:, :, :], rows(g.x, base, h)).then_inc(l_x[h], 16)
                    sp.dma_start(deg[h][:, :], g.deg_s[bass.ds(base, SUP)].rearrange("(p j) -> p j", j=H * J)[:, h * J:(h + 1) * J]).then_inc(l_d[h], 16)

            def body(i, base, following):
                if following is not None:
                    load(i, following)
                for h in range(H):
                    sp.wait_ge(ev.x1, by.now(i, h))
                    if following is None and h == 0:
                        for k in range(H):
                            sp.wait_ge(w_1[k], 32 * FULL)
                            sp.wait_ge(w_o[k], 16 * FULL)
                    for table in (g.tab_a, g.tab_b):
                        sp.dma_start(rows(table, base, h), x1[h][:, :, :]).then_inc(w_1[h], 16)
                for h in range(H):
                    sp.wait_ge(ev.fo, by.now(i, h))
                    sp.dma_start(rows(g.out, base, h), ot[h][:, :, :]).then_inc(w_o[h], 16)

            load(None, 0)
            with sp.Fori(0, FULL - 1) as i:
                body(i, i * SUP, i * SUP + SUP)
            body(FULL - 1, (FULL - 1) * SUP, N - SUP)
            body(FULL, N - SUP, None)
            for h in range(H):
                sp.wait_ge(w_1[h], 32 * (FULL + 1))
                sp.wait_ge(w_o[h], 16 * (FULL + 1))

        @block.gpsimd
        def _(pool):
            by.credit(pool, ev.zh)
            info = g.info_s.rearrange("(n k) o -> n (k o)", k=4)

            def hidden(i):
                for h in range(H):
                    pool.wait_ge(ev.hh, by.now(i, h))
                    pool.tensor_tensor(z[h][:, :, :], z[h][:, :, :], hh[h][:, :, :], ALU.add).then_inc(ev.zh, 1)

            c = Chain(pool, s_p, 2, g)
            with pool.Fori(0, PUTS) as i:
                c.turn(i)
                c.step(pool.tensor_copy(put_now[:, :], g.put_info[:, bass.ds(i * PER_PUT, PER_PUT)]))
                c.step(pool.tensor_copy(no_now[:, :], g.edge_no[:, bass.ds(i * PER_PUT, PER_PUT)]))
                for k in range(PER_PUT):
                    pool.indirect_dma_start(g.info_s, bass.IndirectOffsetOnAxis(ap=put_now[:, k:k + 1], axis=0),
                                            no_now[:, k:k + 1], None, bounds_check=4 * N - 1, oob_is_err=False).then_inc(w_i, 16)
                hidden(i)
                wait_alone(g, pool, w_i, i * 16 * PER_PUT + 16 * PER_PUT)
            c = Chain(pool, s_q, 4, g)
            with pool.Fori(0, TURNS - PUTS) as i:
                c.turn(i)
                c.step(pool.tensor_copy(at_src[:, :], g.src_c[:, bass.ds(i * PER, PER)]))
                c.step(pool.tensor_copy(at_dst[:, :], g.dst_c[:, bass.ds(i * PER, PER)]))
                for k in range(PER):
                    for side, at in enumerate((at_src, at_dst)):
                        pool.indirect_dma_start(slot[:, side, k, :], None, info,
                                                bass.IndirectOffsetOnAxis(ap=at[:, k:k + 1], axis=0)).then_inc(l_i, 16)
                hidden(i + PUTS)
                wait_alone(g, pool, l_i, i * 32 * PER + 32 * PER)
                c.step(pool.tensor_copy(g.by_src[:, bass.ds(i * PER, PER), :], slot[:, 0, :, :]))
                c.step(pool.tensor_copy(g.by_dst[:, bass.ds(i * PER, PER), :], slot[:, 1, :, :]))

        @block.vector
        def _(v):
            by.credit(v, ev.st, ev.ya, ev.ssw, ev.q, ev.x1, ev.z, ev.sz, ev.nm, ev.sh, ev.nn, ev.u, ev.fo)
            c = Chain(v, s_v, 7 * H)

            def body(i, base):
                c.turn(i)
                for h in range(H):
                    v.wait_ge(l_x[h], 16 * i + 16)
                    stats(v, c, g, x[h], st[h], mv[h], ev.st)
                for h in range(H):
                    v.wait_ge(ev.rs, by.now(i, h))
                    v.wait_ge(ev.t1, by.before(i, h))
                    normalise(v, x[h], mv[h], rs[h], y[h], ev.ya)
                for h in range(H):
                    v.wait_ge(l_d[h], 16 * i + 16)
                    c.step(v.reciprocal(inv[h][:, :], deg[h][:, :]))
                    v.wait_ge(ev.ss, by.now(i, h))
                    c.step(v.tensor_tensor(ssw[h][:, :], ss[h][:, :], inv[h][:, :], ALU.mult))
                    c.step(v.tensor_tensor(ssw[h][:, :], ssw[h][:, :], inv[h][:, :], ALU.mult))
                    v.tensor_scalar(ssw[h][:, :], ssw[h][:, :], 1e-30, None, ALU.max).then_inc(ev.ssw, 1)
                for h in range(H):
                    v.wait_ge(ev.ri, by.now(i, h))
                    c.step(v.scalar_tensor_tensor(q[h][:, :], ri[h][:, :], 1e12, inv[h][:, :], ALU.min, ALU.mult))
                    v.tensor_scalar(q[h][:, :], q[h][:, :], 2.0, None, ALU.mult).then_inc(ev.q, 1)
                for h in range(H):
                    v.wait_ge(ev.r2, by.now(i, h))
                    v.wait_ge(w_1[h], 32 * i)
                    v.scalar_tensor_tensor(x1[h][:, :, :], x[h][:, :, :], 1.0, et[h][:, :, :], ALU.add, ALU.subtract).then_inc(ev.x1, 1)
                    v.wait_ge(ev.x1, by.now(i, h))
                    v.wait_ge(ev.fo, by.before(i, h))
                    v.tensor_tensor(z[h][:, :, :], x1[h][:, :, :], g.b1_rows[:, :].unsqueeze(1).broadcast_to([P, J, P]), ALU.add).then_inc(ev.z, 1)
                    v.wait_ge(ev.z, by.now(i, h))
                    stats(v, c, g, z[h], stz[h], mvz[h], ev.sz)
                for h in range(H):
                    v.wait_ge(ev.rz, by.now(i, h))
                    v.scalar_tensor_tensor(nm[h][:, :], mvz[h][:, :, 0], -1.0, rz[h][:, :], ALU.mult, ALU.mult).then_inc(ev.nm, 1)
                for h in range(H):
                    v.wait_ge(ev.hh, by.now(i, h))
                    stats(v, c, g, hh[h], sth[h], mvh[h], ev.sh)
                for h in range(H):
                    v.wait_ge(ev.rh, by.now(i, h))
                    v.wait_ge(ev.t2, by.before(i, h))
                    normalise(v, hh[h], mvh[h], rh[h], n_[h], ev.nn)
                for h in range(H):
                    v.wait_ge(ev.eo, by.now(i, h))
                    v.wait_ge(ev.ou, by.before(i, h))
                    v.scalar_tensor_tensor(u[h][:, :, :], eo[h][:, :, :], 1.0, ro[h][:, :, :], ALU.min, ALU.add).then_inc(ev.u, 1)
                for h in range(H):
                    v.wait_ge(ev.ou, by.now(i, h))
                    v.wait_ge(ev.zh, by.now(i, h))
                    v.wait_ge(w_o[h], 16 * i)
                    v.tensor_tensor(ot[h][:, :, :], four(pO[h][:, 0, :]), z[h][:, :, :], ALU.add).then_inc(ev.fo, 1)
            sweep(v, body)

        @block.scalar
        def _(a):
            a.preload_act_table_set("natural_log_exp_and_others")
            c = Chain(a, s_a, 6 * H)
            by.credit(a, ev.rs, ev.e1, ev.ss, ev.ri, ev.r2, ev.rz, ev.hh, ev.rh, ev.e2, ev.eo)

            def body(i, base):
                c.turn(i)
                for h in range(H):
                    a.wait_ge(ev.st, by.now(i, h))
                    rstd(a, g, c, mv[h], rs[h], ev.rs)
                for h in range(H):
                    a.wait_ge(ev.t1, by.now(i, h))
                    a.wait_ge(ev.yy, by.before(i, h))
                    a.activation(aT[h][:, :], pO[h][:, 0, :], ACT.Relu).then_inc(ev.e1, 1)
                for h in range(H):
                    a.wait_ge(ev.yy, by.now(i, h))
                    a.wait_ge(ev.ss, by.before(i, h))
                    for j in range(J):
                        last = a.activation(junk[h][:, j, :], pO[h][:, 1, j * P:(j + 1) * P], ACT.Square, accum_out=ss[h][:, j:j + 1])
                    last.then_inc(ev.ss, 1)
                for h in range(H):
                    a.wait_ge(ev.ssw, by.now(i, h))
                    c.step(a.activation(ri[h][:, :], ssw[h][:, :], ACT.Ln))
                    a.activation(ri[h][:, :], ri[h][:, :], ACT.Exp, scale=-0.5).then_inc(ev.ri, 1)
                for h in range(H):
                    a.wait_ge(ev.q, by.now(i, h))
                    a.wait_ge(ev.x1, by.before(i, h))
                    for j in range(J):
                        last = a.activation(et[h][:, j, :], pO[h][:, 1, j * P:(j + 1) * P], ACT.Exp, scale=q[h][:, j:j + 1])
                    c.step(last)
                    c.step(a.activation(et[h][:, :, :], et[h][:, :, :], ACT.Ln, bias=1.0))
                    a.activation(et[h][:, :, :], et[h][:, :, :], ACT.Exp, scale=-1.0, bias=g.log2_col[:, :]).then_inc(ev.r2, 1)
                for h in range(H):
                    a.wait_ge(ev.sz, by.now(i, h))
                    rstd(a, g, c, mvz[h], rz[h], ev.rz)
                for h in range(H):
                    a.wait_ge(ev.nm, by.now(i, h))
                    a.wait_ge(ev.zh, by.before(i, h))
                    a.wait_ge(ev.nn, by.before(i, h))
                    for j in range(J):
                        last = a.activation(hh[h][:, j, :], z[h][:, j, :], ACT.Relu, scale=rz[h][:, j:j + 1], bias=nm[h][:, j:j + 1])
                    last.then_inc(ev.hh, 1)
                for h in range(H):
                    a.wait_ge(ev.sh, by.now(i, h))
                    rstd(a, g, c, mvh[h], rh[h], ev.rh)
                for h in range(H):
                    a.wait_ge(ev.t2, by.now(i, h))
                    a.wait_ge(ev.o, by.before(i, h))
                    a.activation(nT[h][:, :], pO[h][:, 0, :], ACT.Identity, scale=g.ln_g[:, :], bias=g.ln_b[:, :]).then_inc(ev.e2, 1)
                for h in range(H):
                    a.wait_ge(ev.o, by.now(i, h))
                    a.wait_ge(ev.u, by.before(i, h))
                    for k in range(2):
                        a.activation(eo[h][:, k, :], pO[h][:, k, :], ACT.Exp, bias=g.b12[:, k:k + 1])
                        last = a.activation(ro[h][:, k, :], pO[h][:, k, :], ACT.Relu, bias=g.b12[:, k:k + 1])
                    last.then_inc(ev.eo, 1)
            sweep(a, body)

        @block.tensor
        def _(pe):
            by.credit(pe, ev.t1, ev.yy, ev.t2, ev.o, ev.ou)

            def body(i, base):
                for h in range(H):
                    pe.wait_ge(ev.ya, by.now(i, h))
                    pe.wait_ge(ev.fo, by.before(i, h))
                    transpose4(pe, g, pO[h][:, 0, :], y[h], ev.t1)
                for h in range(H):
                    pe.wait_ge(ev.e1, by.now(i, h))
                    for j in range(J):
                        last = pe.matmul(pO[h][:, 1, j * P:(j + 1) * P], aT[h][:, j * P:(j + 1) * P], g.w0[:, :], start=True, stop=True)
                    last.then_inc(ev.yy, 1)
                for h in range(H):
                    pe.wait_ge(ev.nn, by.now(i, h))
                    transpose4(pe, g, pO[h][:, 0, :], n_[h], ev.t2)
                for h in range(H):
                    pe.wait_ge(ev.e2, by.now(i, h))
                    pe.wait_ge(ev.eo, by.before(i, h))
                    for k in range(2):
                        last = pe.matmul(pO[h][:, k, :], g.w12[:, k * P:(k + 1) * P], nT[h][:, :], start=True, stop=True)
                    last.then_inc(ev.o, 1)
                for h in range(H):
                    pe.wait_ge(ev.u, by.now(i, h))
                    pe.wait_ge(ev.r2, by.now(i, h))
                    for j in range(J):
                        o = pO[h][:, 0, j * P:(j + 1) * P]
                        pe.matmul(o, u[h][:, 0, j * P:(j + 1) * P], g.wu[:, 0, :], start=True, stop=False)
                        pe.matmul(o, u[h][:, 1, j * P:(j + 1) * P], g.wu[:, 1, :], start=False, stop=False)
                        last = pe.matmul(o, g.ones_row[:, :], g.bu_row[:, :], start=False, stop=True)
                    last.then_inc(ev.ou, 1)
            sweep(pe, body)


class Cut:

    def __init__(self, H):
        self.H, self.size = H, H * HW
        self.full, self.left = EP // self.size, EP % self.size // HW

    def turns(self, h):
        return self.full + (h < self.left)

    def sweep(self, eng, body):
        with eng.Fori(0, self.full) as i:
            body(i, range(self.H))
        if self.left:
            body(self.full, range(self.left))

    def now(self, i, h):
        return self.H * i + h + 1 + self.H

    def before(self, i, h):
        return self.H * i + h + 1

    def credit(self, eng, *sems):
        for s in sems:
            eng.sem_inc(s, self.H)

    def span(self, i, h):
        return bass.ds(i * self.size + h * HW, HW)

    def tiles(self, i, h):
        return bass.ds(i * self.H * J + h * J, J)

    def edge_rows(self, a, base, i, h):
        return a[bass.ds(i * self.size + base + h * HW, HW), :].rearrange("(j p) f -> p j f", p=P)

    def row_part(self, a, i, h):
        return a[self.span(i, h)].partition_broadcast(P)

    def allocators(self, nc, ctx, prefix):
        sb = lambda n, s, d=F32: ctx.enter_context(nc.sbuf_tensor(prefix + n, s, d))
        each_part = lambda n, s, d=F32: [sb(f"{n}{h}", s, d) for h in range(self.H)]
        bank = lambda n: [ctx.enter_context(nc.psum_tensor(f"{prefix}{n}{h}", [P, HW], F32)) for h in range(self.H)]
        return sb, each_part, bank


def gather(pool, table, index, dest, done):
    for j in range(J):
        pool.indirect_dma_start(dest[:, j, :], None, table, bass.IndirectOffsetOnAxis(ap=index[:, j:j + 1], axis=0)).then_inc(done, 16)


def layer0_edges(nc, g):
    by = Cut(4)
    H = by.H
    ctx = ExitStack()
    names = "st sd rs rd ys yd ts td gs gd sc yy ss ssw ri q r2 x1 sx rx yx tx hx pq pe".split()
    ev = events(g, "e0_", names)
    s_v, s_a, s_p, s_0 = g.sem("e0_v"), g.sem("e0_a"), g.sem("e0_p"), g.sem("e0_zero")
    l_s, l_d, l_k, w_x, w_q = ([g.sem(f"e0_{n}{h}") for h in range(H)] for n in ("ls", "ld", "lk", "wx", "wq"))
    with ctx:
        sb, each_part, bank = by.allocators(nc, ctx, "e0_")
        xs, xd, y, yx, junk, et, x1 = (each_part(n, [P, J, P]) for n in ("xs", "xd", "y", "yx", "junk", "et", "x1"))
        yd = each_part("yd", [P, J, P])
        keep, gT, dT, hT = (each_part(n, [P, HW]) for n in ("keep", "gT", "dT", "hT"))
        agg = each_part("agg", [P, HW])
        at_s, at_d = each_part("at_s", [P, J], I32), each_part("at_d", [P, J], I32)
        st, mv, sd, md, sx, mx = (each_part(n, [P, J, 6 if n[0] == "s" else 2]) for n in ("st", "mv", "sd", "md", "sx", "mx"))
        rs, rd, rx, ns, nd, ss, ssw, ri, q = (each_part(n, [P, J]) for n in ("rs", "rd", "rx", "ns", "nd", "ss", "ssw", "ri", "q"))
        pq = each_part("pq", [R_, HW])
        pS = pY = pQ = bank("pS")
        pD = pX = bank("pD")
        block = ctx.enter_context(nc.Block())

        @block.sync
        def _(sp):
            def body(i, part):
                for h in part:
                    sp.wait_ge(ev.sc, by.before(i, h))
                    sp.dma_start(keep[h][:, :], by.row_part(g.keep_s, i, h)).then_inc(l_k[h], 16)
                for h in part:
                    sp.wait_ge(ev.x1, by.now(i, h))
                    sp.dma_start(by.edge_rows(g.tab_a, N, i, h), x1[h][:, :, :]).then_inc(w_x[h], 16)
                for h in part:
                    sp.wait_ge(ev.pe, by.now(i, h))
                    sp.dma_start(g.pq_s[:, by.span(i, h)], pq[h][:, :]).then_inc(w_q[h], 16)
            by.sweep(sp, body)
            for h in range(H):
                sp.wait_ge(w_x[h], 16 * by.turns(h))
                sp.wait_ge(w_q[h], 16 * by.turns(h))

        @block.gpsimd
        def _(pool):
            c = Chain(pool, s_p, 2 * H, g)
            def body(i, part):
                c.turn(i)
                for h in part:
                    wait_alone(g, pool, ev.ys, by.before(i, h))
                    c.step(pool.tensor_copy(at_s[h][:, :], g.src_c[:, by.tiles(i, h)]))
                    gather(pool, g.x, at_s[h], xs[h], l_s[h])
                for h in part:
                    wait_alone(g, pool, ev.x1, by.before(i, h))
                    c.step(pool.tensor_copy(at_d[h][:, :], g.dst_c[:, by.tiles(i, h)]))
                    gather(pool, g.x, at_d[h], xd[h], l_d[h])
            by.sweep(pool, body)

        @block.vector
        def _(v):
            by.credit(v, ev.st, ev.sd, ev.ys, ev.yd, ev.sc, ev.ssw, ev.q, ev.x1, ev.sx, ev.yx)
            v.memset(agg[H - 1][:, HW - 1:HW], 0.0).then_inc(s_0, 1)
            v.wait_ge(s_0, 1)
            c = Chain(v, s_v, 8 * H)

            def body(i, part):
                c.turn(i)
                for h in part:
                    v.wait_ge(l_s[h], 64 * i + 64)
                    stats(v, c, g, xs[h], st[h], mv[h], ev.st)
                for h in part:
                    v.wait_ge(l_d[h], 64 * i + 64)
                    stats(v, c, g, xd[h], sd[h], md[h], ev.sd)
                for h in part:
                    tiles = by.tiles(i, h)
                    v.wait_ge(ev.rs, by.now(i, h))
                    c.step(v.tensor_tensor(ns[h][:, :], rs[h][:, :], g.norm_src[:, tiles], ALU.mult))
                    v.wait_ge(ev.ts, by.before(i, h))
                    normalise(v, xs[h], mv[h], ns[h], y[h], ev.ys)
                for h in part:
                    tiles = by.tiles(i, h)
                    v.wait_ge(ev.rd, by.now(i, h))
                    c.step(v.tensor_tensor(nd[h][:, :], rd[h][:, :], g.norm_dst[:, tiles], ALU.mult))
                    v.wait_ge(ev.td, by.before(i, h))
                    normalise(v, xd[h], md[h], nd[h], yd[h], ev.yd)
                for h in part:
                    v.wait_ge(ev.gs, by.now(i, h))
                    v.wait_ge(l_k[h], 16 * i + 16)
                    v.wait_ge(ev.yy, by.before(i, h))
                    v.wait_ge(ev.sc, by.now(i, h) - 1)
                    v.tensor_tensor_scan(agg[h][:, :], keep[h][:, :], gT[h][:, :], agg[h - 1][:, HW - 1:HW], ALU.mult, ALU.add).then_inc(ev.sc, 1)
                for h in part:
                    tiles = by.tiles(i, h)
                    v.wait_ge(ev.ss, by.now(i, h))
                    c.step(v.tensor_tensor(ssw[h][:, :], ss[h][:, :], g.norm_dst[:, tiles], ALU.mult))
                    c.step(v.tensor_tensor(ssw[h][:, :], ssw[h][:, :], g.norm_dst[:, tiles], ALU.mult))
                    v.tensor_scalar(ssw[h][:, :], ssw[h][:, :], 1e-30, None, ALU.max).then_inc(ev.ssw, 1)
                for h in part:
                    tiles = by.tiles(i, h)
                    v.wait_ge(ev.ri, by.now(i, h))
                    c.step(v.scalar_tensor_tensor(q[h][:, :], ri[h][:, :], 1e12, g.norm_dst[:, tiles], ALU.min, ALU.mult))
                    v.tensor_scalar(q[h][:, :], q[h][:, :], 2.0, None, ALU.mult).then_inc(ev.q, 1)
                for h in part:
                    v.wait_ge(ev.r2, by.now(i, h))
                    v.wait_ge(w_x[h], 16 * i)
                    v.scalar_tensor_tensor(x1[h][:, :, :], xd[h][:, :, :], 1.0, et[h][:, :, :], ALU.add, ALU.subtract).then_inc(ev.x1, 1)
                    v.wait_ge(ev.x1, by.now(i, h))
                    stats(v, c, g, x1[h], sx[h], mx[h], ev.sx)
                for h in part:
                    v.wait_ge(ev.rx, by.now(i, h))
                    v.wait_ge(ev.tx, by.before(i, h))
                    normalise(v, x1[h], mx[h], rx[h], yx[h], ev.yx)
            by.sweep(v, body)

        @block.scalar
        def _(a):
            a.preload_act_table_set("natural_log_exp_and_others")
            c = Chain(a, s_a, 6 * H)
            by.credit(a, ev.rs, ev.rd, ev.gs, ev.gd, ev.ss, ev.ri, ev.r2, ev.rx, ev.hx, ev.pe)

            def body(i, part):
                c.turn(i)
                for h in part:
                    a.wait_ge(ev.st, by.now(i, h))
                    rstd(a, g, c, mv[h], rs[h], ev.rs)
                for h in part:
                    a.wait_ge(ev.sd, by.now(i, h))
                    rstd(a, g, c, md[h], rd[h], ev.rd)
                for h in part:
                    a.wait_ge(ev.ts, by.now(i, h))
                    a.wait_ge(ev.sc, by.before(i, h))
                    a.activation(gT[h][:, :], pS[h][:, :], ACT.Relu).then_inc(ev.gs, 1)
                for h in part:
                    a.wait_ge(ev.td, by.now(i, h))
                    a.wait_ge(ev.yy, by.before(i, h))
                    a.activation(dT[h][:, :], pD[h][:, :], ACT.Relu).then_inc(ev.gd, 1)
                for h in part:
                    a.wait_ge(ev.yy, by.now(i, h))
                    a.wait_ge(ev.ss, by.before(i, h))
                    for j in range(J):
                        last = a.activation(junk[h][:, j, :], pY[h][:, j * P:(j + 1) * P], ACT.Square, accum_out=ss[h][:, j:j + 1])
                    last.then_inc(ev.ss, 1)
                for h in part:
                    a.wait_ge(ev.ssw, by.now(i, h))
                    c.step(a.activation(ri[h][:, :], ssw[h][:, :], ACT.Ln))
                    a.activation(ri[h][:, :], ri[h][:, :], ACT.Exp, scale=-0.5).then_inc(ev.ri, 1)
                for h in part:
                    a.wait_ge(ev.q, by.now(i, h))
                    a.wait_ge(ev.x1, by.before(i, h))
                    for j in range(J):
                        last = a.activation(et[h][:, j, :], pY[h][:, j * P:(j + 1) * P], ACT.Exp, scale=q[h][:, j:j + 1])
                    c.step(last)
                    c.step(a.activation(et[h][:, :, :], et[h][:, :, :], ACT.Ln, bias=1.0))
                    a.activation(et[h][:, :, :], et[h][:, :, :], ACT.Exp, scale=-1.0, bias=g.log2_col[:, :]).then_inc(ev.r2, 1)
                for h in part:
                    a.wait_ge(ev.sx, by.now(i, h))
                    rstd(a, g, c, mx[h], rx[h], ev.rx)
                for h in part:
                    a.wait_ge(ev.tx, by.now(i, h))
                    a.wait_ge(ev.pq, by.before(i, h))
                    a.activation(hT[h][:, :], pX[h][:, :], ACT.Relu).then_inc(ev.hx, 1)
                for h in part:
                    a.wait_ge(ev.pq, by.now(i, h))
                    a.wait_ge(w_q[h], 16 * i)
                    a.activation(pq[h][:, :], pQ[h][0:R_, :], ACT.Copy).then_inc(ev.pe, 1)
            by.sweep(a, body)

        @block.tensor
        def _(pe):
            by.credit(pe, ev.ts, ev.td, ev.yy, ev.tx, ev.pq)

            def body(i, part):
                for h in part:
                    pe.wait_ge(ev.ys, by.now(i, h))
                    pe.wait_ge(ev.pe, by.before(i, h))
                    transpose4(pe, g, pS[h], y[h], ev.ts)
                for h in part:
                    pe.wait_ge(ev.yd, by.now(i, h))
                    pe.wait_ge(ev.hx, by.before(i, h))
                    transpose4(pe, g, pD[h], yd[h], ev.td)
                for h in part:
                    pe.wait_ge(ev.sc, by.now(i, h))
                    pe.wait_ge(ev.gd, by.now(i, h))
                    for j in range(J):
                        cols = slice(j * P, (j + 1) * P)
                        pe.matmul(pY[h][:, cols], agg[h][:, cols], g.w0[:, :], start=True, stop=False)
                        last = pe.matmul(pY[h][:, cols], dT[h][:, cols], g.w0[:, :], start=False, stop=True)
                    last.then_inc(ev.yy, 1)
                for h in part:
                    pe.wait_ge(ev.yx, by.now(i, h))
                    pe.wait_ge(ev.gd, by.now(i, h))
                    transpose4(pe, g, pX[h], yx[h], ev.tx)
                for h in part:
                    pe.wait_ge(ev.hx, by.now(i, h))
                    pe.wait_ge(ev.r2, by.now(i, h))
                    pe.matmul(pQ[h][0:R_, :], g.wq[:, 0:R_], hT[h][:, :], start=True, stop=True).then_inc(ev.pq, 1)
            by.sweep(pe, body)


def relations(nc, g, layer):
    by = Cut(4)
    H = by.H
    ctx = ExitStack()
    names = "st rs ys ts hT mk mm om kq ke".split()
    pre = f"r{layer}_"
    ev = events(g, pre, names)
    s_v, s_a, s_p = g.sem(pre + "v"), g.sem(pre + "a"), g.sem(pre + "p")
    l_s, l_t, w_k = ([g.sem(f"{pre}{n}{h}") for h in range(H)] for n in ("ls", "lt", "wk"))
    table, index = (g.tab_a, g.row_x) if layer == 0 else (g.h_tab, g.row_h)
    with ctx:
        sb, each_part, bank = by.allocators(nc, ctx, pre)
        xs, y = each_part("xs", [P, J, P]), each_part("y", [P, J, P])
        hT, typ = each_part("hT", [P, HW]), each_part("typ", [P, HW])
        NM = 4
        masked = sb("masked", [P, NM, HW])
        at_s = each_part("at_s", [P, J], I32)
        st, mv, rs = each_part("st", [P, J, 6]), each_part("mv", [P, J, 2]), each_part("rs", [P, J])
        kq = each_part("kq", [1, HW])
        pM = bank("pM")
        pS = pK = bank("pS")
        block = ctx.enter_context(nc.Block())

        @block.sync
        def _(sp):
            def body(i, part):
                for h in part:
                    wait_alone(g, sp, ev.mk, (i * H + h + 1) * R_)
                    sp.dma_start(typ[h][:, :], by.row_part(g.vec_s[4, :], i, h)).then_inc(l_t[h], 16)
                for h in part:
                    wait_alone(g, sp, ev.ke, by.now(i, h))
                    sp.dma_start(g.kq_s[by.span(i, h)].unsqueeze(0), kq[h][:, :]).then_inc(w_k[h], 16)
            by.sweep(sp, body)
            for h in range(H):
                sp.wait_ge(w_k[h], 16 * by.turns(h))

        @block.gpsimd
        def _(pool):
            c = Chain(pool, s_p, H, g)
            def body(i, part):
                c.turn(i)
                for h in part:
                    wait_alone(g, pool, ev.ys if layer == 0 else ev.ts, by.before(i, h))
                    c.step(pool.tensor_copy(at_s[h][:, :], index[:, by.tiles(i, h)]))
                    gather(pool, table, at_s[h], xs[h], l_s[h])
            by.sweep(pool, body)

        @block.vector
        def _(v):
            by.credit(v, ev.st, ev.ys)
            v.sem_inc(ev.mk, H * R_)
            c = Chain(v, s_v, H if layer == 0 else 0)

            def body(i, part):
                c.turn(i)
                if layer == 0:
                    for h in part:
                        v.wait_ge(l_s[h], 64 * i + 64)
                        stats(v, c, g, xs[h], st[h], mv[h], ev.st)
                    for h in part:
                        v.wait_ge(ev.rs, by.now(i, h))
                        v.wait_ge(ev.ts, by.before(i, h))
                        normalise(v, xs[h], mv[h], rs[h], y[h], ev.ys)
                for h in part:
                    v.wait_ge(ev.hT, by.now(i, h))
                    v.wait_ge(l_t[h], 16 * i + 16)
                    for r in range(R_):
                        n = h * R_ + r
                        v.wait_ge(ev.mm, i * H * R_ + n + 1)
                        v.scalar_tensor_tensor(masked[:, n % NM, :], typ[h][:, :], float(r), hT[h][:, :], ALU.is_equal,
                                               ALU.mult).then_inc(ev.mk, 1)
            by.sweep(v, body)

        @block.scalar
        def _(a):
            a.preload_act_table_set("natural_log_exp_and_others")
            c = Chain(a, s_a, H)
            by.credit(a, ev.rs, ev.hT, ev.om, ev.ke)

            def body(i, part):
                if layer == 0:
                    c.turn(i)
                    for h in part:
                        a.wait_ge(ev.st, by.now(i, h))
                        rstd(a, g, c, mv[h], rs[h], ev.rs)
                for h in part:
                    a.wait_ge(ev.ts, by.now(i, h))
                    a.wait_ge(ev.mk, (i * H + h + 1) * R_)
                    a.activation(hT[h][:, :], pS[h][:, :], ACT.Relu).then_inc(ev.hT, 1)
                for h in part:
                    wait_alone(g, a, ev.mm, (i * H + h + 1) * R_ + NM)
                    a.activation(g.state.msg[:, by.span(i, h)], pM[h][:, :], ACT.Copy).then_inc(ev.om, 1)
                for h in part:
                    a.wait_ge(ev.kq, by.now(i, h))
                    a.wait_ge(w_k[h], 16 * i)
                    a.activation(kq[h][:, :], pK[h][0:1, :], ACT.Copy).then_inc(ev.ke, 1)
            by.sweep(a, body)

        @block.tensor
        def _(pe):
            by.credit(pe, ev.ts, ev.kq)
            pe.sem_inc(ev.mm, NM)

            def body(i, part):
                for h in part:
                    if layer == 0:
                        pe.wait_ge(ev.ys, by.now(i, h))
                    else:
                        pe.wait_ge(l_s[h], 64 * i + 64)
                    pe.wait_ge(ev.ke, by.before(i, h))
                    transpose4(pe, g, pS[h], y[h] if layer == 0 else xs[h], ev.ts)
                for h in part:
                    pe.wait_ge(ev.om, by.before(i, h))
                    for r in range(R_):
                        n = h * R_ + r
                        pe.wait_ge(ev.mk, (i + 1) * H * R_ + n + 1)
                        pe.matmul(pM[h][:, :], g.wr[:, layer * R_ + r, :], masked[:, n % NM, :], start=(r == 0), stop=(r == R_ - 1)).then_inc(ev.mm, 1)
                for h in part:
                    wait_alone(g, pe, ev.om, by.now(i, h))
                    pe.matmul(pK[h][0:1, :], g.att_k[:, layer:layer + 1], g.state.msg[:, by.span(i, h)], start=True, stop=True).then_inc(ev.kq, 1)
            by.sweep(pe, body)


class Segments:

    def __init__(self, nc, ctx, g, prefix, most):
        sb = lambda n, s: ctx.enter_context(nc.sbuf_tensor(prefix + n, s, F32))
        self.ends, self.whole, self.carry = sb("ends", [P, most]), sb("whole", [P, most]), sb("carry", [P, most])
        self.row_ends, self.row_whole, self.row_carry = (sb(n, [most, P]) for n in ("rowe", "roww", "rowc"))
        self.totals = sb("totals", [P, 3])
        self.ps = ctx.enter_context(nc.psum_tensor(prefix + "ps", [P, 4, P], F32))
        self.ends_done, self.turned, self.row_done, self.back = (g.sem(prefix + n) for n in ("e", "t", "r", "b"))
        self.calls = 0
        self.g = g

    def prepare(self, v, c):
        g = self.g
        v.tensor_reduce(self.totals[:, 0:1], g.keep_w[:, :], AX.X, ALU.min)
        v.tensor_reduce(self.totals[:, 1:2], g.keepneg_w[:, :], AX.X, ALU.add)
        c.step(v.tensor_reduce(self.totals[:, 2:3], g.more_w[:, :], AX.X, ALU.min))

    def scan(self, v, c, kind, K, out, data):
        g, n = self.g, self.calls
        self.calls += 1
        mask, total, op0, op1, zero = dict(sum=(g.keep_w, 0, ALU.mult, ALU.add, 0.0), max=(g.keepneg_w, 1, ALU.add, ALU.max, -BIG),
                                           back=(g.more_w, 2, ALU.mult, ALU.add, 0.0))[kind]
        way = (lambda a: a[:, ::-1]) if kind == "back" else (lambda a: a)
        for k in range(K):
            last = v.tensor_tensor_scan(way(out(k)), way(mask[:, :]), way(data(k)), zero, op0, op1)
        c.step(last)
        end = 0 if kind == "back" else W - 1
        for k in range(K):
            v.tensor_copy(self.ends[:, k:k + 1], out(k)[:, end:end + 1])
        v.tensor_copy(self.whole[:, 0:K], self.totals[:, total:total + 1].broadcast_to([P, K])).then_inc(self.ends_done, 1)
        v.wait_ge(self.turned, n + 1)
        v.memset(self.row_carry[0:K, :], zero)
        v.tensor_copy(self.row_ends[0:K, :], self.ps[0:K, 0, :])
        c.step(v.tensor_copy(self.row_whole[0:K, :], self.ps[0:K, 1, :]))
        if kind == "back":
            to, frm = slice(0, P - 1), slice(1, P)
        else:
            to, frm = slice(1, P), slice(0, P - 1)
        v.tensor_tensor_scan(way(self.row_carry[0:K, to]), way(self.row_whole[0:K, frm]), way(self.row_ends[0:K, frm]),
                             zero, op0, op1).then_inc(self.row_done, 1)
        v.wait_ge(self.back, n + 1)
        c.step(v.tensor_copy(self.carry[:, 0:K], self.ps[:, 2, 0:K]))
        for k in range(K):
            last = v.tensor_tensor_scan(way(out(k)), way(mask[:, :]), way(data(k)), self.carry[:, k:k + 1], op0, op1)
        c.step(last)

    def turns(self, pe, Ks):
        g = self.g
        for n, K in enumerate(Ks):
            pe.wait_ge(self.ends_done, n + 1)
            pe.transpose(self.ps[0:K, 0, :], self.ends[:, 0:K], g.ident[:, :])
            pe.transpose(self.ps[0:K, 1, :], self.whole[:, 0:K], g.ident[:, :]).then_inc(self.turned, 1)
            pe.wait_ge(self.row_done, n + 1)
            pe.matmul(self.ps[:, 2, 0:K], self.row_carry[0:K, :], g.ident[0:K, 0:K], start=True, stop=True).then_inc(self.back, 1)


def wide(a):
    return a.rearrange("(p w) -> p w", w=W)


def each(mask, K):
    return mask[:, :].unsqueeze(1).broadcast_to([P, K, W])


def edge_softmax(nc, g, layer):
    ctx = ExitStack()
    pre = f"s{layer}_"
    s_in, s_v, s_l, s_p, s_out = (g.sem(pre + n) for n in ("in", "v", "l", "p", "out"))
    with ctx:
        sb = lambda n, s: ctx.enter_context(nc.sbuf_tensor(pre + n, s, F32))
        pq, pb = sb("pq", [P, R_, W]), sb("pb", [P, R_, W])
        kq, logit, one, most, tot, al = (sb(n, [P, W]) for n in ("kq", "logit", "one", "most", "tot", "al"))
        seg = Segments(nc, ctx, g, pre, R_)
        block = ctx.enter_context(nc.Block())

        @block.sync
        def _(sp):
            for r in range(R_):
                sp.dma_start(pq[:, r, :], wide(g.pq_s[r, :])).then_inc(s_in, 16)
            sp.dma_start(kq[:, :], wide(g.kq_s)).then_inc(s_in, 16)
            sp.wait_ge(s_out, 1)
            sp.dma_start(wide(g.alpha_s), al[:, :]).then_inc(s_p, 16)
            sp.wait_ge(s_p, 16)

        @block.vector
        def _(v):
            c = Chain(v, s_v)
            seg.prepare(v, c)
            v.wait_ge(s_in, 16 * (R_ + 1))
            c.step(v.tensor_tensor(pq[:, :, :], pq[:, :, :], each(g.last_w, R_), ALU.mult))
            seg.scan(v, c, "back", R_, lambda k: pb[:, k, :], lambda k: pq[:, k, :])
            for r in range(R_):
                last = v.scalar_tensor_tensor(pq[:, r, :], g.typ_w[:, :], float(r), pb[:, r, :], ALU.is_equal, ALU.mult)
            c.step(last)
            for r in range(R_):
                c.step(v.tensor_tensor(kq[:, :], kq[:, :], pq[:, r, :], ALU.add))
            c.step(v.scalar_tensor_tensor(logit[:, :], kq[:, :], 0.2, kq[:, :], ALU.mult, ALU.max))
            seg.scan(v, c, "max", 1, lambda k: most[:, :], lambda k: logit[:, :])
            c.step(v.tensor_tensor(one[:, :], most[:, :], g.last_w[:, :], ALU.mult))
            seg.scan(v, c, "back", 1, lambda k: most[:, :], lambda k: one[:, :])
            v.tensor_tensor(logit[:, :], logit[:, :], most[:, :], ALU.subtract).then_inc(s_l, 1)
            v.wait_ge(s_l, 2)
            seg.scan(v, c, "sum", 1, lambda k: tot[:, :], lambda k: logit[:, :])
            c.step(v.tensor_tensor(one[:, :], tot[:, :], g.last_w[:, :], ALU.mult))
            seg.scan(v, c, "back", 1, lambda k: tot[:, :], lambda k: one[:, :])
            c.step(v.tensor_scalar(tot[:, :], tot[:, :], EPS_SM, None, ALU.add))
            c.step(v.reciprocal(one[:, :], tot[:, :]))
            v.tensor_tensor(al[:, :], one[:, :], logit[:, :], ALU.mult).then_inc(s_out, 1)

        @block.scalar
        def _(a):
            a.preload_act_table_set("natural_log_exp_and_others")
            a.wait_ge(s_l, 1)
            a.activation(logit[:, :], logit[:, :], ACT.Exp).then_inc(s_l, 1)

        @block.tensor
        def _(pe):
            seg.turns(pe, (R_, 1, 1, 1, 1))


def aggregate(nc, g, layer):
    by = Cut(4)
    H = by.H
    ctx = ExitStack()
    pre = f"g{layer}_"
    ev = events(g, pre, "wt sc hT tr ro pq pe".split())
    s_0 = g.sem(pre + "zero")
    l_a, l_k, l_x, w_r, w_q = ([g.sem(f"{pre}{n}{h}") for h in range(H)] for n in ("la", "lk", "lx", "wr", "wq"))
    with ctx:
        sb, each_part, bank = by.allocators(nc, ctx, pre)
        al, keep, wt, agg, hT = (each_part(n, [P, HW]) for n in ("al", "keep", "wt", "agg", "hT"))
        rows = each_part("rows", [P, J, P])
        if layer:
            x1 = each_part("x1", [P, J, P])
        else:
            pq = each_part("pq", [R_, HW])
        pT, pQ = bank("pT"), bank("pQ")
        table, first = (g.h_tab, 0) if layer == 0 else (g.tab_a, N)
        block = ctx.enter_context(nc.Block())

        @block.sync
        def _(sp):
            def body(i, part):
                for h in part:
                    wait_alone(g, sp, ev.sc, by.before(i, h))
                    sp.dma_start(al[h][:, :], by.row_part(g.alpha_s, i, h)).then_inc(l_a[h], 16)
                    sp.dma_start(keep[h][:, :], by.row_part(g.keep_s, i, h)).then_inc(l_k[h], 16)
                    if layer:
                        wait_alone(g, sp, ev.ro, by.before(i, h))
                        sp.dma_start(x1[h][:, :, :], by.edge_rows(g.tab_a, N, i, h)).then_inc(l_x[h], 16)
                for h in part:
                    wait_alone(g, sp, ev.ro, by.now(i, h))
                    sp.dma_start(by.edge_rows(table, first, i, h), rows[h][:, :, :]).then_inc(w_r[h], 16)
                    if not layer:
                        wait_alone(g, sp, ev.pe, by.now(i, h))
                        sp.dma_start(g.pq_s[:, by.span(i, h)], pq[h][:, :]).then_inc(w_q[h], 16)
            by.sweep(sp, body)
            for h in range(H):
                sp.wait_ge(w_r[h], 16 * by.turns(h))
                if not layer:
                    sp.wait_ge(w_q[h], 16 * by.turns(h))

        @block.vector
        def _(v):
            by.credit(v, ev.wt, ev.sc)
            v.memset(agg[H - 1][:, HW - 1:HW], 0.0).then_inc(s_0, 1)
            v.wait_ge(s_0, 1)
            if layer:
                by.credit(v, ev.ro)

            def body(i, part):
                for h in part:
                    v.wait_ge(l_a[h], 16 * i + 16)
                    v.tensor_tensor(wt[h][:, :], g.state.msg[:, by.span(i, h)], al[h][:, :], ALU.mult).then_inc(ev.wt, 1)
                for h in part:
                    v.wait_ge(ev.wt, by.now(i, h))
                    v.wait_ge(l_k[h], 16 * i + 16)
                    v.wait_ge(ev.hT, by.before(i, h))
                    v.wait_ge(ev.sc, by.now(i, h) - 1)
                    v.tensor_tensor_scan(agg[h][:, :], keep[h][:, :], wt[h][:, :], agg[h - 1][:, HW - 1:HW], ALU.mult, ALU.add).then_inc(ev.sc, 1)
                if layer:
                    for h in part:
                        v.wait_ge(ev.tr, by.now(i, h))
                        v.wait_ge(l_x[h], 16 * i + 16)
                        v.wait_ge(w_r[h], 16 * i)
                        v.tensor_tensor(rows[h][:, :, :], four(pT[h][:, :]), x1[h][:, :, :], ALU.add).then_inc(ev.ro, 1)
            by.sweep(v, body)

        @block.scalar
        def _(a):
            by.credit(a, ev.hT, ev.pe)
            if not layer:
                by.credit(a, ev.ro)

            def body(i, part):
                for h in part:
                    a.wait_ge(ev.sc, by.now(i, h))
                    a.wait_ge(ev.tr, by.before(i, h))
                    if not layer:
                        a.wait_ge(ev.pq, by.before(i, h))
                    a.activation(hT[h][:, :], agg[h][:, :], ACT.Relu, bias=g.b1_col[:, layer:layer + 1]).then_inc(ev.hT, 1)
                if not layer:
                    for h in part:
                        a.wait_ge(ev.tr, by.now(i, h))
                        a.wait_ge(w_r[h], 16 * i)
                        a.activation(rows[h][:, :, :], four(pT[h][:, :]), ACT.Copy).then_inc(ev.ro, 1)
                        a.wait_ge(ev.pq, by.now(i, h))
                        a.wait_ge(w_q[h], 16 * i)
                        a.activation(pq[h][:, :], pQ[h][0:R_, :], ACT.Copy).then_inc(ev.pe, 1)
            by.sweep(a, body)

        @block.tensor
        def _(pe):
            by.credit(pe, ev.tr, ev.pq)

            def body(i, part):
                for h in part:
                    pe.wait_ge(ev.hT, by.now(i, h))
                    pe.wait_ge(ev.ro, by.before(i, h))
                    transpose4(pe, g, pT[h], four(hT[h][:, :]), ev.tr)
                    if layer == 0:
                        pe.wait_ge(ev.pe, by.before(i, h))
                        pe.matmul(pQ[h][0:R_, :], g.wq[:, R_:2 * R_], hT[h][:, :], start=True, stop=True).then_inc(ev.pq, 1)
            by.sweep(pe, body)


def interaction(nc, g):
    by = Cut(4)
    H = by.H
    ctx = ExitStack()
    names = "xx st rs ys ts hT ff at ac hd si hi ww wc y4 mm tm mc ll sc tb x3".split()
    ev = events(g, "i_", names)
    s_v, s_a, s_p, s_0 = (g.sem("i_" + n) for n in ("v", "a", "p", "zero"))
    l_s, l_8, l_4, l_k, l_x, w_x = ([g.sem(f"i_{n}{h}") for h in range(H)] for n in ("ls", "l8", "l4", "lk", "lx", "wx"))
    c_in = float(1 / np.sqrt(NSC))
    V3 = 3 * MUL
    with ctx:
        sb, each_part, bank = by.allocators(nc, ctx, "i_")
        raw, x, y, x2, x3, ws = (each_part(n, [P, J, P]) for n in ("raw", "x", "y", "x2", "x3", "ws"))
        a8, a4, ya = each_part("a8", [P, J, NSC]), each_part("a4", [P, J, 4]), each_part("ya", [P, J, 4])
        st, mv, rs, nohas, vd = each_part("st", [P, J, 6]), each_part("mv", [P, J, 2]), each_part("rs", [P, J]), each_part("nohas", [P, J]), each_part("vd", [P, J])
        keep, hT, agg = each_part("keep", [P, HW]), each_part("hT", [P, HW]), each_part("agg", [P, HW])
        a8T, sg, hid = each_part("a8T", [NSC, HW]), each_part("sg", [HID, HW]), each_part("hid", [HID, HW])
        m, mT = each_part("m", [P, J, 2 * P]), each_part("mT", [P, 2, HW])
        t02, t1, g3, r3 = each_part("t02", [P, J, 2, MUL]), each_part("t1", [P, J, MUL]), each_part("g3", [P, J, V3]), each_part("r3", [P, J, MUL])
        at_s = each_part("at_s", [P, J], I32)
        pA8 = pH = pW = pL = bank("pW")
        pT = pF = pR = bank("pT")
        block = ctx.enter_context(nc.Block())

        @block.sync
        def _(sp):
            def body(i, part):
                for h in part:
                    wait_alone(g, sp, ev.at, by.before(i, h))
                    sp.dma_start(a8[h][:, :, :], by.edge_rows(g.attr8_s, 0, i, h)).then_inc(l_8[h], 16)
                    wait_alone(g, sp, ev.y4, by.before(i, h))
                    sp.dma_start(a4[h][:, :, :], by.edge_rows(g.attr4_s, 0, i, h)).then_inc(l_4[h], 16)
                    wait_alone(g, sp, ev.x3, by.before(i, h))
                    sp.dma_start(keep[h][:, :], by.row_part(g.keep_s, i, h)).then_inc(l_k[h], 16)
                    sp.dma_start(x2[h][:, :, :], by.edge_rows(g.tab_a, N, i, h)).then_inc(l_x[h], 16)
                for h in part:
                    wait_alone(g, sp, ev.x3, by.now(i, h))
                    sp.dma_start(by.edge_rows(g.tab_b, N, i, h), x3[h][:, :, :]).then_inc(w_x[h], 16)
            by.sweep(sp, body)
            for h in range(H):
                sp.wait_ge(w_x[h], 16 * by.turns(h))

        @block.gpsimd
        def _(pool):
            c = Chain(pool, s_p, H, g)
            def body(i, part):
                c.turn(i)
                for h in part:
                    wait_alone(g, pool, ev.xx, by.before(i, h))
                    c.step(pool.tensor_copy(at_s[h][:, :], g.row_x[:, by.tiles(i, h)]))
                    gather(pool, g.tab_a, at_s[h], raw[h], l_s[h])
            by.sweep(pool, body)

        @block.vector
        def _(v):
            by.credit(v, ev.xx, ev.st, ev.ys, ev.hi, ev.y4, ev.mm, ev.sc, ev.x3)
            v.memset(agg[H - 1][:, HW - 1:HW], 0.0).then_inc(s_0, 1)
            v.wait_ge(s_0, 1)
            c = Chain(v, s_v, 5 * H)

            def body(i, part):
                c.turn(i)
                for h in part:
                    tiles = by.tiles(i, h)
                    v.wait_ge(l_s[h], 64 * i + 64)
                    c.step(v.tensor_copy(nohas[h][:, :], g.nohas[:, tiles]))
                    for j in range(J):
                        last = v.scalar_tensor_tensor(x[h][:, j, :], g.b1_rows[:, :], nohas[h][:, j:j + 1], raw[h][:, j, :], ALU.mult, ALU.add)
                    last.then_inc(ev.xx, 1)
                    v.wait_ge(ev.xx, by.now(i, h))
                    stats(v, c, g, x[h], st[h], mv[h], ev.st)
                for h in part:
                    v.wait_ge(ev.rs, by.now(i, h))
                    v.wait_ge(ev.ts, by.before(i, h))
                    normalise(v, x[h], mv[h], rs[h], y[h], ev.ys)
                for h in part:
                    v.wait_ge(ev.si, by.now(i, h))
                    v.scalar_tensor_tensor(hid[h][:, :], pH[h][0:HID, :], c_in, sg[h][:, :], ALU.mult, ALU.mult).then_inc(ev.hi, 1)
                for h in part:
                    tiles = by.tiles(i, h)
                    v.wait_ge(l_4[h], 16 * i + 16)
                    v.tensor_tensor(ya[h][:, :, :], a4[h][:, :, :], g.vec_src[:, tiles].unsqueeze(2).broadcast_to([P, J, 4]), ALU.mult).then_inc(ev.y4, 1)
                    v.wait_ge(ev.y4, by.now(i, h))
                    v.wait_ge(ev.wc, by.now(i, h))
                    v.wait_ge(ev.ff, by.now(i, h))
                    v.wait_ge(ev.tm, by.before(i, h))
                    s_f = four(pF[h][:, :])[:, :, 0:MUL]
                    v_f = four(pF[h][:, :])[:, :, MUL:P].rearrange("p j (u i) -> p j u i", i=3)
                    w4 = ws[h][:, :, :].rearrange("p j (k u) -> p j k u", k=4)
                    ys = ya[h][:, :, 0:1]
                    yv = ya[h][:, :, 1:4].unsqueeze(2).broadcast_to([P, J, MUL, 3])
                    g34 = g3[h][:, :, :].rearrange("p j (u i) -> p j u i", i=3)
                    over = lambda a: a.unsqueeze(3).broadcast_to([P, J, MUL, 3])
                    m_v = lambda n: m[h][:, :, 2 * MUL + n * V3:2 * MUL + (n + 1) * V3].rearrange("p j (u i) -> p j u i", i=3)
                    v.tensor_tensor(t02[h][:, :, :, :], w4[:, :, 0::2, :], ys.unsqueeze(3).broadcast_to([P, J, 2, MUL]), ALU.mult)
                    v.tensor_tensor(t1[h][:, :, :], s_f, w4[:, :, 1, :], ALU.mult)
                    c.step(v.tensor_tensor(g34, v_f, yv, ALU.mult))
                    v.tensor_tensor(m[h][:, :, 0:MUL], s_f, t02[h][:, :, 0, :], ALU.mult)
                    v.tensor_tensor(m_v(0), over(t1[h][:, :, :]), yv, ALU.mult)
                    v.tensor_tensor(m_v(1), v_f, over(t02[h][:, :, 1, :]), ALU.mult)
                    c.step(v.tensor_reduce(r3[h][:, :, :], g34, AX.X, ALU.add))
                    v.tensor_tensor(m[h][:, :, MUL:2 * MUL], r3[h][:, :, :], w4[:, :, 3, :], ALU.mult).then_inc(ev.mm, 1)
                for h in part:
                    v.wait_ge(ev.ll, by.now(i, h))
                    v.wait_ge(l_k[h], 16 * i + 16)
                    v.wait_ge(ev.tb, by.before(i, h))
                    v.wait_ge(ev.sc, by.now(i, h) - 1)
                    v.tensor_tensor_scan(agg[h][:, :], keep[h][:, :], pL[h][:, :], agg[h - 1][:, HW - 1:HW], ALU.mult, ALU.add).then_inc(ev.sc, 1)
                for h in part:
                    tiles = by.tiles(i, h)
                    c.step(v.tensor_copy(vd[h][:, :], g.vec_dst[:, tiles]))
                    v.wait_ge(ev.tb, by.now(i, h))
                    v.wait_ge(l_x[h], 16 * i + 16)
                    v.wait_ge(w_x[h], 16 * i)
                    for j in range(J):
                        last = v.scalar_tensor_tensor(x3[h][:, j, :], pR[h][:, j * P:(j + 1) * P], vd[h][:, j:j + 1], x2[h][:, j, :], ALU.mult, ALU.add)
                    last.then_inc(ev.x3, 1)
            by.sweep(v, body)

        @block.scalar
        def _(a):
            a.preload_act_table_set("natural_log_exp_and_others")
            c = Chain(a, s_a, 3 * H)
            by.credit(a, ev.rs, ev.hT, ev.ac, ev.si, ev.wc, ev.mc)

            def body(i, part):
                c.turn(i)
                for h in part:
                    a.wait_ge(ev.at, by.now(i, h))
                    a.wait_ge(ev.hd, by.before(i, h))
                    a.activation(a8T[h][:, :], pA8[h][0:NSC, :], ACT.Copy).then_inc(ev.ac, 1)
                for h in part:
                    a.wait_ge(ev.st, by.now(i, h))
                    rstd(a, g, c, mv[h], rs[h], ev.rs)
                for h in part:
                    a.wait_ge(ev.hd, by.now(i, h))
                    a.wait_ge(ev.hi, by.before(i, h))
                    c.step(a.activation(sg[h][:, :], pH[h][0:HID, :], ACT.Exp, scale=-c_in))
                    c.step(a.activation(sg[h][:, :], sg[h][:, :], ACT.Ln, bias=1.0))
                    a.activation(sg[h][:, :], sg[h][:, :], ACT.Exp, scale=-1.0).then_inc(ev.si, 1)
                for h in part:
                    a.wait_ge(ev.ts, by.now(i, h))
                    a.wait_ge(ev.ff, by.before(i, h))
                    a.activation(hT[h][:, :], pT[h][:, :], ACT.Relu).then_inc(ev.hT, 1)
                for h in part:
                    a.wait_ge(ev.ww, by.now(i, h))
                    a.wait_ge(ev.mm, by.before(i, h))
                    a.activation(ws[h][:, :, :], four(pW[h][:, :]), ACT.Copy).then_inc(ev.wc, 1)
                for h in part:
                    a.wait_ge(ev.tm, by.now(i, h))
                    a.wait_ge(ev.ll, by.before(i, h))
                    a.activation(mT[h][:, 0, :], pF[h][:, :], ACT.Copy)
                    a.activation(mT[h][:, 1, :], pW[h][:, :], ACT.Copy).then_inc(ev.mc, 1)
            by.sweep(a, body)

        @block.tensor
        def _(pe):
            by.credit(pe, ev.ts, ev.ff, ev.at, ev.hd, ev.ww, ev.tm, ev.ll, ev.tb)

            def body(i, part):
                for h in part:
                    pe.wait_ge(l_8[h], 16 * i + 16)
                    pe.wait_ge(ev.sc, by.before(i, h))
                    for j in range(J):
                        last = pe.transpose(pA8[h][0:NSC, j * P:(j + 1) * P], a8[h][:, j, :], g.ident[:, :])
                    last.then_inc(ev.at, 1)
                for h in part:
                    pe.wait_ge(ev.ac, by.now(i, h))
                    pe.matmul(pH[h][0:HID, :], g.wfc1[:, :], a8T[h][:, :], start=True, stop=True).then_inc(ev.hd, 1)
                for h in part:
                    pe.wait_ge(ev.ys, by.now(i, h))
                    pe.wait_ge(ev.x3, by.before(i, h))
                    transpose4(pe, g, pT[h], y[h], ev.ts)
                for h in part:
                    pe.wait_ge(ev.hi, by.now(i, h))
                    for j in range(J):
                        last = pe.matmul(pW[h][:, j * P:(j + 1) * P], hid[h][:, j * P:(j + 1) * P], g.wfc2[:, :], start=True, stop=True)
                    last.then_inc(ev.ww, 1)
                for h in part:
                    pe.wait_ge(ev.hT, by.now(i, h))
                    for j in range(J):
                        last = pe.matmul(pF[h][:, j * P:(j + 1) * P], hT[h][:, j * P:(j + 1) * P], g.w1big[:, :], start=True, stop=True)
                    last.then_inc(ev.ff, 1)
                for h in part:
                    pe.wait_ge(ev.mm, by.now(i, h))
                    for k, bank_ in enumerate((pF, pW)):
                        for j in range(J):
                            last = pe.transpose(bank_[h][:, j * P:(j + 1) * P], m[h][:, j, k * P:(k + 1) * P], g.ident[:, :])
                    last.then_inc(ev.tm, 1)
                for h in part:
                    pe.wait_ge(ev.mc, by.now(i, h))
                    for k in range(2):
                        last = pe.matmul(pL[h][:, :], g.w2big[:, k, :], mT[h][:, k, :], start=(k == 0), stop=(k == 1))
                    last.then_inc(ev.ll, 1)
                for h in part:
                    pe.wait_ge(ev.sc, by.now(i, h))
                    transpose4(pe, g, pR[h], four(agg[h][:, :]), ev.tb)
            by.sweep(pe, body)


def gat_rows(nc, g):
    by = Cut(2)
    H = by.H
    ctx = ExitStack()
    names = "xx st rs nm hh sh rh ys ts nT at ae ba nd".split()
    ev = [events(g, f"q{s}_", names) for s in range(2)]
    s_v, s_a, s_p = (g.sem("q_" + n) for n in ("v", "a", "p"))
    l_s, w_a, w_n, w_b = ([[g.sem(f"q{s}_{n}{h}") for h in range(H)] for s in range(2)] for n in ("ls", "wa", "wn", "wb"))
    with ctx:
        sb, each_part, bank = by.allocators(nc, ctx, "q_")
        side = lambda n, s, d=F32: [each_part(f"{n}{k}_", s, d) for k in range(2)]
        raw, hh, y = side("raw", [P, J, P]), side("hh", [P, J, P]), side("y", [P, J, P])
        x = each_part("x", [P, J, P])
        st, mv, sh, mh = side("st", [P, J, 6]), side("mv", [P, J, 2]), side("sh", [P, J, 6]), side("mh", [P, J, 2])
        rs, rh, nm = side("rs", [P, J]), side("rh", [P, J]), side("nm", [P, J])
        nohas = each_part("nohas", [P, J])
        ndT, base = each_part("ndT", [P, HW]), each_part("base", [P, J, P])
        att = [each_part("att0_", [NH, HW]), each_part("att1_", [2 * NH, HW])]
        at_s = each_part("at_s", [P, J], I32)
        pT = [bank("pS"), bank("pD")]
        pA = [bank("pA"), bank("pB")]
        xx = [x, raw[1]]
        block = ctx.enter_context(nc.Block())
        turns = lambda part: [(s, h) for s in range(2) for h in part]

        @block.sync
        def _(sp):
            def body(i, part):
                for h in part:
                    wait_alone(g, sp, ev[1].ba, by.before(i, h))
                    wait_alone(g, sp, ev[1].hh, by.before(i, h))
                    sp.dma_start(raw[1][h][:, :, :], by.edge_rows(g.tab_b, N, i, h)).then_inc(l_s[1][h], 16)
                for h in part:
                    wait_alone(g, sp, ev[1].ba, by.now(i, h))
                    sp.dma_start(by.edge_rows(g.base_s, 0, i, h), base[h][:, :, :]).then_inc(w_b[1][h], 16)
                for h in part:
                    wait_alone(g, sp, ev[1].nT, by.now(i, h))
                    sp.dma_start(g.ndt_s[:, by.span(i, h)], ndT[h][:, :]).then_inc(w_n[1][h], 16)
                for s, h in turns(part):
                    wait_alone(g, sp, ev[s].ae, by.now(i, h))
                    rows = g.att_s[0:NH, :] if s == 0 else g.att_s[NH:3 * NH, :]
                    sp.dma_start(rows[:, by.span(i, h)], att[s][h][:, :]).then_inc(w_a[s][h], 16)
            by.sweep(sp, body)
            for h in range(H):
                for w in (w_b[1][h], w_n[1][h], w_a[0][h], w_a[1][h]):
                    sp.wait_ge(w, 16 * by.turns(h))

        @block.gpsimd
        def _(pool):
            c = Chain(pool, s_p, H, g)
            def body(i, part):
                c.turn(i)
                for h in part:
                    wait_alone(g, pool, ev[0].xx, by.before(i, h))
                    c.step(pool.tensor_copy(at_s[h][:, :], g.row_x[:, by.tiles(i, h)]))
                    gather(pool, g.tab_b, at_s[h], raw[0][h], l_s[0][h])
            by.sweep(pool, body)

        @block.vector
        def _(v):
            for s in range(2):
                by.credit(v, ev[s].xx, ev[s].st, ev[s].nm, ev[s].sh, ev[s].ys, ev[s].ba)
            c = Chain(v, s_v, 5 * H)

            def body(i, part):
                c.turn(i)
                for s, h in turns(part):
                    if s == 0:
                        tiles = by.tiles(i, h)
                        v.wait_ge(l_s[0][h], 64 * i + 64)
                        c.step(v.tensor_copy(nohas[h][:, :], g.nohas[:, tiles]))
                        v.wait_ge(ev[0].hh, by.before(i, h))
                        for j in range(J):
                            last = v.scalar_tensor_tensor(x[h][:, j, :], g.b1_rows[:, :], nohas[h][:, j:j + 1], raw[0][h][:, j, :], ALU.mult, ALU.add)
                        last.then_inc(ev[0].xx, 1)
                        v.wait_ge(ev[0].xx, by.now(i, h))
                    else:
                        v.wait_ge(l_s[1][h], 16 * i + 16)
                    stats(v, c, g, xx[s][h], st[s][h], mv[s][h], ev[s].st)
                for s, h in turns(part):
                    v.wait_ge(ev[s].rs, by.now(i, h))
                    v.scalar_tensor_tensor(nm[s][h][:, :], mv[s][h][:, :, 0], -1.0, rs[s][h][:, :], ALU.mult, ALU.mult).then_inc(ev[s].nm, 1)
                for s, h in turns(part):
                    v.wait_ge(ev[s].hh, by.now(i, h))
                    stats(v, c, g, hh[s][h], sh[s][h], mh[s][h], ev[s].sh)
                for h in part:
                    v.wait_ge(w_b[1][h], 16 * i)
                    v.tensor_tensor(base[h][:, :, :], raw[1][h][:, :, :], hh[1][h][:, :, :], ALU.add).then_inc(ev[1].ba, 1)
                for s, h in turns(part):
                    v.wait_ge(ev[s].rh, by.now(i, h))
                    v.wait_ge(ev[s].ts, by.before(i, h))
                    normalise(v, hh[s][h], mh[s][h], rh[s][h], y[s][h], ev[s].ys)
            by.sweep(v, body)

        @block.scalar
        def _(a):
            a.preload_act_table_set("natural_log_exp_and_others")
            c = Chain(a, s_a, 4 * H)
            for s in range(2):
                by.credit(a, ev[s].rs, ev[s].hh, ev[s].rh, ev[s].nT, ev[s].ae)

            def body(i, part):
                c.turn(i)
                for s, h in turns(part):
                    a.wait_ge(ev[s].st, by.now(i, h))
                    rstd(a, g, c, mv[s][h], rs[s][h], ev[s].rs)
                for s, h in turns(part):
                    a.wait_ge(ev[s].nm, by.now(i, h))
                    a.wait_ge(ev[s].ys, by.before(i, h))
                    if s:
                        a.wait_ge(ev[1].ba, by.before(i, h))
                    for j in range(J):
                        last = a.activation(hh[s][h][:, j, :], xx[s][h][:, j, :], ACT.Relu, scale=rs[s][h][:, j:j + 1], bias=nm[s][h][:, j:j + 1])
                    last.then_inc(ev[s].hh, 1)
                for s, h in turns(part):
                    a.wait_ge(ev[s].sh, by.now(i, h))
                    rstd(a, g, c, mh[s][h], rh[s][h], ev[s].rh)
                for s, h in turns(part):
                    wait_alone(g, a, ev[s].ts, by.now(i, h))
                    if s:
                        a.wait_ge(w_n[1][h], 16 * i)
                        a.wait_ge(ev[1].at, by.before(i, h))
                    dest = ndT[h][:, :] if s else g.state.msg[:, by.span(i, h)]
                    a.activation(dest, pT[s][h][:, :], ACT.Identity, scale=g.ln_g[:, :], bias=g.ln_b[:, :]).then_inc(ev[s].nT, 1)
                for s, h in turns(part):
                    a.wait_ge(ev[s].at, by.now(i, h))
                    a.wait_ge(w_a[s][h], 16 * i)
                    a.activation(att[s][h][:, :], pA[s][h][0:(s + 1) * NH, :], ACT.Copy).then_inc(ev[s].ae, 1)
            by.sweep(a, body)

        @block.tensor
        def _(pe):
            for s in range(2):
                by.credit(pe, ev[s].ts, ev[s].at)

            def body(i, part):
                for s, h in turns(part):
                    pe.wait_ge(ev[s].ys, by.now(i, h))
                    pe.wait_ge(ev[s].nT, by.before(i, h))
                    transpose4(pe, g, pT[s][h], y[s][h], ev[s].ts)
                for s, h in turns(part):
                    wait_alone(g, pe, ev[s].nT, by.now(i, h))
                    wait_alone(g, pe, ev[s].ae, by.before(i, h))
                    rhs = ndT[h][:, :] if s else g.state.msg[:, by.span(i, h)]
                    M = (s + 1) * NH
                    pe.matmul(pA[s][h][0:M, :], g.wa[:, 0:M], rhs, start=True, stop=True).then_inc(ev[s].at, 1)
            by.sweep(pe, body)


def head_softmax(nc, g):
    ctx = ExitStack()
    s_in, s_v, s_l, s_p, s_out = (g.sem("h_" + n) for n in ("in", "v", "l", "p", "out"))
    with ctx:
        sb = lambda n, s: ctx.enter_context(nc.sbuf_tensor("h_" + n, s, F32))
        a_, b_, c_ = sb("a", [P, 3 * NH, W]), sb("b", [P, 2 * NH, W]), sb("c", [P, NH, W])
        part = lambda t, n: t[:, n * NH:(n + 1) * NH, :]
        of = lambda t, n: (lambda k: t[:, n * NH + k, :])
        seg = Segments(nc, ctx, g, "h_", 2 * NH)
        block = ctx.enter_context(nc.Block())
        logit, own = part(a_, 0), part(b_, 0)

        @block.sync
        def _(sp):
            for k in range(3 * NH):
                sp.dma_start(a_[:, k, :], wide(g.att_s[k, :])).then_inc(s_in, 16)
            sp.wait_ge(s_out, 1)
            for k in range(NH):
                sp.dma_start(wide(g.alpha3_s[k, :]), a_[:, 2 * NH + k, :]).then_inc(s_p, 16)
                sp.dma_start(wide(g.alpha3_s[NH + k, :]), a_[:, k, :]).then_inc(s_p, 16)
            sp.wait_ge(s_p, 2 * NH * 16)

        @block.vector
        def _(v):
            c = Chain(v, s_v)
            seg.prepare(v, c)
            v.wait_ge(s_in, 16 * 3 * NH)
            c.step(v.tensor_tensor(a_[:, NH:, :], a_[:, NH:, :], each(g.last_w, 2 * NH), ALU.mult))
            seg.scan(v, c, "back", 2 * NH, of(b_, 0), of(a_, 1))
            v.tensor_tensor(logit, logit, part(b_, 1), ALU.add)
            c.step(v.tensor_tensor(own, own, part(b_, 1), ALU.add))
            v.scalar_tensor_tensor(logit, logit, 0.2, logit, ALU.mult, ALU.max)
            c.step(v.scalar_tensor_tensor(own, own, 0.2, own, ALU.mult, ALU.max))
            seg.scan(v, c, "max", NH, of(a_, 1), of(a_, 0))
            c.step(v.tensor_tensor(part(a_, 2), part(a_, 1), each(g.last_w, NH), ALU.mult))
            seg.scan(v, c, "back", NH, of(c_, 0), of(a_, 2))
            c.step(v.tensor_tensor(part(a_, 1), c_[:, :, :], own, ALU.max))
            v.tensor_tensor(logit, logit, part(a_, 1), ALU.subtract)
            v.tensor_tensor(own, own, part(a_, 1), ALU.subtract).then_inc(s_l, 1)
            v.wait_ge(s_l, 3)
            seg.scan(v, c, "sum", NH, of(a_, 1), of(a_, 0))
            c.step(v.tensor_tensor(part(a_, 2), part(a_, 1), each(g.last_w, NH), ALU.mult))
            seg.scan(v, c, "back", NH, of(c_, 0), of(a_, 2))
            c.step(v.tensor_tensor(c_[:, :, :], c_[:, :, :], own, ALU.add))
            c.step(v.tensor_scalar(c_[:, :, :], c_[:, :, :], EPS_SM, None, ALU.add))
            c.step(v.reciprocal(part(a_, 1), c_[:, :, :]))
            c.step(v.tensor_tensor(part(a_, 2), logit, part(a_, 1), ALU.mult))
            v.tensor_tensor(part(a_, 0), own, part(a_, 1), ALU.mult).then_inc(s_out, 1)

        @block.scalar
        def _(a):
            a.preload_act_table_set("natural_log_exp_and_others")
            a.wait_ge(s_l, 1)
            a.activation(logit, logit, ACT.Exp).then_inc(s_l, 1)
            a.activation(own, own, ACT.Exp).then_inc(s_l, 1)

        @block.tensor
        def _(pe):
            seg.turns(pe, (2 * NH, NH, NH, NH, NH))


def gat_out(nc, g):
    by = Cut(2)
    H = by.H
    ctx = ExitStack()
    names = "os xs cs wt sc od xd cd wd eo u ou ot".split()
    ev = events(g, "o_", names)
    s_v, s_p, s_0 = (g.sem("o_" + n) for n in ("v", "p", "zero"))
    l_a, l_k, l_n, l_b, w_o = ([g.sem(f"o_{n}{h}") for h in range(H)] for n in ("la", "lk", "ln", "lb", "wo"))
    with ctx:
        sb, each_part, _ = by.allocators(nc, ctx, "o_")
        al, own = each_part("al", [NH, HW]), each_part("own", [NH, HW])
        keep, ndT = each_part("keep", [P, HW]), each_part("ndT", [P, HW])
        ax, wt, agg = (each_part(n, [P, 2, HW]) for n in ("ax", "wt", "agg"))
        base, ot = each_part("base", [P, J, P]), each_part("ot", [P, J, P])
        at_o = each_part("at_o", [P, J], I32)
        pO = [ctx.enter_context(nc.psum_tensor(f"o_pO{h}", [P, 2, HW], F32)) for h in range(H)]
        pX = [ctx.enter_context(nc.psum_tensor(f"o_pX{h}", [P, 2, HW], F32)) for h in range(H)]
        block = ctx.enter_context(nc.Block())

        @block.sync
        def _(sp):
            def body(i, part):
                for h in part:
                    wait_alone(g, sp, ev.xd, by.before(i, h))
                    sp.dma_start(al[h][:, :], g.alpha3_s[0:NH, :][:, by.span(i, h)]).then_inc(l_a[h], 16)
                    sp.dma_start(own[h][:, :], g.alpha3_s[NH:2 * NH, :][:, by.span(i, h)]).then_inc(l_a[h], 16)
                    sp.dma_start(ndT[h][:, :], g.ndt_s[:, by.span(i, h)]).then_inc(l_n[h], 16)
                    wait_alone(g, sp, ev.ot, by.before(i, h))
                    sp.dma_start(keep[h][:, :], by.row_part(g.keep_s, i, h)).then_inc(l_k[h], 16)
                    sp.dma_start(base[h][:, :, :], by.edge_rows(g.base_s, 0, i, h)).then_inc(l_b[h], 16)
            by.sweep(sp, body)

        @block.gpsimd
        def _(pool):
            c = Chain(pool, s_p, H, g)
            def body(i, part):
                c.turn(i)
                for h in part:
                    c.step(pool.tensor_copy(at_o[h][:, :], g.put[:, by.tiles(i, h)]))
                    wait_alone(g, pool, ev.ot, by.now(i, h))
                    for j in range(J):
                        pool.indirect_dma_start(g.out, bass.IndirectOffsetOnAxis(ap=at_o[h][:, j:j + 1], axis=0), ot[h][:, j, :], None,
                                                bounds_check=N - 1, oob_is_err=False).then_inc(w_o[h], 16)
                for h in part:
                    wait_alone(g, pool, w_o[h], 64 * i + 64)
            by.sweep(pool, body)

        @block.vector
        def _(v):
            by.credit(v, ev.wt, ev.sc, ev.wd, ev.u, ev.ot)
            v.memset(agg[H - 1][:, :, HW - 1:HW], 0.0).then_inc(s_0, 1)
            v.wait_ge(s_0, 1)
            c = Chain(v, s_v, H)

            def body(i, part):
                c.turn(i)
                for h in part:
                    v.wait_ge(ev.cs, by.now(i, h))
                    v.tensor_tensor(wt[h][:, :, :], pO[h][:, :, :], ax[h][:, :, :], ALU.mult).then_inc(ev.wt, 1)
                for h in part:
                    v.wait_ge(ev.wt, by.now(i, h))
                    v.wait_ge(l_k[h], 16 * i + 16)
                    v.wait_ge(ev.sc, by.now(i, h) - 1)
                    for k in range(2):
                        last = v.tensor_tensor_scan(agg[h][:, k, :], keep[h][:, :], wt[h][:, k, :], agg[h - 1][:, k, HW - 1:HW], ALU.mult, ALU.add)
                    last.then_inc(ev.sc, 1)
                for h in part:
                    v.wait_ge(ev.cd, by.now(i, h))
                    v.wait_ge(ev.sc, by.now(i, h))
                    c.step(v.tensor_tensor(wt[h][:, :, :], pO[h][:, :, :], ax[h][:, :, :], ALU.mult))
                    v.tensor_tensor(wt[h][:, :, :], wt[h][:, :, :], agg[h][:, :, :], ALU.add).then_inc(ev.wd, 1)
                for h in part:
                    v.wait_ge(ev.eo, by.now(i, h))
                    v.scalar_tensor_tensor(wt[h][:, :, :], ax[h][:, :, :], 1.0, wt[h][:, :, :], ALU.min, ALU.add).then_inc(ev.u, 1)
                for h in part:
                    v.wait_ge(ev.ou, by.now(i, h))
                    v.wait_ge(l_b[h], 16 * i + 16)
                    v.wait_ge(w_o[h], 64 * i)
                    v.tensor_tensor(ot[h][:, :, :], four(pO[h][:, 0, :]), base[h][:, :, :], ALU.add).then_inc(ev.ot, 1)
            by.sweep(v, body)

        @block.scalar
        def _(a):
            a.preload_act_table_set("natural_log_exp_and_others")
            by.credit(a, ev.cs, ev.cd, ev.eo)

            def body(i, part):
                for h in part:
                    a.wait_ge(ev.xs, by.now(i, h))
                    a.wait_ge(ev.u, by.before(i, h))
                    a.activation(ax[h][:, :, :], pX[h][:, :, :], ACT.Copy).then_inc(ev.cs, 1)
                for h in part:
                    a.wait_ge(ev.xd, by.now(i, h))
                    a.wait_ge(ev.wt, by.now(i, h))
                    a.activation(ax[h][:, :, :], pX[h][:, :, :], ACT.Copy).then_inc(ev.cd, 1)
                for h in part:
                    a.wait_ge(ev.wd, by.now(i, h))
                    for k in range(2):
                        a.activation(ax[h][:, k, :], wt[h][:, k, :], ACT.Exp, bias=g.b12[:, k:k + 1])
                    for k in range(2):
                        last = a.activation(wt[h][:, k, :], wt[h][:, k, :], ACT.Relu, bias=g.b12[:, k:k + 1])
                    last.then_inc(ev.eo, 1)
            by.sweep(a, body)

        @block.tensor
        def _(pe):
            by.credit(pe, ev.xs, ev.xd, ev.ou)

            def body(i, part):
                for h in part:
                    wait_alone(g, pe, ev.ot, by.before(i, h))
                    for k in range(2):
                        pe.matmul(pO[h][:, k, :], g.w12[:, k * P:(k + 1) * P], g.state.msg[:, by.span(i, h)], start=True, stop=True)
                    pe.wait_ge(l_a[h], 32 * i + 32)
                    pe.wait_ge(ev.cd, by.before(i, h))
                    for k in range(2):
                        last = pe.matmul(pX[h][:, k, :], g.ex[:, k, :], al[h][:, :], start=True, stop=True)
                    last.then_inc(ev.xs, 1)
                for h in part:
                    pe.wait_ge(ev.wt, by.now(i, h))
                    pe.wait_ge(l_n[h], 16 * i + 16)
                    for k in range(2):
                        pe.matmul(pO[h][:, k, :], g.w12[:, k * P:(k + 1) * P], ndT[h][:, :], start=True, stop=True)
                    pe.wait_ge(ev.cs, by.now(i, h))
                    for k in range(2):
                        last = pe.matmul(pX[h][:, k, :], g.ex[:, k, :], own[h][:, :], start=True, stop=True)
                    last.then_inc(ev.xd, 1)
                for h in part:
                    pe.wait_ge(ev.u, by.now(i, h))
                    pe.wait_ge(ev.wd, by.now(i, h))
                    for j in range(J):
                        o = pO[h][:, 0, j * P:(j + 1) * P]
                        pe.matmul(o, wt[h][:, 0, j * P:(j + 1) * P], g.wu[:, 0, :], start=True, stop=False)
                        pe.matmul(o, wt[h][:, 1, j * P:(j + 1) * P], g.wu[:, 1, :], start=False, stop=False)
                        last = pe.matmul(o, g.ones_row[:, :], g.bu_row[:, :], start=False, stop=True)
                    last.then_inc(ev.ou, 1)
            by.sweep(pe, body)


def shared(nc, ctx, inputs):
    state = State()

    def sem(name):
        state.sems.append(nc.alloc_semaphore(name=name))
        return state.sems[-1]

    sb = lambda n, s, d=F32: ctx.enter_context(nc.sbuf_tensor(n, s, d))
    have = dict(inputs, state=state, sem=sem)
    for name, shape in dict(
            ident=[P, P], eps_ln=[P, 1], ones_row=[1, P], ones_col=[P, 1], log2_col=[P, 1], edge_no=[P, T],
            w0=[P, P], w12=[P, 2 * P], wu=[P, 2, P], wr=[P, NREL_LAYERS * R_, P], wfc1=[NSC, HID], wfc2=[HID, P],
            b1_rows=[P, P], b0_row=[1, P], att_q=[P, 2], att_k=[P, 2], b1_col=[P, 2], ln_g=[P, 1], ln_b=[P, 1],
            b12=[P, 2], w1big=[P, P], w2big=[P, 2, P], wq=[P, NREL_LAYERS * R_], wa=[P, 2 * NH], bu_row=[1, P], ex=[NH, 2, P],
            keep_w=[P, W], more_w=[P, W], last_w=[P, W], keepneg_w=[P, W], typ_w=[P, W],
            src_f=[P, T], norm_src=[P, T], norm_dst=[P, T], vec_src=[P, T], vec_dst=[P, T], nohas=[P, T]).items():
        have[name] = sb(name, shape)
    for name in ("src_c", "dst_c", "put", "put_info", "row_x", "row_h"):
        have[name] = sb(name, [P, T], I32)
    for name in ("by_src", "by_dst"):
        have[name] = sb(name, [P, T, 4])
    have["unsorted"] = sb("unsorted", [1, 1], I32)
    have["iota_lo"] = sb("iota_lo", [P, HL], F16)
    for name, shape, dt in (
            ("src_s", [EP, 1], I32), ("dst_s", [EP + 2, 1], I32), ("typ_s", [EP, 1], I32), ("vec_s", [5, EP], F32), ("keep_s", [EP], F32),
            ("deg_s", [NPAD], F32), ("info_s", [N * 4, 1], F32), ("w1big_s", [P, P], F32), ("w2big_s", [2 * P, P], F32),
            ("tab_a", [TABROWS, D], F32), ("tab_b", [TABROWS, D], F32), ("h_tab", [HROWS, D], F32),
            ("pq_s", [R_, EP], F32), ("kq_s", [EP], F32), ("alpha_s", [EP], F32),
            ("att_s", [3 * NH, EP], F32), ("alpha3_s", [2 * NH, EP], F32), ("ndt_s", [P, EP], F32),
            ("base_s", [EP, D], F32), ("attr8_s", [EP, NSC], F32), ("attr4_s", [EP, 4], F32)):
        have[name] = nc.dram_tensor(name, shape, dt, kind="Internal").ap()
    return namedtuple("Shared", list(have))(**have)


def run(nc, g, stage, *args):
    outer, g.state.sems = g.state.sems, []
    g.state.runs += 1
    g.state.waits = g.sem(f"waits{g.state.runs}")
    stage(nc, g, *args)
    nc.clear_and_free_semaphores(g.state.sems)
    nc.all_engine_barrier()
    g.state.sems = outer


def gnn(nc, inputs, out):
    ctx = ExitStack()
    with ctx:
        g = shared(nc, ctx, dict(inputs, out=out))
        for stage in STAGES:
            run(nc, g, stage)


def rgat(nc, g):
    with nc.sbuf_tensor("msg", [P, EP], F32) as msg:
        g.state.msg = msg
        for layer in range(NREL_LAYERS):
            run(nc, g, relations, layer)
            run(nc, g, edge_softmax, layer)
            run(nc, g, aggregate, layer)


def gat(nc, g):
    with nc.sbuf_tensor("source_rows", [P, EP], F32) as msg:
        g.state.msg = msg
        run(nc, g, gat_rows)
        run(nc, g, head_softmax)
        run(nc, g, gat_out)


STAGES = [dense_identity, edges_copy, edges_sorted, edges_in, degrees, node_info, weights, node_dense, edge_columns, layer0_edges, rgat, interaction, gat]

_INS = ["x", "src", "dst", "edge_attr_4", "edge_attr_8", "edge_type_8", "node_vec1", "node_vec1_n2", "L0_gnn_W",
        "L1_gnn_W", "L1_gnn_att_q", "L1_gnn_att_k", "L1_gnn_bias", "L2_gnn_w1_s", "L2_gnn_w1_v", "L2_gnn_Wfc1",
        "L2_gnn_Wfc2", "L2_gnn_w2_s", "L2_gnn_w2_v", "L3_gnn_ln_g", "L3_gnn_ln_b", "L3_gnn_W1", "L3_gnn_a1s",
        "L3_gnn_a1d", "L3_gnn_b1", "L3_gnn_W2", "L3_gnn_a2s", "L3_gnn_a2d", "L3_gnn_b2", "L3_gnn_Wu", "L3_gnn_bu"]
_NAMES = {"edge_attr_4": "attr4", "edge_attr_8": "attr8", "edge_type_8": "typ", "node_vec1": "vec1", "node_vec1_n2": "vec2"}


def short(name):
    return _NAMES.get(name, name.replace("_gnn_", "_"))


def kernel(**inputs):
    import numpy as _np
    import concourse.bacc as _bacc
    from concourse import mybir as _mybir
    from concourse.bass_utils import run_bass_kernel_spmd as _run

    nc = _bacc.Bacc("TRN2", target_bir_lowering=False, num_devices=1)
    arrays, aps = {}, {}
    for name in _INS:
        a = _np.ascontiguousarray(inputs[name])
        arrays[f"in_{name}"] = a
        aps[short(name)] = nc.dram_tensor(f"in_{name}", a.shape, _mybir.dt.from_np(a.dtype), kind="ExternalInput").ap()
    out = nc.dram_tensor("out_0", (N, D), _mybir.dt.float32, kind="ExternalOutput").ap()
    gnn(nc, aps, out)
    r = _run(nc, [arrays], core_ids=[0])
    return r.results[0]["out_0"]
```
